# Optimizing a Trainium2 kernel written in Bass

```python
import numpy as np
import jax
import jax.numpy as jnp

def _softmax(x, axis=-1):
    return jax.nn.softmax(x, axis=axis)

def _gelu(x):
    return jax.nn.gelu(x, approximate=True)

def _silu(x):
    return jax.nn.silu(x)

def _sigmoid(x):
    return jax.nn.sigmoid(x)

def _layernorm(x, axis=-1, eps=1e-05):
    m = jnp.mean(x, axis=axis, keepdims=True)
    v = jnp.var(x, axis=axis, keepdims=True)
    return (x - m) / jnp.sqrt(v + eps)

def _scatter_add(tgt, idx, src, axis=0):
    return tgt.at[idx].add(src)

def _segment_sum(src, seg, n):
    return jax.ops.segment_sum(src, seg, n)
kernel_name = 'mk_adj_ffn_d1_adj_r2_56a2d4'

def setup_inputs(seed: int=0):
    np.random.seed(seed)
    _w = jnp.asarray

    def _rec_inputs():
        import jax
        import jax.numpy as jnp
        _gk = jax.random.key(seed)
        x = 7.22e-05 + 1 * jax.random.normal(jax.random.fold_in(_gk, 1), (8, 1024, 128), jnp.float32)
        _a = jax.random.bernoulli(jax.random.fold_in(_gk, 2), 0.0078125, (8, 1024, 1024))
        _af = _a.astype(jnp.float32)
        adj = _af
        _nm = jnp.ones((8, 1024), dtype=bool)
        nodemask = jnp.where(_nm, 1.0, 0.0).astype(jnp.float32)
        return (x, adj, nodemask)
    x, adj, nodemask = _rec_inputs()

    def _L0_gnn_setup():
        import jax, jax.numpy as jnp
        import numpy as np
        B, N, D, C, L = (64, 256, 128, 128, 5)
        EDGE_P = 0.02

        def _gru_cell(m, h, w_ih, w_hh, b_ih, b_hh):
            gi = m @ w_ih.T + b_ih
            gh = h @ w_hh.T + b_hh
            i_r, i_z, i_n = jnp.split(gi, 3, axis=-1)
            h_r, h_z, h_n = jnp.split(gh, 3, axis=-1)
            r = jax.nn.sigmoid(i_r + h_r)
            z = jax.nn.sigmoid(i_z + h_z)
            n = jnp.tanh(i_n + r * h_n)
            return (1.0 - z) * n + z * h
        key = jax.random.key(seed)
        ks = jax.random.split(key, 8)
        x = jax.random.normal(ks[0], (B, N, D), dtype=jnp.float32)
        adj = (jax.random.uniform(ks[1], (B, N, N)) < EDGE_P).astype(jnp.float32)
        mask = jnp.ones((B, N), dtype=jnp.float32)
        s = 1.0 / np.sqrt(C).astype(np.float32)
        weight = jax.random.uniform(ks[2], (L, C, C), minval=-s, maxval=s, dtype=jnp.float32)
        w_ih = jax.random.uniform(ks[3], (3 * C, C), minval=-s, maxval=s, dtype=jnp.float32)
        w_hh = jax.random.uniform(ks[4], (3 * C, C), minval=-s, maxval=s, dtype=jnp.float32)
        b_ih = jax.random.uniform(ks[5], (3 * C,), minval=-s, maxval=s, dtype=jnp.float32)
        b_hh = jax.random.uniform(ks[6], (3 * C,), minval=-s, maxval=s, dtype=jnp.float32)
        return dict(x=x, adj=adj, mask=mask, weight=weight, w_ih=w_ih, w_hh=w_hh, b_ih=b_ih, b_hh=b_hh)
    _L0_gnn_all = _L0_gnn_setup()
    _L0_gnn_in = {k: v for k, v in _L0_gnn_all.items() if k in ('weight', 'w_ih', 'w_hh', 'b_ih', 'b_hh')}
    del _L0_gnn_all

    def _L0_ffn_setup():
        import math
        import jax, jax.numpy as jnp
        import numpy as np
        CAPACITY_FACTOR = 1.25
        TOP_K = 2
        LN_EPS = 1e-05

        def _layer_norm(x, gamma, beta):
            mu = jnp.mean(x, axis=-1, keepdims=True)
            var = jnp.var(x, axis=-1, keepdims=True)
            return (x - mu) * jax.lax.rsqrt(var + LN_EPS) * gamma + beta
        key = jax.random.key(seed)
        ks = jax.random.split(key, 4)
        B, S, D, F, E = (8, 2048, 128, 256, 8)
        x = jax.random.normal(ks[0], (B, S, D), dtype=jnp.float32)
        Wr = jax.random.normal(ks[1], (D, E), dtype=jnp.float32) / np.sqrt(D)
        br = jnp.zeros((E,), jnp.float32)
        W1 = jax.random.normal(ks[2], (E, D, F), dtype=jnp.float32) / np.sqrt(D)
        b1 = jnp.zeros((E, F), jnp.float32)
        W2 = jax.random.normal(ks[3], (E, F, D), dtype=jnp.float32) / np.sqrt(F)
        b2 = jnp.zeros((E, D), jnp.float32)
        gamma = jnp.ones((D,), jnp.float32)
        beta = jnp.zeros((D,), jnp.float32)
        return {'x': x, 'Wr': Wr, 'br': br, 'W1': W1, 'b1': b1, 'W2': W2, 'b2': b2, 'gamma': gamma, 'beta': beta}
    _L0_ffn_all = _L0_ffn_setup()
    _L0_ffn_in = {k: v for k, v in _L0_ffn_all.items() if k in ('Wr', 'br', 'W1', 'b1', 'W2', 'b2', 'gamma', 'beta')}
    del _L0_ffn_all
    return {'x': x, 'adj': adj, 'nodemask': nodemask, 'L0_gnn_weight': _L0_gnn_in['weight'], 'L0_gnn_w_ih': _L0_gnn_in['w_ih'], 'L0_gnn_w_hh': _L0_gnn_in['w_hh'], 'L0_gnn_b_ih': _L0_gnn_in['b_ih'], 'L0_gnn_b_hh': _L0_gnn_in['b_hh'], 'L0_ffn_Wr': _L0_ffn_in['Wr'], 'L0_ffn_br': _L0_ffn_in['br'], 'L0_ffn_W1': _L0_ffn_in['W1'], 'L0_ffn_b1': _L0_ffn_in['b1'], 'L0_ffn_W2': _L0_ffn_in['W2'], 'L0_ffn_b2': _L0_ffn_in['b2'], 'L0_ffn_gamma': _L0_ffn_in['gamma'], 'L0_ffn_beta': _L0_ffn_in['beta']}

def reference(x, adj, nodemask, L0_gnn_weight, L0_gnn_w_ih, L0_gnn_w_hh, L0_gnn_b_ih, L0_gnn_b_hh, L0_ffn_Wr, L0_ffn_br, L0_ffn_W1, L0_ffn_b1, L0_ffn_W2, L0_ffn_b2, L0_ffn_gamma, L0_ffn_beta):
    import jax
    import jax.numpy as jnp

    def _L0_gnn_ref(x, adj, mask, weight, w_ih, w_hh, b_ih, b_hh):
        import jax, jax.numpy as jnp
        import numpy as np
        B, N, D, C, L = (64, 256, 128, 128, 5)
        EDGE_P = 0.02

        def _gru_cell(m, h, w_ih, w_hh, b_ih, b_hh):
            gi = m @ w_ih.T + b_ih
            gh = h @ w_hh.T + b_hh
            i_r, i_z, i_n = jnp.split(gi, 3, axis=-1)
            h_r, h_z, h_n = jnp.split(gh, 3, axis=-1)
            r = jax.nn.sigmoid(i_r + h_r)
            z = jax.nn.sigmoid(i_z + h_z)
            n = jnp.tanh(i_n + r * h_n)
            return (1.0 - z) * n + z * h
        A = (adj != 0).astype(x.dtype)
        h = x
        for l in range(weight.shape[0]):
            m = jnp.einsum('bnd,de->bne', h, weight[l])
            agg = jnp.einsum('bij,bid->bjd', A, m)
            h = _gru_cell(agg, h, w_ih, w_hh, b_ih, b_hh)
        return h * mask[..., None]

    def _L0_ffn_ref(x, Wr, br, W1, b1, W2, b2, gamma, beta):
        import math
        import jax, jax.numpy as jnp
        import numpy as np
        CAPACITY_FACTOR = 1.25
        TOP_K = 2
        LN_EPS = 1e-05

        def _layer_norm(x, gamma, beta):
            mu = jnp.mean(x, axis=-1, keepdims=True)
            var = jnp.var(x, axis=-1, keepdims=True)
            return (x - mu) * jax.lax.rsqrt(var + LN_EPS) * gamma + beta
        B, S, D = x.shape
        E = Wr.shape[1]
        N = B * S
        K = TOP_K
        logits = jnp.mean(x, axis=1) @ Wr + br
        routing_weights = jax.nn.softmax(logits, axis=-1)
        capacity = float(math.ceil(N * CAPACITY_FACTOR / E))
        expected_loads = routing_weights.sum(axis=0) * (N / B)
        scale = jnp.where(expected_loads > capacity, capacity / expected_loads, 1.0)
        routing_weights = jax.nn.softmax(routing_weights * scale, axis=-1)
        rw_tok = jnp.broadcast_to(routing_weights[:, None, :], (B, S, E)).reshape(N, E)
        top_w, top_i = jax.lax.top_k(rw_tok, K)
        top_w = jax.nn.softmax(top_w, axis=-1)
        xf = x.reshape(N, D)
        h = jax.nn.gelu(jnp.einsum('nd,edf->enf', xf, W1) + b1[:, None, :], approximate=False)
        y = jnp.einsum('enf,efd->end', h, W2) + b2[:, None, :]
        w_dense = jnp.zeros((N, E), x.dtype).at[jnp.arange(N)[:, None], top_i].add(top_w)
        out = jnp.einsum('ne,end->nd', w_dense, y).reshape(B, S, D)
        out = _layer_norm(out + x, gamma, beta)
        return out
    x = x + _L0_gnn_ref(_layernorm(x, axis=-1), adj, nodemask, L0_gnn_weight, L0_gnn_w_ih, L0_gnn_w_hh, L0_gnn_b_ih, L0_gnn_b_hh)
    x = x + _L0_ffn_ref(_layernorm(x, axis=-1), L0_ffn_Wr, L0_ffn_br, L0_ffn_W1, L0_ffn_b1, L0_ffn_W2, L0_ffn_b2, L0_ffn_gamma, L0_ffn_beta)
    return x

_drawn_inputs = setup_inputs


def setup_inputs(seed=0):
    import zlib

    import numpy as np

    out = dict(_drawn_inputs(seed))
    spreads = {'L0_ffn_br': (0.0, 0.1),
     'L0_ffn_b1': (0.0, 0.379),
     'L0_ffn_b2': (0.0, 0.1),
     'L0_ffn_gamma': (1.0, 0.2),
     'L0_ffn_beta': (0.0, 0.1)}
    factors = {}
    for name, (base, spread) in spreads.items():
        noise = np.random.default_rng([zlib.crc32(name.encode()), seed]).standard_normal(out[name].shape)
        drawn = base * np.exp(spread * noise) if base else spread * noise
        out[name] = jnp.asarray(drawn.astype(out[name].dtype))
    for name, factor in factors.items():
        out[name] = (out[name] * factor).astype(out[name].dtype)
    return out
```

```python
from contextlib import ExitStack

import concourse.bass as bass
from concourse import mybir

ALU = mybir.AluOpType
ACT = mybir.ActivationFunctionType
F32 = mybir.dt.float32
F32R = mybir.dt.float32r
U8 = mybir.dt.uint8
U32 = mybir.dt.uint32
AX_X = mybir.AxisListType.X

P = 128
LN_EPS = 1e-5
TOP_K = 2
CAPACITY_FACTOR = 1.25



def exact(ap):
    return ap.bitcast(F32)


def build_gnn_ffn(nc, x, adj, nodemask, gnn_w, w_ih, w_hh, b_ih, b_hh, Wr, br, W1, b1, W2, b2, gamma, beta, out):
    B, N, D = x.shape
    LAYERS = gnn_w.shape[0]
    E, _, F = W1.shape
    KB = N // P
    HW = N // 2
    HK = KB // 2
    G = 3 * D
    PAIRS = B // 2
    SLOTS = 4
    S_PAIR = SLOTS * LAYERS
    LAST = LAYERS - 1
    CHUNKS = 2 * KB
    FB = F // P
    UNITS = 2 * TOP_K * FB
    CAPACITY = float(-(-B * N * 5 // (4 * E)))
    assert D == P and HW == 512 and CHUNKS == SLOTS * (LAYERS - 1) and FB == 2 and UNITS == 8 and PAIRS >= 2

    wc_dram = nc.dram_tensor("wc_dram", [LAYERS, P, 2 * G], F32, kind="Internal").ap()
    x1_dram = nc.dram_tensor("x1_dram", [B, N, D], F32, kind="Internal").ap()
    z_dram = nc.dram_tensor("z_dram", [B, N, D], F32, kind="Internal").ap()

    def batch(t, b):
        return t.rearrange("b (k p) d -> b p k d", p=P)[b]

    adj_rows = adj.rearrange("b i j -> (b i) j")

    with ExitStack() as whole:
        def alloc_in(stack, space):
            return lambda name, shape, dt=F32: stack.enter_context(space(name, shape, dt))

        def sem_in(stack):
            return lambda name: stack.enter_context(nc.semaphore(name))

        sb = alloc_in(whole, nc.sbuf_tensor)
        sem = sem_in(whole)
        ident = sb("ident", [P, P])
        zsum = sb("zsum", [P, B, D])
        neg_half = sb("neg_half", [P, KB])
        ident_zero, ident_ready, consts_ready = sem("ident_zero"), sem("ident_ready"), sem("consts_ready")
        waits_passed = sem("waits_passed")

        def detach(eng):
            eng.sem_inc(waits_passed, 1)

        def token_stats(dve, blocks, src, stat6, mv, step_sem, step, done_sem):
            if not (isinstance(step, int) and step == 1):
                dve.wait_ge(done_sem, step - 1)
            for k in range(blocks):
                ins = nc.vector.bn_stats(stat6[:, k, :], src[:, k, :])
            ins.then_inc(step_sem, 1)
            dve.wait_ge(step_sem, step)
            detach(dve)
            for k in range(blocks):
                ins = nc.vector.bn_aggr(mv[:, k, :], stat6[:, k, :])
            ins.then_inc(done_sem, 1)

        def norm_apply(pool, blocks, src, dst, mv, rstd, stats_sem, stats_count, step_sem, step, done_sem):
            pool.wait_ge(stats_sem, stats_count)
            detach(pool)
            nc.gpsimd.tensor_scalar(rstd[:, 0:blocks], mv[:, :, 1], LN_EPS, None, ALU.add).then_inc(step_sem, 1)
            pool.wait_ge(step_sem, step)
            nc.gpsimd.tensor_tensor(rstd[:, 0:blocks], rstd[:, 0:blocks], neg_half[:, 0:blocks], ALU.pow).then_inc(step_sem, 1)
            pool.wait_ge(step_sem, step + 1)
            detach(pool)
            for k in range(blocks):
                ins = nc.gpsimd.tensor_scalar(dst[:, k, :], src[:, k, :], mv[:, k, 0:1], rstd[:, k:k + 1],
                                              ALU.subtract, ALU.mult)
            ins.then_inc(done_sem, 1)

        with ExitStack() as phase1:
            sb = alloc_in(phase1, nc.sbuf_tensor)
            sem = sem_in(phase1)
            a_mat = [sb(f"a_mat{n}", [P, KB, N], F32R) for n in range(2)]
            a_next = sb("a_next", [P, CHUNKS, N], U8)
            a_raw = sb("a_raw", [P, 2, N])
            w_cur = [sb(f"w_cur{n}", [P, 2 * G], F32R) for n in range(2)]
            w_hhT = sb("w_hhT", [P, 2 * G], F32R)
            hT = [sb(f"hT{n}", [P, N]) for n in range(2)]
            hT_hi = [sb(f"hT_hi{n}", [P, N], F32R) for n in range(2)]
            hT_lo = [sb(f"hT_lo{n}", [P, N], F32R) for n in range(2)]
            nat_hi = [sb(f"nat_hi{n}", [P, KB, D], F32R) for n in range(2)]
            nat_lo = [sb(f"nat_lo{n}", [P, KB, D], F32R) for n in range(2)]
            agg_hi = [sb(f"agg_hi{h}", [P, HW], F32R) for h in range(2)]
            agg_lo = [sb(f"agg_lo{h}", [P, HW], F32R) for h in range(2)]
            xbuf = [sb(f"xbuf{n}", [P, KB, D]) for n in range(2)]
            xn = [sb(f"xn{n}", [P, KB, D]) for n in range(2)]
            z_nat = sb("z_nat", [P, KB, D])
            z_fold = sb("z_fold", [P, HK, D])
            masked = sb("masked", [P, HK, D])
            cand = sb("cand", [P, HW])
            gate_z = sb("gate_z", [P, HW])
            diff = sb("diff", [P, HW])
            stat6 = sb("stat6", [P, KB, 6])
            mv1 = [sb(f"mv1_{n}", [P, KB, 2]) for n in range(2)]
            mv2 = [sb(f"mv2_{n}", [P, KB, 2]) for n in range(2)]
            rstd = sb("rstd", [P, KB])
            bias_ih, bias_hh, bias_rz = sb("bias_ih", [P, 3]), sb("bias_hh", [P, 3]), sb("bias_rz", [P, 2])
            mask_tok = sb("mask_tok", [P, B, KB])

            a_raw_loaded = [sem("a_raw_loaded0"), sem("a_raw_loaded1")]
            a_compared = sem("a_compared")
            stats_step, stats_done, norm_step = sem("stats_step"), sem("stats_done"), sem("norm_step")
            ln1_done = [sem(f"ln1_done{n}") for n in range(2)]
            xbuf_loaded = [sem(f"xbuf_loaded{n}") for n in range(2)]

            with ExitStack() as stage0:
                sb0, ps0, sem = alloc_in(stage0, nc.sbuf_tensor), alloc_in(stage0, nc.psum_tensor), sem_in(stage0)
                w_ih_nat, w_hh_nat = sb0("w_ih_nat", [P, 3, D]), sb0("w_hh_nat", [P, 3, D])
                w_nat, w_T = sb0("w_nat", [P, LAYERS, D]), sb0("w_T", [P, LAYERS, D])
                w_ihT = sb0("w_ihT", [P, G])
                mask_nat = sb0("mask_nat", [B * KB, P])
                wc_split = [sb0(f"wc_split{i}", [P, 2 * G], F32R) for i in range(2)]
                ps_ih, ps_hh, ps_wt = ps0("ps_ih", [P, G]), ps0("ps_hh", [P, G]), ps0("ps_wt", [P, 2, 512])
                ps_mask = ps0("ps_mask", [P, B * KB])
                ps_wc = [ps0(f"ps_wc{i}", [P, G]) for i in range(2)]
                w_loaded, x_loaded, mask_loaded, bias_loaded = (
                    sem(n) for n in ("w_loaded", "x_loaded", "mask_loaded", "bias_loaded"))
                transposed, turned, hi_done, wc_done, wc_lo_done, wc_stored, bias_added = (
                    sem(n) for n in ("transposed", "turned", "hi_done", "wc_done", "wc_lo_done", "wc_stored", "bias_added"))
                block = stage0.enter_context(nc.Block())

                @block.sync
                def _(sp):
                    sp.dma_start(w_ih_nat[:], w_ih.rearrange("(g p) d -> p g d", p=P)).then_inc(w_loaded, 16)
                    sp.dma_start(w_hh_nat[:], w_hh.rearrange("(g p) d -> p g d", p=P)).then_inc(w_loaded, 16)
                    sp.dma_start(w_nat[:], gnn_w.rearrange("l d e -> d l e")).then_inc(w_loaded, 16)
                    for lane in range(2):
                        sp.dma_start(xn[lane][:], batch(x, lane)).then_inc(x_loaded, 16)
                    for c in range(CHUNKS):
                        if c >= 2:
                            sp.wait_ge(a_compared, c - 1)
                        sp.dma_start(a_raw[:, c % 2], adj_rows[c * P:(c + 1) * P, :]).then_inc(a_raw_loaded[c % 2], 16)

                @block.scalar
                def _(act):
                    act.dma_start(mask_nat[:], nodemask.rearrange("b (k p) -> (b k) p", p=P)).then_inc(mask_loaded, 16)
                    with nc.allow_non_contiguous_dma(reason="384 bias values, one per partition"):
                        act.dma_start(bias_ih[:], b_ih.rearrange("(g p) -> p g", p=P)).then_inc(bias_loaded, 16)
                        act.dma_start(bias_hh[:], b_hh.rearrange("(g p) -> p g", p=P)).then_inc(bias_loaded, 16)
                    act.wait_ge(transposed, 2)
                    nc.scalar.activation(w_hhT[:, 0:G], ps_hh[:], ACT.Copy).then_inc(hi_done, 1)
                    for n in range(LAYERS + 1):
                        if n < LAYERS:
                            act.wait_ge(wc_done, n + 1)
                            if n >= 2:
                                act.wait_ge(wc_stored, 16 * (n - 1))
                            nc.scalar.activation(wc_split[n % 2][:, 0:G], ps_wc[n % 2][:], ACT.Copy).then_inc(hi_done, 1)
                        if n >= 1:
                            act.wait_ge(wc_lo_done, n)
                            act.dma_start(wc_dram[n - 1], exact(wc_split[(n - 1) % 2][:])).then_inc(wc_stored, 16)
                    act.wait_ge(wc_stored, 16 * LAYERS)

                @block.gpsimd
                def _(pool):
                    nc.gpsimd.memset(ident[:], 0.0).then_inc(ident_zero, 1)
                    nc.gpsimd.memset(neg_half[:], -0.5).then_inc(consts_ready, 1)
                    pool.wait_ge(ident_zero, 1)
                    nc.gpsimd.affine_select(out=ident[:], in_=ident[:], compare_op=ALU.not_equal, fill=1.0, base=0,
                                            pattern=[[-1, P]], channel_multiplier=1).then_inc(ident_ready, 1)
                    pool.wait_ge(consts_ready, 1)
                    for lane in range(2):
                        pool.dma_start(xbuf[lane][:], batch(x, lane)).then_inc(xbuf_loaded[lane], 16)
                    for lane in range(2):
                        norm_apply(pool, KB, xn[lane], xn[lane], mv1[lane], rstd, stats_done, lane + 1,
                                   norm_step, 2 * lane + 1, ln1_done[lane])
                        pool.wait_ge(ln1_done[lane], 1)

                @block.tensor
                def _(pe):
                    pe.wait_ge(ident_ready, 1)
                    pe.wait_ge(w_loaded, 48)
                    for g in range(3):
                        tr = nc.tensor.transpose(ps_ih[:, g * D:(g + 1) * D], w_ih_nat[:, g, :], ident[:])
                    tr.then_inc(transposed, 1)
                    for g in range(3):
                        tr = nc.tensor.transpose(ps_hh[:, g * D:(g + 1) * D], w_hh_nat[:, g, :], ident[:])
                    tr.then_inc(transposed, 1)
                    for n in range(LAYERS):
                        tr = nc.tensor.transpose(ps_wt[:, n // 4, n % 4 * D:(n % 4 + 1) * D], w_nat[:, n, :], ident[:])
                    tr.then_inc(transposed, 1)
                    pe.wait_ge(mask_loaded, 16)
                    nc.tensor.transpose(ps_mask[:], mask_nat[:], ident[0:B * KB, 0:B * KB]).then_inc(transposed, 1)
                    pe.wait_ge(turned, 3)
                    for n in range(LAYERS):
                        if n >= 2:
                            pe.wait_ge(wc_lo_done, n - 1)
                        nc.tensor.matmul(ps_wc[n % 2][:], w_T[:, n, :], w_ihT[:], start=True, stop=True).then_inc(wc_done, 1)

                @block.vector
                def _(dve):
                    dve.wait_ge(transposed, 1)
                    nc.vector.tensor_copy(w_ihT[:], ps_ih[:]).then_inc(turned, 1)
                    dve.wait_ge(transposed, 3)
                    nc.vector.tensor_copy(w_T[:, 0:4, :], ps_wt[:, 0, :].rearrange("p (l d) -> p l d", d=D)).then_inc(turned, 1)
                    nc.vector.tensor_copy(w_T[:, 4, :], ps_wt[:, 1, 0:D]).then_inc(turned, 1)
                    dve.wait_ge(transposed, 4)
                    nc.vector.tensor_copy(mask_tok[:].rearrange("p b k -> p (b k)"), ps_mask[:]).then_inc(turned, 1)
                    dve.wait_ge(hi_done, 1)
                    nc.vector.tensor_tensor(w_hhT[:, G:2 * G], ps_hh[:], exact(w_hhT[:, 0:G]), ALU.subtract).then_inc(turned, 1)
                    dve.wait_ge(x_loaded, 32)
                    for lane in range(2):
                        token_stats(dve, KB, xn[lane], stat6, mv1[lane], stats_step, lane + 1, stats_done)
                    for n in range(LAYERS):
                        dve.wait_ge(hi_done, 2 + n)
                        nc.vector.tensor_tensor(wc_split[n % 2][:, G:2 * G], ps_wc[n % 2][:], exact(wc_split[n % 2][:, 0:G]),
                                                ALU.subtract).then_inc(wc_lo_done, 1)
                    dve.wait_ge(bias_loaded, 32)
                    nc.vector.tensor_tensor(bias_rz[:], bias_ih[:, 0:2], bias_hh[:, 0:2], ALU.add).then_inc(bias_added, 1)
                    for c in range(CHUNKS):
                        dve.wait_ge(a_raw_loaded[c % 2], 16 * (c // 2 + 1))
                        nc.vector.tensor_scalar(a_mat[c // KB][:, c % KB, :], a_raw[:, c % 2], 0.0, None,
                                                ALU.not_equal).then_inc(a_compared, 1)

            with ExitStack() as stage1:
                ps1, sem = alloc_in(stage1, nc.psum_tensor), sem_in(stage1)
                ps_agg = [ps1(f"ps_agg{h}", [P, HW]) for h in range(2)]
                ps_t = [ps1(f"ps_t{h}", [P, HW]) for h in range(2)]
                ps_r, ps_z, ps_hn, ps_in = (ps1(n, [P, HW]) for n in ("ps_r", "ps_z", "ps_hn", "ps_in"))

                w_cur_loaded = [sem(f"w_cur_loaded{n}") for n in range(2)]
                xn_loaded = [sem(f"xn_loaded{n}") for n in range(2)]
                a_act, a_dve = [sem(f"a_act{n}") for n in range(2)], [sem(f"a_dve{n}") for n in range(2)]
                trans_done, xt_done = sem("trans_done"), sem("xt_done")
                nat_hi_done, nat_ready = sem("nat_hi_done"), sem("nat_ready")
                agg_done, agg_hi_done, agg_split = sem("agg_done"), sem("agg_hi_done"), sem("agg_split")
                r_mm, hn_mm, in_mm, z_mm = sem("r_mm"), sem("hn_mm"), sem("in_mm"), sem("z_mm")
                r_act, n_act, z_act = sem("r_act"), sem("n_act"), sem("z_act")
                cand_done, pre_done, diff_done, zd_done = sem("cand_done"), sem("pre_done"), sem("diff_done"), sem("zd_done")
                h_done = sem("h_done")
                hT_hi_done = [sem(f"hT_hi_done{n}") for n in range(2)]
                hT_ready = [sem(f"hT_ready{n}") for n in range(2)]
                final_read, x1_done, ln2_done, fold_step = sem("final_read"), sem("x1_done"), sem("ln2_done"), sem("fold_step")
                x1z_stored = sem("x1z_stored")
                block = stage1.enter_context(nc.Block())

                def half(h):
                    return slice(h * HW, (h + 1) * HW)

                def hblocks(h):
                    return slice(h * HK, (h + 1) * HK)

                def flat(ap):
                    return ap.rearrange("p k d -> p (k d)")

                def before(q):
                    return (q - 1) % SLOTS // 2, (q - 1) % 2

                @block.sync
                def _(sp):
                    def chunk(p, l, q):
                        c = CHUNKS * (p + 1) + SLOTS * l + q - 2
                        sp.wait_ge(a_compared, c - 1)
                        sp.dma_start(a_raw[:, q % 2], adj_rows[bass.ds(c * P, P), :]).then_inc(a_raw_loaded[q % 2], 16)

                    def weights(lane, layer, slots_done):
                        sp.wait_ge(z_mm, slots_done)
                        sp.dma_start(exact(w_cur[lane][:]), wc_dram[layer]).then_inc(w_cur_loaded[lane], 16)

                    def pair(p, last):
                        if not last:
                            chunk(p, 0, 2)
                            chunk(p, 0, 3)
                        if not last:
                            for lane in range(2):
                                sp.wait_ge(hT_ready[lane], 2 * LAYERS * p + 2)
                                detach(sp)
                                sp.wait_ge(nat_ready, S_PAIR * p + 2 + 2 * lane)
                                sp.dma_start(xn[lane][:], batch(x, 2 * p + 2 + lane)).then_inc(xn_loaded[lane], 16)
                        weights(0, 1, S_PAIR * p + 2)
                        with sp.Fori(1, LAST) as l:
                            if not last:
                                chunk(p, l, 0)
                                chunk(p, l, 1)
                            weights(1, l, S_PAIR * p + SLOTS * l)
                            if not last:
                                chunk(p, l, 2)
                                chunk(p, l, 3)
                            weights(0, l + 1, S_PAIR * p + SLOTS * l + 2)
                        if not last:
                            chunk(p, LAST, 0)
                            chunk(p, LAST, 1)
                        weights(1, LAST, S_PAIR * p + SLOTS * LAST)
                        if not last:
                            weights(0, 0, S_PAIR * p + SLOTS * LAST + 2)
                            weights(1, 0, S_PAIR * (p + 1))

                    for lane in range(2):
                        sp.dma_start(exact(w_cur[lane][:]), wc_dram[0]).then_inc(w_cur_loaded[lane], 16)
                    with sp.Fori(0, PAIRS - 1) as p:
                        pair(p, False)
                    pair(PAIRS - 1, True)

                @block.gpsimd
                def _(pool):
                    def norm_out(p, lane, number, last):
                        b = 2 * p + lane
                        pool.wait_ge(x1_done, 2 * b + 2)
                        detach(pool)
                        pool.dma_start(batch(x1_dram, b), xbuf[lane][:]).then_inc(x1z_stored, 16)
                        norm_apply(pool, KB, xbuf[lane], z_nat, mv2[lane], rstd, stats_done, number + 1,
                                   norm_step, 2 * number + 1, ln2_done)
                        pool.wait_ge(ln2_done, b + 1)
                        detach(pool)
                        pool.dma_start(batch(z_dram, b), z_nat[:]).then_inc(x1z_stored, 16)
                        nc.gpsimd.tensor_tensor(z_fold[:], z_nat[:, 0:HK, :], z_nat[:, HK:KB, :], ALU.add).then_inc(fold_step, 1)
                        pool.wait_ge(fold_step, 3 * b + 1)
                        nc.gpsimd.tensor_tensor(z_fold[:, 0:2, :], z_fold[:, 0:2, :], z_fold[:, 2:4, :], ALU.add).then_inc(fold_step, 1)
                        pool.wait_ge(fold_step, 3 * b + 2)
                        nc.gpsimd.tensor_tensor(zsum[:, b, :], z_fold[:, 0, :], z_fold[:, 1, :], ALU.add).then_inc(fold_step, 1)
                        pool.wait_ge(x1z_stored, 32 * b + 32)
                        pool.wait_ge(fold_step, 3 * b + 3)
                        if not last:
                            pool.dma_start(xbuf[lane][:], batch(x, b + 2)).then_inc(xbuf_loaded[lane], 16)

                    with pool.Fori(0, PAIRS - 1) as p:
                        for lane in range(2):
                            number = 4 * p + 2 + lane
                            norm_apply(pool, KB, xn[lane], xn[lane], mv1[lane], rstd, stats_done, number + 1,
                                       norm_step, 2 * number + 1, ln1_done[lane])
                            pool.wait_ge(ln1_done[lane], p + 2)
                        for lane in range(2):
                            norm_out(p, lane, 4 * p + 4 + lane, False)
                    for lane in range(2):
                        norm_out(PAIRS - 1, lane, 4 * PAIRS - 2 + lane, True)

                @block.tensor
                def _(pe):
                    def x_to_features(lane, h):
                        for k in range(HK):
                            tr = nc.tensor.transpose(ps_t[h][:, k * P:(k + 1) * P], xn[lane][:, h * HK + k, :], ident[:])
                        tr.then_inc(xt_done, 1)

                    def state_to_tokens(s, q):
                        lane, h = before(q)
                        pe.wait_ge(h_done, s)
                        for k in range(HK):
                            tr = nc.tensor.transpose(ps_t[h][:, k * P:(k + 1) * P],
                                                     hT[lane][:, h * HW + k * P:h * HW + (k + 1) * P], ident[:])
                        tr.then_inc(trans_done, 1)

                    def aggregate(lane, h, nat_count):
                        for k in range(KB):
                            if k == 0 and nat_count is not None:
                                pe.wait_ge(nat_ready, nat_count)
                            if k == HK and nat_count is not None:
                                pe.wait_ge(nat_ready, nat_count + 1)
                            for part in (nat_hi, nat_lo):
                                mm = nc.tensor.matmul(ps_agg[h][:], part[lane][:, k, :], a_mat[lane][:, k, half(h)],
                                                      start=(k == 0 and part is nat_hi), stop=(k == KB - 1 and part is nat_lo))
                        mm.then_inc(agg_done, 1)

                    def gates(s, t, q, first):
                        lane, h = q // 2, q % 2
                        w_in, w_rec = w_cur[lane], w_hhT
                        inp = (agg_hi[h][:], agg_lo[h][:])
                        rec = (hT_hi[lane][:, half(h)], hT_lo[lane][:, half(h)])

                        def products(ps, gate, sides):
                            terms = []
                            for w, (hi, lo) in sides:
                                w_hi, w_lo = (w[:, o + gate * D:o + (gate + 1) * D] for o in (0, G))
                                terms += [(w_hi, hi), (w_hi, lo), (w_lo, hi)]
                            for n, (a, b) in enumerate(terms):
                                mm = nc.tensor.matmul(ps[:], a, b, start=(n == 0), stop=(n == len(terms) - 1))
                            return mm

                        pe.wait_ge(hT_ready[lane], 2 * t + h + 1)
                        if not first:
                            pe.wait_ge(cand_done, s)
                        products(ps_hn, 2, [(w_rec, rec)]).then_inc(hn_mm, 1)
                        pe.wait_ge(agg_split, s + 1)
                        pe.wait_ge(w_cur_loaded[lane], 16 * t + 16)
                        if not first:
                            pe.wait_ge(r_act, s)
                        products(ps_r, 0, [(w_rec, rec), (w_in, inp)]).then_inc(r_mm, 1)
                        if not first:
                            pe.wait_ge(pre_done, s)
                        products(ps_in, 2, [(w_in, inp)]).then_inc(in_mm, 1)
                        if not first:
                            pe.wait_ge(z_act, s)
                        products(ps_z, 1, [(w_rec, rec), (w_in, inp)]).then_inc(z_mm, 1)

                    def slot(p, l, q, edge="", last=False):
                        t = LAYERS * p + l
                        s = SLOTS * t + q
                        h = q % 2
                        very_first = edge == "head" and isinstance(p, int) and p == 0 and q == 0
                        if not very_first:
                            if not (isinstance(p, int) and p == 0 and edge == "head") and not (edge == "tail" and q == 3 and last):
                                pe.wait_ge(nat_ready, s + 2)
                            if edge == "head":
                                if q == 0:
                                    pe.wait_ge(hT_ready[0], 2 * t + 2)
                                else:
                                    pe.wait_ge(hT_ready[1], 2 * t + q)
                            if edge == "tail" and q == 3:
                                if last:
                                    pe.wait_ge(final_read, 4 * p + 1)
                                else:
                                    pe.wait_ge(hT_ready[0], 2 * t + 3)
                            state_to_tokens(s, q)
                        gates(s, t, q, very_first)
                        if edge == "head" and q < 2:
                            if not (isinstance(p, int) and p == 0):
                                pe.wait_ge(final_read, 4 * p - 1 + q)
                            pe.wait_ge(ln1_done[1], p + 1)
                            x_to_features(1, h)
                            if q == 0:
                                if isinstance(p, int) and p == 0:
                                    pe.wait_ge(a_compared, CHUNKS)
                                else:
                                    pe.wait_ge(a_act[1], 2 * p)
                                    pe.wait_ge(a_dve[1], 2 * p)
                        if edge == "tail" and q >= 2 and not last:
                            pe.wait_ge(final_read, 4 * p - 1 + q)
                            pe.wait_ge(ln1_done[0], p + 2)
                            x_to_features(0, h)
                            if q == 2:
                                pe.wait_ge(a_act[0], 2 * p + 2)
                                pe.wait_ge(a_dve[0], 2 * p + 2)
                        if not (edge == "tail" and q >= 2 and last):
                            aggregate(1 - q // 2, h, s + 3 if h == 0 else None)

                    def pair(p, last):
                        slot(p, 0, 2, "head")
                        slot(p, 0, 3, "")
                        with pe.Fori(1, LAST) as l:
                            for q in range(SLOTS):
                                slot(p, l, q)
                        for q in range(SLOTS):
                            slot(p, LAST, q, "tail", last)

                    pe.wait_ge(ln1_done[0], 1)
                    for h in range(2):
                        x_to_features(0, h)
                    pe.wait_ge(a_compared, KB)
                    aggregate(0, 0, 1)
                    aggregate(0, 1, None)
                    slot(0, 0, 0, "head")
                    slot(0, 0, 1, "head")
                    with pe.Fori(0, PAIRS - 1) as p:
                        pair(p, False)
                        slot(p + 1, 0, 0, "head")
                        slot(p + 1, 0, 1, "head")
                    pair(PAIRS - 1, True)
                    pe.wait_ge(final_read, 4 * PAIRS - 2)
                    state_to_tokens(S_PAIR * PAIRS, 0)

                @block.scalar
                def _(act):
                    def new_x_tokens(lane, h):
                        nc.scalar.activation(nat_hi[lane][:, hblocks(h), :], xn[lane][:, hblocks(h), :],
                                             ACT.Copy).then_inc(nat_hi_done, 1)

                    def new_x_features(lane, h, number):
                        act.wait_ge(xt_done, number + 1)
                        nc.scalar.activation(hT[lane][:, half(h)], ps_t[h][:], ACT.Copy).then_inc(hT_hi_done[lane], 1)
                        nc.scalar.activation(hT_hi[lane][:, half(h)], ps_t[h][:], ACT.Copy).then_inc(hT_hi_done[lane], 1)

                    def slot(p, l, q, edge="", last=False):
                        t = LAYERS * p + l
                        s = SLOTS * t + q
                        lane, h = q // 2, q % 2
                        before_lane, before_h = before(q)
                        at_start = isinstance(p, int) and p == 0 and edge == "head"
                        if not (edge == "tail" and q == 3 and last):
                            act.wait_ge(agg_done, s + 2)
                            nc.scalar.activation(agg_hi[1 - h][:], ps_agg[1 - h][:], ACT.Copy).then_inc(agg_hi_done, 1)
                        if not (at_start and q == 0):
                            new_batch = (edge == "tail" and q >= 1) or (edge == "head" and q == 0)
                            if not (new_batch and last):
                                act.wait_ge(trans_done, s)
                                if new_batch:
                                    if q == 0:
                                        act.wait_ge(ln1_done[1], p + 1)
                                    else:
                                        act.wait_ge(ln1_done[before_lane], p + 2)
                                    new_x_tokens(before_lane, before_h)
                                else:
                                    nc.scalar.activation(flat(nat_hi[before_lane][:, hblocks(before_h), :]), ps_t[before_h][:],
                                                         ACT.Copy).then_inc(nat_hi_done, 1)
                        act.wait_ge(r_mm, s + 1)
                        if not (at_start and q == 0):
                            act.wait_ge(h_done, s)
                        nc.scalar.activation(cand[:], ps_r[:], ACT.Sigmoid, bias=bias_rz[:, 0:1]).then_inc(r_act, 1)
                        act.wait_ge(pre_done, s + 1)
                        nc.scalar.activation(cand[:], cand[:], ACT.Tanh, bias=bias_ih[:, 2:3]).then_inc(n_act, 1)
                        act.wait_ge(z_mm, s + 1)
                        nc.scalar.activation(gate_z[:], ps_z[:], ACT.Sigmoid, bias=bias_rz[:, 1:2]).then_inc(z_act, 1)
                        if edge == "head" and q < 2:
                            new_x_features(1, h, 4 * p + 2 + h)
                        if edge == "tail" and q >= 2 and not last:
                            new_x_features(0, h, 4 * p + 4 + h)
                        if edge == "tail" and not last:
                            act.wait_ge(a_compared, CHUNKS * (p + 1) + (lane + 1) * KB)
                            act.wait_ge(agg_done, 4 * t + 2 * lane + 2)
                            nc.scalar.activation(a_mat[lane][:, 4 * h:4 * h + 2, :], a_next[:, KB * lane + 4 * h:KB * lane + 4 * h + 2, :],
                                                 ACT.Copy).then_inc(a_act[lane], 1)
                        if edge != "tail":
                            act.wait_ge(h_done, s + 1)
                            nc.scalar.activation(hT_hi[lane][:, half(h)], hT[lane][:, half(h)], ACT.Copy).then_inc(hT_hi_done[lane], 2)

                    def pair(p, last):
                        slot(p, 0, 2)
                        slot(p, 0, 3)
                        with act.Fori(1, LAST) as l:
                            for q in range(SLOTS):
                                slot(p, l, q)
                        for q in range(SLOTS):
                            slot(p, LAST, q, "tail", last)

                    act.wait_ge(ln1_done[0], 1)
                    new_x_tokens(0, 0)
                    new_x_tokens(0, 1)
                    new_x_features(0, 0, 0)
                    new_x_features(0, 1, 1)
                    act.wait_ge(ln1_done[1], 1)
                    new_x_tokens(1, 0)
                    new_x_tokens(1, 1)
                    act.wait_ge(agg_done, 1)
                    nc.scalar.activation(agg_hi[0][:], ps_agg[0][:], ACT.Copy).then_inc(agg_hi_done, 1)
                    slot(0, 0, 0, "head")
                    slot(0, 0, 1, "head")
                    with act.Fori(0, PAIRS - 1) as p:
                        pair(p, False)
                        slot(p + 1, 0, 0, "head")
                        slot(p + 1, 0, 1, "head")
                    pair(PAIRS - 1, True)

                @block.vector
                def _(dve):
                    def new_x_tokens(lane, h):
                        nc.vector.tensor_tensor(nat_lo[lane][:, hblocks(h), :], xn[lane][:, hblocks(h), :],
                                                exact(nat_hi[lane][:, hblocks(h), :]), ALU.subtract).then_inc(nat_ready, 1)

                    def new_x_features(lane, h, n):
                        dve.wait_ge(hT_hi_done[lane], 2 * n + 2)
                        nc.vector.tensor_tensor(hT_lo[lane][:, half(h)], ps_t[h][:], exact(hT_hi[lane][:, half(h)]),
                                                ALU.subtract).then_inc(hT_ready[lane], 1)

                    def final_state(p, lane, h):
                        n = 4 * p + 2 * lane + h
                        mask = mask_tok[:, 2 * p + lane, hblocks(h)].unsqueeze(2).to_broadcast([P, HK, D])
                        if h == 0:
                            dve.wait_ge(xbuf_loaded[lane], 16 * p + 16)
                        if (lane, h) != (0, 0):
                            dve.wait_ge(x1_done, n)
                        nc.vector.tensor_tensor(masked[:], ps_t[h][:].rearrange("p (k d) -> p k d", d=D), mask,
                                                ALU.mult).then_inc(final_read, 1)
                        dve.wait_ge(final_read, n + 1)
                        nc.vector.tensor_tensor(xbuf[lane][:, hblocks(h), :], xbuf[lane][:, hblocks(h), :], masked[:],
                                                ALU.add).then_inc(x1_done, 1)

                    def slot(p, l, q, edge="", last=False):
                        t = LAYERS * p + l
                        s = SLOTS * t + q
                        lane, h = q // 2, q % 2
                        before_lane, before_h = before(q)
                        at_start = isinstance(p, int) and p == 0 and edge == "head"
                        if not (edge == "tail" and q == 3 and last):
                            dve.wait_ge(agg_hi_done, s + 2)
                            nc.vector.tensor_tensor(agg_lo[1 - h][:], ps_agg[1 - h][:], exact(agg_hi[1 - h][:]),
                                                    ALU.subtract).then_inc(agg_split, 1)
                        if not (at_start and q == 0):
                            new_batch = (edge == "tail" and q >= 1) or (edge == "head" and q == 0)
                            if not (new_batch and last):
                                dve.wait_ge(nat_hi_done, s + 4)
                                if new_batch:
                                    new_x_tokens(before_lane, before_h)
                                else:
                                    nc.vector.tensor_tensor(flat(nat_lo[before_lane][:, hblocks(before_h), :]), ps_t[before_h][:],
                                                            exact(flat(nat_hi[before_lane][:, hblocks(before_h), :])),
                                                            ALU.subtract).then_inc(nat_ready, 1)
                            if new_batch:
                                dve.wait_ge(trans_done, s)
                                final_state(p - 1 if q == 0 else p, before_lane, before_h)
                        dve.wait_ge(r_act, s + 1)
                        dve.wait_ge(hn_mm, s + 1)
                        nc.vector.scalar_tensor_tensor(cand[:], ps_hn[:], bias_hh[:, 2:3], cand[:], ALU.add, ALU.mult).then_inc(cand_done, 1)
                        dve.wait_ge(in_mm, s + 1)
                        dve.wait_ge(cand_done, s + 1)
                        nc.vector.tensor_tensor(cand[:], ps_in[:], cand[:], ALU.add).then_inc(pre_done, 1)
                        if not last and (edge == "" or (edge == "tail" and q < 2)):
                            c = CHUNKS * (p + 1) + SLOTS * l + q - 2
                            dve.wait_ge(a_raw_loaded[q % 2], 16 * (KB * (p + 1) + 2 * l + q // 2))
                            nc.vector.tensor_scalar(a_next[:, SLOTS * l + q - 2, :], a_raw[:, q % 2], 0.0, None,
                                                    ALU.not_equal).then_inc(a_compared, 1)
                        if edge == "tail" and not last:
                            dve.wait_ge(agg_done, 4 * t + 2 * lane + 2)
                            nc.vector.tensor_copy(a_mat[lane][:, 4 * h + 2:4 * h + 4, :],
                                                  a_next[:, KB * lane + 4 * h + 2:KB * lane + 4 * h + 4, :]).then_inc(a_dve[lane], 1)
                        if edge == "" and isinstance(l, int) and not last:
                            dve.wait_ge(xn_loaded[h], 16 * p + 16)
                            token_stats(dve, KB, xn[h], stat6, mv1[h], stats_step, 4 * p + 3 + h, stats_done)
                        if edge == "tail" and q == 3:
                            number = 4 * p + (2 if last else 4)
                            dve.wait_ge(x1_done, 4 * p + 2)
                            token_stats(dve, KB, xbuf[0], stat6, mv2[0], stats_step, number + 1, stats_done)
                        if edge == "head" and q == 1 and not at_start:
                            for n in range(2):
                                dve.wait_ge(a_act[n], 2 * p)
                            dve.wait_ge(x1_done, 4 * p)
                            token_stats(dve, KB, xbuf[1], stat6, mv2[1], stats_step, 4 * p + 2, stats_done)
                        dve.wait_ge(n_act, s + 1)
                        nc.vector.tensor_tensor(diff[:], hT[lane][:, half(h)], cand[:], ALU.subtract).then_inc(diff_done, 1)
                        dve.wait_ge(z_act, s + 1)
                        dve.wait_ge(diff_done, s + 1)
                        nc.vector.tensor_tensor(gate_z[:], gate_z[:], diff[:], ALU.mult).then_inc(zd_done, 1)
                        dve.wait_ge(zd_done, s + 1)
                        nc.vector.tensor_tensor(hT[lane][:, half(h)], cand[:], gate_z[:], ALU.add).then_inc(h_done, 1)
                        if edge == "head" and q < 2:
                            new_x_features(1, h, 2 * t + h)
                        if edge == "tail" and q >= 2 and not last:
                            new_x_features(0, h, 2 * t + 2 + h)
                        if edge != "tail":
                            n = 2 * t + 2 + h
                            dve.wait_ge(hT_hi_done[lane], 2 * n + 2)
                            nc.vector.tensor_tensor(hT_lo[lane][:, half(h)], hT[lane][:, half(h)], exact(hT_hi[lane][:, half(h)]),
                                                    ALU.subtract).then_inc(hT_ready[lane], 1)

                    def pair(p, last):
                        slot(p, 0, 2, "", last)
                        slot(p, 0, 3, "", last)
                        with dve.Fori(1, LAST) as l:
                            for q in range(SLOTS):
                                slot(p, l, q, "", last)
                        for q in range(SLOTS):
                            slot(p, LAST, q, "tail", last)

                    for lane in range(2):
                        for h in range(2):
                            dve.wait_ge(nat_hi_done, 2 * lane + h + 1)
                            new_x_tokens(lane, h)
                        if lane == 0:
                            new_x_features(0, 0, 0)
                            new_x_features(0, 1, 1)
                    dve.wait_ge(agg_hi_done, 1)
                    nc.vector.tensor_tensor(agg_lo[0][:], ps_agg[0][:], exact(agg_hi[0][:]), ALU.subtract).then_inc(agg_split, 1)
                    slot(0, 0, 0, "head")
                    slot(0, 0, 1, "head")
                    with dve.Fori(0, PAIRS - 1) as p:
                        pair(p, False)
                        slot(p + 1, 0, 0, "head")
                        slot(p + 1, 0, 1, "head")
                    pair(PAIRS - 1, True)
                    dve.wait_ge(trans_done, S_PAIR * PAIRS)
                    final_state(PAIRS - 1, 1, 1)
                    dve.wait_ge(x1_done, 4 * PAIRS)
                    token_stats(dve, KB, xbuf[1], stat6, mv2[1], stats_step, 4 * PAIRS, stats_done)

        with ExitStack() as phase2:
            sb, ps, sem = alloc_in(phase2, nc.sbuf_tensor), alloc_in(phase2, nc.psum_tensor), sem_in(phase2)
            C = B * TOP_K
            w_raw = [sb(f"w_raw{i}", [P, TOP_K, 2 * F]) for i in range(2)]
            w_hi = [sb(f"w_hi{i}", [P, TOP_K, 2 * F], F32R) for i in range(2)]
            w_lo = [sb(f"w_lo{i}", [P, TOP_K, 2 * F], F32R) for i in range(2)]
            z_in = [sb(f"z_in{i}", [P, KB, D]) for i in range(2)]
            z_res = [sb(f"z_res{i}", [P, KB, D]) for i in range(2)]
            x_res = [sb(f"x_res{i}", [P, KB, D]) for i in range(2)]
            zT_hi, zT_lo = sb("zT_hi", [P, N], F32R), sb("zT_lo", [P, N], F32R)
            act_out = [sb(f"act_out{i}", [P, HW]) for i in range(2)]
            g_hi = [sb(f"g_hi{i}", [P, HW], F32R) for i in range(4)]
            g_lo = [sb(f"g_lo{i}", [P, HW], F32R) for i in range(4)]
            yT = [sb(f"yT{h}", [P, HW]) for h in range(2)]
            res = [sb(f"res{h}", [P, HK, D]) for h in range(2)]
            stat6b = sb("stat6b", [P, HK, 6])
            mvb = [sb(f"mvb{h}", [P, HK, 2]) for h in range(2)]
            rstdb = sb("rstdb", [P, HK])
            b1_sel = sb("b1_sel", [P, FB, C])
            b2_mix = sb("b2_mix", [P, B])
            top_w_all = sb("top_w_all", [P, C])
            gamma_all, beta_all = sb("gamma_all", [P, D]), sb("beta_all", [P, D])
            expert_row = sb("expert_row", [1, C], U32)
            z_in_loaded = [sem(f"z_in_loaded{i}") for i in range(2)]
            z_res_loaded = [sem(f"z_res_loaded{i}") for i in range(2)]
            x_res_loaded = [sem(f"x_res_loaded{i}") for i in range(2)]
            row_loaded = sem("row_loaded")

            with ExitStack() as routing:
                sbr, psr, semr = alloc_in(routing, nc.sbuf_tensor), alloc_in(routing, nc.psum_tensor), sem_in(routing)
                Wr_sb, br_row = sbr("Wr_sb", [P, E]), sbr("br_row", [1, E])
                b1_sb, b2_sb = sbr("b1_sb", [E, F]), sbr("b2_sb", [E, D])
                gb_row = sbr("gb_row", [1, 2, D])
                ones = sbr("ones", [E, P])
                mean_w = sbr("mean_w", [P, 1])
                meanT = sbr("meanT", [P, B])
                iota_e = sbr("iota_e", [B, E])
                logits, rw, rw2, e2 = (sbr(n, [B, E]) for n in ("logits", "rw", "rw2", "e2"))
                peak, total, inv_total = sbr("peak", [B, 4]), sbr("total", [B, 4]), sbr("inv_total", [B, 4])
                load, over, quot = (sbr(n, [B, E]) for n in ("load", "over", "quot"))
                top, top_i, top_f = sbr("top", [B, 8]), sbr("top_i", [B, 8], U32), sbr("top_f", [B, 8])
                onehot, w_dense = sbr("onehot", [B, TOP_K, E]), sbr("w_dense", [B, E])
                top_e, top_w = sbr("top_e", [B, TOP_K]), sbr("top_w", [B, TOP_K])
                w_diag = sbr("w_diag", [B, TOP_K, B])
                oh_T, wd_T = sbr("oh_T", [E, C]), sbr("wd_T", [E, B])
                ps_mean, ps_small = psr("ps_mean", [P, B]), psr("ps_small", [P, 512])
                ps_load, ps_t8 = psr("ps_load", [P, 512]), psr("ps_t8", [P, 512])
                ps_sel, ps_bc = psr("ps_sel", [P, 512]), psr("ps_bc", [P, 512])
                params_loaded = semr("params_loaded")
                pe_step, act_step, dve_step, pool_step = (semr(n) for n in ("pe_step", "act_step", "dve_step", "pool_step"))
                block = routing.enter_context(nc.Block())

                @block.sync
                def _(sp):
                    for dst, src in ((Wr_sb[:], Wr), (br_row[:], br.rearrange("(o e) -> o e", o=1)), (b1_sb[:], b1), (b2_sb[:], b2),
                                     (gb_row[:, 0, :], gamma.rearrange("(o d) -> o d", o=1)),
                                     (gb_row[:, 1, :], beta.rearrange("(o d) -> o d", o=1))):
                        sp.dma_start(dst, src).then_inc(params_loaded, 16)
                    for i in range(2):
                        sp.dma_start(z_in[i][:], batch(z_dram, i)).then_inc(z_in_loaded[i], 16)
                    sp.wait_ge(dve_step, 17)
                    for k in range(TOP_K):
                        sp.dma_start(expert_row[:, k * B:(k + 1) * B].rearrange("o (b c) -> o b c", c=1),
                                     top_i[:, k:k + 1]).then_inc(row_loaded, 16)
                    sp.wait_ge(row_loaded, 16 * TOP_K)

                @block.gpsimd
                def _(pool):
                    nc.gpsimd.memset(mean_w[:], 1.0 / N).then_inc(pool_step, 1)
                    nc.gpsimd.memset(ones[:], 1.0).then_inc(pool_step, 1)
                    nc.gpsimd.iota(iota_e[:], pattern=[[1, E]], base=0, channel_multiplier=0,
                                   allow_small_or_imprecise_dtypes=True).then_inc(pool_step, 1)
                    for i in range(2):
                        pool.dma_start(z_res[i][:], batch(z_dram, i)).then_inc(z_res_loaded[i], 16)
                        pool.dma_start(x_res[i][:], batch(x1_dram, i)).then_inc(x_res_loaded[i], 16)

                @block.tensor
                def _(pe):
                    pe.wait_ge(pool_step, 3)
                    for b in range(B):
                        mm = nc.tensor.matmul(ps_mean[:, b:b + 1], zsum[:, b, :], mean_w[:], start=True, stop=True)
                    mm.then_inc(pe_step, 1)
                    pe.wait_ge(params_loaded, 96)
                    nc.tensor.matmul(ps_bc[:, 256:384], ones[0:1, :], gb_row[:, 0, :], start=True, stop=True)
                    nc.tensor.matmul(ps_bc[:, 384:512], ones[0:1, :], gb_row[:, 1, :], start=True, stop=True).then_inc(pe_step, 1)
                    pe.wait_ge(dve_step, 1)
                    nc.tensor.matmul(ps_small[0:B, 0:E], meanT[:], Wr_sb[:], start=True, stop=False)
                    nc.tensor.matmul(ps_small[0:B, 0:E], ones[0:1, 0:B], br_row[:], start=False, stop=True).then_inc(pe_step, 1)
                    pe.wait_ge(dve_step, 5)
                    nc.tensor.matmul(ps_load[0:B, 0:E], ones[:, 0:B], rw[:], start=True, stop=True).then_inc(pe_step, 1)
                    pe.wait_ge(dve_step, 25)
                    for k in range(TOP_K):
                        nc.tensor.transpose(ps_t8[0:E, k * B:(k + 1) * B], onehot[:, k, :], ident[0:B, 0:B])
                    nc.tensor.transpose(ps_t8[0:E, C:C + B], w_dense[:], ident[0:B, 0:B]).then_inc(pe_step, 1)
                    pe.wait_ge(dve_step, 27)
                    for f in range(FB):
                        nc.tensor.matmul(ps_sel[:, f * C:(f + 1) * C], b1_sb[:, f * P:(f + 1) * P], oh_T[:], start=True, stop=True)
                    nc.tensor.matmul(ps_sel[:, FB * C:FB * C + B], b2_sb[:], wd_T[:], start=True, stop=True)
                    nc.tensor.matmul(ps_bc[:, 0:C], ones[:], w_diag[:].rearrange("b k c -> b (k c)"), start=True,
                                     stop=True).then_inc(pe_step, 1)

                @block.scalar
                def _(act):
                    act.wait_ge(dve_step, 3)
                    nc.scalar.activation(rw[:], logits[:], ACT.Exp, bias=peak[:, 0:1], accum_out=total[:, 0:1]).then_inc(act_step, 1)
                    act.wait_ge(dve_step, 13)
                    nc.scalar.activation(e2[:], rw2[:], ACT.Exp, bias=peak[:, 1:2], accum_out=total[:, 1:2]).then_inc(act_step, 1)
                    act.wait_ge(dve_step, 18)
                    nc.scalar.activation(top_e[:], top[:, 0:TOP_K], ACT.Exp, bias=peak[:, 2:3], accum_out=total[:, 2:3]).then_inc(act_step, 1)

                @block.vector
                def _(dve):
                    def step(ins, n):
                        ins.then_inc(dve_step, 1)
                        dve.wait_ge(dve_step, n)

                    dve.wait_ge(pe_step, 1)
                    step(nc.vector.tensor_copy(meanT[:], ps_mean[:]), 1)
                    dve.wait_ge(pe_step, 3)
                    step(nc.vector.tensor_copy(logits[:], ps_small[0:B, 0:E]), 2)
                    step(nc.vector.tensor_reduce(peak[:, 0:1], logits[:], AX_X, ALU.max, negate=True), 3)
                    dve.wait_ge(act_step, 1)
                    step(nc.vector.reciprocal(inv_total[:, 0:1], total[:, 0:1]), 4)
                    step(nc.vector.tensor_scalar(rw[:], rw[:], inv_total[:, 0:1], None, ALU.mult), 5)
                    dve.wait_ge(pe_step, 4)
                    step(nc.vector.tensor_scalar(load[:], ps_load[0:B, 0:E], float(N), CAPACITY, ALU.mult, ALU.max), 6)
                    step(nc.vector.reciprocal(quot[:], load[:]), 7)
                    step(nc.vector.tensor_scalar(over[:], load[:], CAPACITY, None, ALU.is_gt), 8)
                    step(nc.vector.scalar_tensor_tensor(quot[:], quot[:], CAPACITY, over[:], ALU.mult, ALU.mult), 9)
                    step(nc.vector.tensor_scalar(over[:], over[:], -1.0, 1.0, ALU.mult, ALU.add), 10)
                    step(nc.vector.tensor_tensor(quot[:], quot[:], over[:], ALU.add), 11)
                    step(nc.vector.tensor_tensor(rw2[:], rw[:], quot[:], ALU.mult), 12)
                    step(nc.vector.tensor_reduce(peak[:, 1:2], rw2[:], AX_X, ALU.max, negate=True), 13)
                    dve.wait_ge(act_step, 2)
                    step(nc.vector.reciprocal(inv_total[:, 1:2], total[:, 1:2]), 14)
                    step(nc.vector.tensor_scalar(rw2[:], e2[:], inv_total[:, 1:2], None, ALU.mult), 15)
                    step(nc.vector.max(top[:], rw2[:]), 16)
                    step(nc.vector.max_index(top_i[:], top[:], rw2[:]), 17)
                    step(nc.vector.tensor_scalar(peak[:, 2:3], top[:, 0:1], -1.0, None, ALU.mult), 18)
                    step(nc.vector.tensor_copy(top_f[:], top_i[:]), 19)
                    dve.wait_ge(act_step, 3)
                    step(nc.vector.reciprocal(inv_total[:, 2:3], total[:, 2:3]), 20)
                    step(nc.vector.tensor_scalar(top_w[:], top_e[:], inv_total[:, 2:3], None, ALU.mult), 21)
                    dve.wait_ge(pool_step, 3)
                    for k in range(TOP_K):
                        ins = nc.vector.tensor_scalar(onehot[:, k, :], iota_e[:], top_f[:, k:k + 1], None, ALU.is_equal)
                    step(ins, 22)
                    for k in range(TOP_K):
                        ins = nc.vector.tensor_scalar(w_diag[:, k, :], ident[0:B, 0:B], top_w[:, k:k + 1], None, ALU.mult)
                    step(ins, 23)
                    step(nc.vector.tensor_scalar(w_dense[:], onehot[:, 0, :], top_w[:, 0:1], None, ALU.mult), 24)
                    step(nc.vector.scalar_tensor_tensor(w_dense[:], onehot[:, 1, :], top_w[:, 1:2], w_dense[:], ALU.mult, ALU.add), 25)
                    dve.wait_ge(pe_step, 5)
                    step(nc.vector.tensor_copy(oh_T[:], ps_t8[0:E, 0:C]), 26)
                    step(nc.vector.tensor_copy(wd_T[:], ps_t8[0:E, C:C + B]), 27)
                    dve.wait_ge(pe_step, 6)
                    nc.vector.tensor_copy(b1_sel[:].rearrange("p f c -> p (f c)"), ps_sel[:, 0:FB * C])
                    nc.vector.tensor_copy(b2_mix[:], ps_sel[:, FB * C:FB * C + B])
                    nc.vector.tensor_copy(top_w_all[:], ps_bc[:, 0:C])
                    nc.vector.tensor_copy(gamma_all[:], ps_bc[:, 256:384])
                    step(nc.vector.tensor_copy(beta_all[:], ps_bc[:, 384:512]), 28)

            ps_l1 = [ps(f"ps_l1_{i}", [P, HW]) for i in range(4)]
            ps_y = [ps(f"ps_y{h}", [P, HW]) for h in range(2)]
            ps_zt, ps_yt = ps("ps_zt", [P, HW]), ps("ps_yt", [P, HW])
            w_raw_loaded = [sem(f"w_raw_loaded{i}") for i in range(2)]
            w_hi_done, w_split = sem("w_hi_done"), sem("w_split")
            zt_done, zt_hi_done, zt_split = sem("zt_done"), sem("zt_hi_done"), sem("zt_split")
            l1_done, gelu_done, g_hi_done, g_split = (
                sem(n) for n in ("l1_done", "gelu_done", "g_hi_done", "g_split"))
            y_mm, y_copied, yt_done, res_added, res_step, res_stats = (
                sem(n) for n in ("y_mm", "y_copied", "yt_done", "res_added", "res_step", "res_stats"))
            out_step, out_normed = sem("out_step"), sem("out_normed")
            out_stored = [sem(f"out_stored{h}") for h in range(2)]
            block = phase2.enter_context(nc.Block())

            def number(bt):
                return 2 * bt[0] + bt[1]

            def following(bt):
                return (bt[0], 1) if bt[1] == 0 else (bt[0] + 1, 0)

            def ahead(bt, u, n):
                return (bt, u + n) if u + n < UNITS else (following(bt), u + n - UNITS)

            def half(h):
                return slice(h * HW, (h + 1) * HW)

            def hblocks(h):
                return slice(h * HK, (h + 1) * HK)

            def steps(eng, step):
                def round_(bt, last=False):
                    for u in range(3, UNITS):
                        step(bt, u, False, last)
                    if not last:
                        for u in range(3):
                            step(following(bt), u, False, False)

                for u in range(3):
                    step((0, 0), u, True, False)
                round_((0, 0))
                with eng.Fori(0, B // 2 - 1) as i:
                    round_((i, 1))
                    round_((i + 1, 0))
                round_((B // 2 - 1, 1), True)

            @block.sync
            def _(sp):
                def gather(bt):
                    i, parity = bt
                    for k in range(TOP_K):
                        e = sp.value_load(expert_row[0:1, bass.ds(k * B + number(bt), 1)], min_val=0, max_val=E - 1)
                        sp.dma_start(w_raw[parity][:, k, 0:F], W1[e]).then_inc(w_raw_loaded[parity], 16)
                        sp.dma_start(w_raw[parity][:, k, F:2 * F].rearrange("p (c d) -> p c d", d=D),
                                     W2.rearrange("e (c p) d -> e p c d", p=P)[e]).then_inc(w_raw_loaded[parity], 16)

                gather((0, 0))
                gather((0, 1))
                with sp.Fori(0, B // 2 - 1) as i:
                    for parity in range(2):
                        b = 2 * i + parity
                        sp.wait_ge(zt_done, 2 * b + 2)
                        sp.dma_start(z_in[parity][:], batch(z_dram, b + 2)).then_inc(z_in_loaded[parity], 16)
                        sp.wait_ge(w_split, 2 * b + 2)
                        gather((i + 1, parity))

            @block.gpsimd
            def _(pool):
                def finish(bt, h, last=False):
                    i, parity = bt
                    n = 2 * number(bt) + h
                    shape = [P, HK, D]
                    norm_apply(pool, HK, res[h], res[h], mvb[h], rstdb, res_stats, n + 1, out_step, 5 * n + 1, out_normed)
                    pool.wait_ge(out_normed, n + 1)
                    nc.gpsimd.tensor_tensor(res[h][:], res[h][:], gamma_all[:].unsqueeze(1).to_broadcast(shape), ALU.mult).then_inc(out_step, 1)
                    pool.wait_ge(out_step, 5 * n + 3)
                    nc.gpsimd.tensor_tensor(res[h][:], res[h][:], beta_all[:].unsqueeze(1).to_broadcast(shape), ALU.add).then_inc(out_step, 1)
                    pool.wait_ge(out_step, 5 * n + 4)
                    pool.wait_ge(x_res_loaded[parity], 16 * i + 16)
                    nc.gpsimd.tensor_tensor(res[h][:], res[h][:], x_res[parity][:, hblocks(h), :], ALU.add).then_inc(out_step, 1)
                    pool.wait_ge(out_step, 5 * n + 5)
                    pool.dma_start(batch(out, number(bt))[:, hblocks(h), :], res[h][:]).then_inc(out_stored[h], 16)
                    if h == 1 and not last:
                        pool.dma_start(z_res[parity][:], batch(z_dram, number(bt) + 2)).then_inc(z_res_loaded[parity], 16)
                        pool.dma_start(x_res[parity][:], batch(x1_dram, number(bt) + 2)).then_inc(x_res_loaded[parity], 16)

                with pool.Fori(0, B // 2 - 1) as i:
                    for parity in range(2):
                        for h in range(2):
                            finish((i, parity), h)
                for parity in range(2):
                    for h in range(2):
                        finish((B // 2 - 1, parity), h, last=True)
                for h in range(2):
                    pool.wait_ge(out_stored[h], 16 * B)

            @block.tensor
            def _(pe):
                def tokens_to_features(bt, h):
                    n = 2 * number(bt) + h
                    pe.wait_ge(z_in_loaded[bt[1]], 16 * bt[0] + 16)
                    if not (isinstance(n, int) and n == 0):
                        pe.wait_ge(zt_split, n)
                    for k in range(HK):
                        tr = nc.tensor.transpose(ps_zt[:, k * P:(k + 1) * P], z_in[bt[1]][:, h * HK + k, :], ident[:])
                    tr.then_inc(zt_done, 1)

                def features_to_tokens(bt, h):
                    n = 2 * number(bt) + h
                    pe.wait_ge(y_copied, n + 1)
                    if not (isinstance(n, int) and n == 0):
                        pe.wait_ge(res_added, n)
                    for k in range(HK):
                        tr = nc.tensor.transpose(ps_yt[:, k * P:(k + 1) * P], yT[h][:, k * P:(k + 1) * P], ident[:])
                    tr.then_inc(yt_done, 1)

                def first_product(bt, u):
                    h, k, f = u // 4, u // 2 % 2, u % 2
                    if u % 4 == 0:
                        pe.wait_ge(zt_split, 2 * number(bt) + h + 1)
                    if u == 0:
                        pe.wait_ge(w_split, 2 * number(bt) + 2)
                    w_h, w_l = (w[bt[1]][:, k, f * P:(f + 1) * P] for w in (w_hi, w_lo))
                    z_h, z_l = zT_hi[:, half(h)], zT_lo[:, half(h)]
                    nc.tensor.matmul(ps_l1[u % 4][:], w_h, z_h, start=True, stop=False)
                    nc.tensor.matmul(ps_l1[u % 4][:], w_h, z_l, start=False, stop=False)
                    nc.tensor.matmul(ps_l1[u % 4][:], w_l, z_h, start=False, stop=True).then_inc(l1_done, 1)

                def second_product(bt, u):
                    h, k, f = u // 4, u // 2 % 2, u % 2
                    pe.wait_ge(g_split, UNITS * number(bt) + u + 1)
                    w_h, w_l = (w[bt[1]][:, k, F + f * P:F + (f + 1) * P] for w in (w_hi, w_lo))
                    nc.tensor.matmul(ps_y[h][:], w_h, g_hi[u % 4][:], start=(u % 4 == 0), stop=False)
                    nc.tensor.matmul(ps_y[h][:], w_h, g_lo[u % 4][:], start=False, stop=False)
                    mm = nc.tensor.matmul(ps_y[h][:], w_l, g_hi[u % 4][:], start=False, stop=(u % 4 == 3))
                    if u % 4 == 3:
                        mm.then_inc(y_mm, 1)

                def step(bt, u, first, last):
                    nbt, nu = ahead(bt, u, 2)
                    if not (last and u + 2 >= UNITS):
                        first_product(nbt, nu)
                    second_product(bt, u)
                    if u == 0:
                        tokens_to_features(bt, 1)
                    if u == 1 and not first:
                        features_to_tokens((bt[0] - 1, 1) if bt[1] == 0 else (bt[0], 0), 1)
                    if u == 3 and not last:
                        tokens_to_features(following(bt), 0)
                    if u == 5:
                        features_to_tokens(bt, 0)

                tokens_to_features((0, 0), 0)
                first_product((0, 0), 0)
                first_product((0, 0), 1)
                steps(pe, step)
                features_to_tokens((B // 2 - 1, 1), 1)

            @block.scalar
            def _(act):
                def split_tokens(bt, h):
                    act.wait_ge(zt_done, 2 * number(bt) + h + 1)
                    nc.scalar.activation(zT_hi[:, half(h)], ps_zt[:], ACT.Copy).then_inc(zt_hi_done, 1)

                def copy_mixture(bt, h):
                    act.wait_ge(y_mm, 2 * number(bt) + h + 1)
                    detach(act)
                    nc.scalar.activation(yT[h][:], ps_y[h][:], ACT.Identity,
                                         bias=b2_mix[:, bass.ds(number(bt), 1)]).then_inc(y_copied, 1)

                def activate(bt, u):
                    k, f = u // 2 % 2, u % 2
                    U = UNITS * number(bt) + u
                    col = k * B + number(bt)
                    act.wait_ge(l1_done, U + 1)
                    if not (isinstance(U, int) and U < 2):
                        act.wait_ge(g_split, U - 1)
                    detach(act)
                    nc.scalar.activation(act_out[u % 2][:], ps_l1[u % 4][:], ACT.Gelu,
                                         bias=b1_sel[:, f, bass.ds(col, 1)]).then_inc(gelu_done, 1)
                    act.wait_ge(gelu_done, U + 1)
                    detach(act)
                    nc.scalar.activation(g_hi[u % 4][:], act_out[u % 2][:], ACT.Copy,
                                         scale=top_w_all[:, bass.ds(col, 1)]).then_inc(g_hi_done, 1)

                def step(bt, u, first, last):
                    if not (last and u == UNITS - 1):
                        activate(*ahead(bt, u, 1))
                    if u == 0:
                        split_tokens(bt, 1)
                        if not first:
                            copy_mixture((bt[0] - 1, 1) if bt[1] == 0 else (bt[0], 0), 1)
                    if u == 4:
                        if not last:
                            split_tokens(following(bt), 0)
                        copy_mixture(bt, 0)

                split_tokens((0, 0), 0)
                activate((0, 0), 0)
                steps(act, step)
                copy_mixture((B // 2 - 1, 1), 1)

            @block.vector
            def _(dve):
                def split_tokens(bt, h):
                    dve.wait_ge(zt_hi_done, 2 * number(bt) + h + 1)
                    nc.vector.tensor_tensor(zT_lo[:, half(h)], ps_zt[:], exact(zT_hi[:, half(h)]), ALU.subtract).then_inc(zt_split, 1)

                def split_weights(bt, k):
                    i, parity = bt
                    if k == 0:
                        dve.wait_ge(w_raw_loaded[parity], 32 * TOP_K * i + 32 * TOP_K)
                        if not (isinstance(i, int) and number(bt) <= 1):
                            dve.wait_ge(y_mm, 2 * (number(bt) - 1))
                    nc.vector.tensor_copy(w_hi[parity][:, k, :], w_raw[parity][:, k, :]).then_inc(w_hi_done, 1)
                    dve.wait_ge(w_hi_done, 2 * number(bt) + k + 1)
                    nc.vector.tensor_tensor(w_lo[parity][:, k, :], w_raw[parity][:, k, :], exact(w_hi[parity][:, k, :]),
                                            ALU.subtract).then_inc(w_split, 1)

                def split_activations(bt, u):
                    col = u // 2 % 2 * B + number(bt)
                    dve.wait_ge(g_hi_done, UNITS * number(bt) + u + 1)
                    nc.vector.scalar_tensor_tensor(g_lo[u % 4][:], act_out[u % 2][:], top_w_all[:, bass.ds(col, 1)],
                                                   exact(g_hi[u % 4][:]), ALU.mult, ALU.subtract).then_inc(g_split, 1)

                def add_residual(bt, h):
                    i, parity = bt
                    n = 2 * number(bt) + h
                    dve.wait_ge(yt_done, n + 1)
                    dve.wait_ge(z_res_loaded[parity], 16 * i + 16)
                    if not (isinstance(i, int) and number(bt) == 0):
                        dve.wait_ge(out_stored[h], 16 * number(bt))
                    nc.vector.tensor_tensor(res[h][:], ps_yt[:].rearrange("p (k d) -> p k d", d=D), z_res[parity][:, hblocks(h), :],
                                            ALU.add).then_inc(res_added, 1)
                    dve.wait_ge(res_added, n + 1)
                    token_stats(dve, HK, res[h], stat6b, mvb[h], res_step, n + 1, res_stats)

                def step(bt, u, first, last):
                    if not (last and u == UNITS - 1):
                        split_activations(*ahead(bt, u, 1))
                    if u == 0:
                        split_tokens(bt, 1)
                    if u == 2 and not first:
                        add_residual((bt[0] - 1, 1) if bt[1] == 0 else (bt[0], 0), 1)
                    if u in (3, 4) and not last:
                        split_weights(following(bt), u - 3)
                    if u == 4 and not last:
                        split_tokens(following(bt), 0)
                    if u == 6:
                        add_residual(bt, 0)

                split_tokens((0, 0), 0)
                for k in range(TOP_K):
                    split_weights((0, 0), k)
                split_activations((0, 0), 0)
                steps(dve, step)
                add_residual((B // 2 - 1, 1), 1)


_INS = ["x", "adj", "nodemask", "L0_gnn_weight", "L0_gnn_w_ih", "L0_gnn_w_hh", "L0_gnn_b_ih", "L0_gnn_b_hh", "L0_ffn_Wr",
        "L0_ffn_br", "L0_ffn_W1", "L0_ffn_b1", "L0_ffn_W2", "L0_ffn_b2", "L0_ffn_gamma", "L0_ffn_beta"]


def kernel(**inputs):
    import numpy as _np
    import concourse.bacc as _bacc
    from concourse import mybir as _mybir
    from concourse.bass_utils import run_bass_kernel_spmd as _run

    nc = _bacc.Bacc("TRN2", target_bir_lowering=False, num_devices=1)
    arrays, args = {}, []
    for name in _INS:
        a = _np.ascontiguousarray(inputs[name])
        arrays[f"in_{name}_dram"] = a
        args.append(nc.dram_tensor(f"in_{name}_dram", a.shape, _mybir.dt.from_np(a.dtype), kind="ExternalInput").ap())
    args.append(nc.dram_tensor("out_dram", inputs["x"].shape, F32, kind="ExternalOutput").ap())
    build_gnn_ffn(nc, *args)
    return _run(nc, [arrays], core_ids=[0]).results[0]["out_dram"]
```

```python
from contextlib import ExitStack

import concourse.bass as bass
from concourse import mybir

ALU = mybir.AluOpType
ACT = mybir.ActivationFunctionType
F32 = mybir.dt.float32
F32R = mybir.dt.float32r
U8 = mybir.dt.uint8
U32 = mybir.dt.uint32
AX_X = mybir.AxisListType.X

P = 128
LN_EPS = 1e-5
TOP_K = 2
CAPACITY_FACTOR = 1.25



def exact(ap):
    return ap.bitcast(F32)


def build_gnn_ffn(nc, x, adj, nodemask, gnn_w, w_ih, w_hh, b_ih, b_hh, Wr, br, W1, b1, W2, b2, gamma, beta, out):
    B, N, D = x.shape
    LAYERS = gnn_w.shape[0]
    E, _, F = W1.shape
    KB = N // P
    HW = N // 2
    HK = KB // 2
    G = 3 * D
    PAIRS = B // 2
    SLOTS = 4
    S_PAIR = SLOTS * LAYERS
    LAST = LAYERS - 1
    CHUNKS = 2 * KB
    FB = F // P
    UNITS = 2 * TOP_K * FB
    CAPACITY = float(-(-B * N * 5 // (4 * E)))
    assert D == P and HW == 512 and CHUNKS == SLOTS * (LAYERS - 1) and FB == 2 and UNITS == 8 and PAIRS >= 2

    wc_dram = nc.dram_tensor("wc_dram", [LAYERS, P, 2 * G], F32, kind="Internal").ap()
    x1_dram = nc.dram_tensor("x1_dram", [B, N, D], F32, kind="Internal").ap()
    z_dram = nc.dram_tensor("z_dram", [B, N, D], F32, kind="Internal").ap()

    def batch(t, b):
        return t.rearrange("b (k p) d -> b p k d", p=P)[b]

    adj_rows = adj.rearrange("b i j -> (b i) j")

    with ExitStack() as whole:
        def alloc_in(stack, space):
            return lambda name, shape, dt=F32: stack.enter_context(space(name, shape, dt))

        def sem_in(stack):
            return lambda name: stack.enter_context(nc.semaphore(name))

        sb = alloc_in(whole, nc.sbuf_tensor)
        sem = sem_in(whole)
        ident = sb("ident", [P, P])
        zsum = sb("zsum", [P, B, D])
        neg_half = sb("neg_half", [P, KB])
        ident_zero, ident_ready, consts_ready = sem("ident_zero"), sem("ident_ready"), sem("consts_ready")
        waits_passed = sem("waits_passed")

        def detach(eng):
            eng.sem_inc(waits_passed, 1)

        def token_stats(dve, blocks, src, stat6, mv, step_sem, step, done_sem):
            if not (isinstance(step, int) and step == 1):
                dve.wait_ge(done_sem, step - 1)
            for k in range(blocks):
                ins = nc.vector.bn_stats(stat6[:, k, :], src[:, k, :])
            ins.then_inc(step_sem, 1)
            dve.wait_ge(step_sem, step)
            detach(dve)
            for k in range(blocks):
                ins = nc.vector.bn_aggr(mv[:, k, :], stat6[:, k, :])
            ins.then_inc(done_sem, 1)

        def inverse_deviation(pool, mv, rstd, stats_sem, stats_count, step_sem, step, done_sem):
            pool.wait_ge(stats_sem, stats_count)
            detach(pool)
            blocks = mv.shape[1]
            nc.gpsimd.tensor_scalar(rstd[:, 0:blocks], mv[:, :, 1], LN_EPS, None, ALU.add).then_inc(step_sem, 1)
            pool.wait_ge(step_sem, step)
            nc.gpsimd.tensor_tensor(rstd[:, 0:blocks], rstd[:, 0:blocks], neg_half[:, 0:blocks], ALU.pow).then_inc(done_sem, 1)

        def norm_apply(pool, blocks, src, dst, mv, rstd, stats_sem, stats_count, step_sem, step, done_sem):
            pool.wait_ge(stats_sem, stats_count)
            detach(pool)
            nc.gpsimd.tensor_scalar(rstd[:, 0:blocks], mv[:, :, 1], LN_EPS, None, ALU.add).then_inc(step_sem, 1)
            pool.wait_ge(step_sem, step)
            nc.gpsimd.tensor_tensor(rstd[:, 0:blocks], rstd[:, 0:blocks], neg_half[:, 0:blocks], ALU.pow).then_inc(step_sem, 1)
            pool.wait_ge(step_sem, step + 1)
            detach(pool)
            for k in range(blocks):
                ins = nc.gpsimd.tensor_scalar(dst[:, k, :], src[:, k, :], mv[:, k, 0:1], rstd[:, k:k + 1],
                                              ALU.subtract, ALU.mult)
            ins.then_inc(done_sem, 1)

        with ExitStack() as phase1:
            sb = alloc_in(phase1, nc.sbuf_tensor)
            sem = sem_in(phase1)
            a_mat = [sb(f"a_mat{n}", [P, KB, N], F32R) for n in range(2)]
            a_next = sb("a_next", [P, CHUNKS, N], U8)
            a_raw = sb("a_raw", [P, 2, N])
            w_cur = [sb(f"w_cur{n}", [P, 2 * G], F32R) for n in range(2)]
            w_hhT = sb("w_hhT", [P, 2 * G], F32R)
            hT = [sb(f"hT{n}", [P, N]) for n in range(2)]
            hT_hi = [sb(f"hT_hi{n}", [P, N], F32R) for n in range(2)]
            hT_lo = [sb(f"hT_lo{n}", [P, N], F32R) for n in range(2)]
            nat_hi = [sb(f"nat_hi{n}", [P, KB, D], F32R) for n in range(2)]
            nat_lo = [sb(f"nat_lo{n}", [P, KB, D], F32R) for n in range(2)]
            agg_hi = [sb(f"agg_hi{h}", [P, HW], F32R) for h in range(2)]
            agg_lo = [sb(f"agg_lo{h}", [P, HW], F32R) for h in range(2)]
            xbuf = [sb(f"xbuf{n}", [P, KB, D]) for n in range(2)]
            xn = [sb(f"xn{n}", [P, KB, D]) for n in range(2)]
            z_nat = sb("z_nat", [P, KB, D])
            z_fold = sb("z_fold", [P, HK, D])
            masked = sb("masked", [P, HK, D])
            cand = [sb(f"cand{h}", [P, HW]) for h in range(2)]
            gate_z = [sb(f"gate_z{h}", [P, HW]) for h in range(2)]
            diff = sb("diff", [P, HW])
            stat6 = sb("stat6", [P, KB, 6])
            mv1 = [sb(f"mv1_{n}", [P, KB, 2]) for n in range(2)]
            mv2 = [sb(f"mv2_{n}", [P, KB, 2]) for n in range(2)]
            rstd = sb("rstd", [P, KB])
            bias_ih, bias_hh, bias_rz = sb("bias_ih", [P, 3]), sb("bias_hh", [P, 3]), sb("bias_rz", [P, 2])
            mask_tok = sb("mask_tok", [P, B, KB])

            rstd_first = sb("rstd_first", [P, KB])
            a_first = [exact(a_next[:, 4 * r:4 * r + 4, :]).rearrange("p c n -> p (c n)") for r in range(4)] + [a_raw[:, r] for r in range(2)]
            first_loaded = [sem(f"first_loaded{r}") for r in range(6)]
            a_raw_loaded = [sem("a_raw_loaded0"), sem("a_raw_loaded1")]
            wc_stored = sem("wc_stored")
            w_cur_loaded = [sem(f"w_cur_loaded{n}") for n in range(2)]
            a_compared = sem("a_compared")
            stats_step, stats_done, norm_step = sem("stats_step"), sem("stats_done"), sem("norm_step")
            ln1_done = [sem(f"ln1_done{n}") for n in range(2)]
            xbuf_loaded = [sem(f"xbuf_loaded{n}") for n in range(2)]

            def compare_first(c):
                nc.vector.tensor_scalar(a_mat[c // KB][:, c % KB, :], a_first[c % 6], 0.0, None, ALU.not_equal).then_inc(a_compared, 1)

            with ExitStack() as stage0:
                sb0, ps0, sem = alloc_in(stage0, nc.sbuf_tensor), alloc_in(stage0, nc.psum_tensor), sem_in(stage0)
                w_ih_nat, w_hh_nat = sb0("w_ih_nat", [P, 3, D]), sb0("w_hh_nat", [P, 3, D])
                w_nat, w_T = sb0("w_nat", [P, LAYERS, D]), sb0("w_T", [P, LAYERS, D])
                w_ihT = sb0("w_ihT", [P, G])
                mask_nat = sb0("mask_nat", [B * KB, P])
                wc_split = [w_cur[0][:], hT_hi[1][:, 0:2 * G], hT_lo[1][:, 0:2 * G]] + [a_mat[1][:, KB - k, 0:2 * G] for k in (2, 1)]
                ps_ih, ps_hh, ps_wt = ps0("ps_ih", [P, G]), ps0("ps_hh", [P, G]), ps0("ps_wt", [P, 2, 512])
                ps_mask = ps0("ps_mask", [P, B * KB])
                ps_wc = [ps0(f"ps_wc{i}", [P, G]) for i in range(2)]
                w_loaded, mask_loaded, bias_loaded = (sem(n) for n in ("w_loaded", "mask_loaded", "bias_loaded"))
                x_loaded = [sem(f"x_loaded{n}") for n in range(2)]
                transposed, turned, hi_done, wc_done, wc_lo_done, bias_added = (
                    sem(n) for n in ("transposed", "turned", "hi_done", "wc_done", "wc_lo_done", "bias_added"))
                block = stage0.enter_context(nc.Block())

                @block.sync
                def _(sp):
                    sp.dma_start(w_ih_nat[:], w_ih.rearrange("(g p) d -> p g d", p=P)).then_inc(w_loaded, 16)
                    sp.dma_start(w_hh_nat[:], w_hh.rearrange("(g p) d -> p g d", p=P)).then_inc(w_loaded, 16)
                    sp.dma_start(w_nat[:], gnn_w.rearrange("l d e -> d l e")).then_inc(w_loaded, 16)
                    for lane in range(2):
                        sp.dma_start(xn[lane][:], batch(x, lane)).then_inc(x_loaded[lane], 16)
                    for c in range(CHUNKS - 2):
                        if c >= 6:
                            sp.wait_ge(a_compared, c - 5)
                        sp.dma_start(a_first[c % 6], adj_rows[c * P:(c + 1) * P, :]).then_inc(first_loaded[c % 6], 16)

                @block.scalar
                def _(act):
                    act.dma_start(mask_nat[:], nodemask.rearrange("b (k p) -> (b k) p", p=P)).then_inc(mask_loaded, 16)
                    with nc.allow_non_contiguous_dma(reason="384 bias values, one per partition"):
                        act.dma_start(bias_ih[:], b_ih.rearrange("(g p) -> p g", p=P)).then_inc(bias_loaded, 16)
                        act.dma_start(bias_hh[:], b_hh.rearrange("(g p) -> p g", p=P)).then_inc(bias_loaded, 16)
                    act.wait_ge(transposed, 2)
                    nc.scalar.activation(w_hhT[:, 0:G], ps_hh[:], ACT.Copy).then_inc(hi_done, 1)
                    for n in range(LAYERS):
                        act.wait_ge(wc_done, n + 1)
                        nc.scalar.activation(wc_split[n][:, 0:G], ps_wc[n % 2][:], ACT.Copy).then_inc(hi_done, 1)
                        act.wait_ge(wc_lo_done, n + 1)
                        if n == 0:
                            nc.scalar.activation(w_cur[1][:], w_cur[0][:], ACT.Copy).then_inc(w_cur_loaded[1], 16)
                            act.sem_inc(w_cur_loaded[0], 16)
                        act.dma_start(wc_dram[n], exact(wc_split[n])).then_inc(wc_stored, 16)

                @block.gpsimd
                def _(pool):
                    nc.gpsimd.memset(ident[:], 0.0).then_inc(ident_zero, 1)
                    nc.gpsimd.memset(neg_half[:], -0.5).then_inc(consts_ready, 1)
                    pool.wait_ge(ident_zero, 1)
                    nc.gpsimd.affine_select(out=ident[:], in_=ident[:], compare_op=ALU.not_equal, fill=1.0, base=0,
                                            pattern=[[-1, P]], channel_multiplier=1).then_inc(ident_ready, 1)
                    pool.wait_ge(consts_ready, 1)
                    inverse_deviation(pool, mv1[0], rstd_first, stats_done, 1, norm_step, 1, norm_step)
                    norm_apply(pool, KB, xn[1], xn[1], mv1[1], rstd, stats_done, 2, norm_step, 3, ln1_done[1])
                    pool.wait_ge(ln1_done[1], 1)

                @block.tensor
                def _(pe):
                    pe.wait_ge(ident_ready, 1)
                    pe.wait_ge(w_loaded, 48)
                    for g in range(3):
                        tr = nc.tensor.transpose(ps_ih[:, g * D:(g + 1) * D], w_ih_nat[:, g, :], ident[:])
                    tr.then_inc(transposed, 1)
                    for g in range(3):
                        tr = nc.tensor.transpose(ps_hh[:, g * D:(g + 1) * D], w_hh_nat[:, g, :], ident[:])
                    tr.then_inc(transposed, 1)
                    for n in range(LAYERS):
                        tr = nc.tensor.transpose(ps_wt[:, n // 4, n % 4 * D:(n % 4 + 1) * D], w_nat[:, n, :], ident[:])
                    tr.then_inc(transposed, 1)
                    pe.wait_ge(mask_loaded, 16)
                    nc.tensor.transpose(ps_mask[:], mask_nat[:], ident[0:B * KB, 0:B * KB]).then_inc(transposed, 1)
                    pe.wait_ge(turned, 3)
                    for n in range(LAYERS):
                        if n >= 2:
                            pe.wait_ge(wc_lo_done, n - 1)
                        nc.tensor.matmul(ps_wc[n % 2][:], w_T[:, n, :], w_ihT[:], start=True, stop=True).then_inc(wc_done, 1)

                @block.vector
                def _(dve):
                    def compare(c):
                        dve.wait_ge(first_loaded[c % 6], 16 * (c // 6 + 1))
                        compare_first(c)

                    dve.wait_ge(transposed, 1)
                    nc.vector.tensor_copy(w_ihT[:], ps_ih[:]).then_inc(turned, 1)
                    dve.wait_ge(transposed, 3)
                    nc.vector.tensor_copy(w_T[:, 0:4, :], ps_wt[:, 0, :].rearrange("p (l d) -> p l d", d=D)).then_inc(turned, 1)
                    nc.vector.tensor_copy(w_T[:, 4, :], ps_wt[:, 1, 0:D]).then_inc(turned, 1)
                    for lane in range(2):
                        dve.wait_ge(x_loaded[lane], 16)
                        token_stats(dve, KB, xn[lane], stat6, mv1[lane], stats_step, lane + 1, stats_done)
                    compare(0)
                    for n in range(LAYERS):
                        dve.wait_ge(hi_done, 2 + n)
                        nc.vector.tensor_tensor(wc_split[n][:, G:2 * G], ps_wc[n % 2][:], exact(wc_split[n][:, 0:G]),
                                                ALU.subtract).then_inc(wc_lo_done, 1)
                        if n == 0:
                            dve.wait_ge(norm_step, 2)
                        for k in range(2 * n, min(2 * n + 2, KB)):
                            ins = nc.vector.tensor_scalar(xn[0][:, k, :], xn[0][:, k, :], mv1[0][:, k, 0:1], rstd_first[:, k:k + 1],
                                                          ALU.subtract, ALU.mult)
                        if n == 3:
                            ins.then_inc(ln1_done[0], 1)
                        compare(n + 1)
                    for c in range(LAYERS + 1, KB):
                        compare(c)
                    dve.wait_ge(hi_done, 1)
                    nc.vector.tensor_tensor(w_hhT[:, G:2 * G], ps_hh[:], exact(w_hhT[:, 0:G]), ALU.subtract).then_inc(turned, 1)
                    dve.wait_ge(transposed, 4)
                    nc.vector.tensor_copy(mask_tok[:].rearrange("p b k -> p (b k)"), ps_mask[:]).then_inc(turned, 1)
                    dve.wait_ge(bias_loaded, 32)
                    nc.vector.tensor_tensor(bias_rz[:], bias_ih[:, 0:2], bias_hh[:, 0:2], ALU.add).then_inc(bias_added, 1)

            with ExitStack() as stage1:
                ps1, sem = alloc_in(stage1, nc.psum_tensor), sem_in(stage1)
                ps_agg = [ps1(f"ps_agg{h}", [P, HW]) for h in range(2)]
                ps_t = [ps1(f"ps_t{h}", [P, HW]) for h in range(2)]
                ps_r, ps_z, ps_hn, ps_in = (ps1(n, [P, HW]) for n in ("ps_r", "ps_z", "ps_hn", "ps_in"))

                xn_loaded = [sem(f"xn_loaded{n}") for n in range(2)]
                a_act, a_dve = [sem(f"a_act{n}") for n in range(2)], [sem(f"a_dve{n}") for n in range(2)]
                trans_done, xt_done = sem("trans_done"), sem("xt_done")
                nat_hi_done, nat_ready = sem("nat_hi_done"), sem("nat_ready")
                agg_done, agg_hi_done, agg_split = sem("agg_done"), sem("agg_hi_done"), sem("agg_split")
                r_mm, hn_mm, in_mm, z_mm = sem("r_mm"), sem("hn_mm"), sem("in_mm"), sem("z_mm")
                r_act, n_act, z_act = sem("r_act"), sem("n_act"), sem("z_act")
                cand_done, pre_done, diff_done, zd_done = sem("cand_done"), sem("pre_done"), sem("diff_done"), sem("zd_done")
                h_done = sem("h_done")
                hT_hi_done = [sem(f"hT_hi_done{n}") for n in range(2)]
                hT_ready = [sem(f"hT_ready{n}") for n in range(2)]
                final_read, x1_done, ln2_done, fold_step = sem("final_read"), sem("x1_done"), sem("ln2_done"), sem("fold_step")
                x1z_stored = sem("x1z_stored")
                block = stage1.enter_context(nc.Block())

                def half(h):
                    return slice(h * HW, (h + 1) * HW)

                def hblocks(h):
                    return slice(h * HK, (h + 1) * HK)

                def flat(ap):
                    return ap.rearrange("p k d -> p (k d)")

                def before(q):
                    return (q - 1) % SLOTS // 2, (q - 1) % 2

                @block.sync
                def _(sp):
                    def chunk(p, l, q):
                        c = CHUNKS * (p + 1) + SLOTS * l + q - 2
                        sp.wait_ge(a_compared, c - 1)
                        sp.dma_start(a_raw[:, q % 2], adj_rows[bass.ds(c * P, P), :]).then_inc(a_raw_loaded[q % 2], 16)

                    def weights(lane, layer, slots_done):
                        sp.wait_ge(z_mm, slots_done)
                        sp.dma_start(exact(w_cur[lane][:]), wc_dram[layer]).then_inc(w_cur_loaded[lane], 16)

                    def pair(p, last):
                        if not last:
                            chunk(p, 0, 2)
                            chunk(p, 0, 3)
                        if not last:
                            for lane in range(2):
                                sp.wait_ge(hT_ready[lane], 2 * LAYERS * p + 2)
                                detach(sp)
                                sp.wait_ge(nat_ready, S_PAIR * p + 2 + 2 * lane)
                                sp.dma_start(xn[lane][:], batch(x, 2 * p + 2 + lane)).then_inc(xn_loaded[lane], 16)
                        weights(0, 1, S_PAIR * p + 2)
                        with sp.Fori(1, LAST) as l:
                            if not last:
                                chunk(p, l, 0)
                                chunk(p, l, 1)
                            weights(1, l, S_PAIR * p + SLOTS * l)
                            if not last:
                                chunk(p, l, 2)
                                chunk(p, l, 3)
                            weights(0, l + 1, S_PAIR * p + SLOTS * l + 2)
                        if not last:
                            chunk(p, LAST, 0)
                            chunk(p, LAST, 1)
                        weights(1, LAST, S_PAIR * p + SLOTS * LAST)
                        if not last:
                            weights(0, 0, S_PAIR * p + SLOTS * LAST + 2)
                            weights(1, 0, S_PAIR * (p + 1))

                    for c in range(CHUNKS - 2, CHUNKS):
                        sp.wait_ge(a_compared, c - 5)
                        sp.dma_start(a_first[c % 6], adj_rows[c * P:(c + 1) * P, :]).then_inc(first_loaded[c % 6], 16)
                    sp.wait_ge(wc_stored, 16 * LAYERS)
                    with sp.Fori(0, PAIRS - 1) as p:
                        pair(p, False)
                    pair(PAIRS - 1, True)

                @block.gpsimd
                def _(pool):
                    def norm_out(p, lane, number, last):
                        b = 2 * p + lane
                        pool.wait_ge(x1_done, 2 * b + 2)
                        detach(pool)
                        pool.dma_start(batch(x1_dram, b), xbuf[lane][:]).then_inc(x1z_stored, 16)
                        norm_apply(pool, KB, xbuf[lane], z_nat, mv2[lane], rstd, stats_done, number + 1,
                                   norm_step, 2 * number + 1, ln2_done)
                        pool.wait_ge(ln2_done, b + 1)
                        detach(pool)
                        pool.dma_start(batch(z_dram, b), z_nat[:]).then_inc(x1z_stored, 16)
                        nc.gpsimd.tensor_tensor(z_fold[:], z_nat[:, 0:HK, :], z_nat[:, HK:KB, :], ALU.add).then_inc(fold_step, 1)
                        pool.wait_ge(fold_step, 3 * b + 1)
                        nc.gpsimd.tensor_tensor(z_fold[:, 0:2, :], z_fold[:, 0:2, :], z_fold[:, 2:4, :], ALU.add).then_inc(fold_step, 1)
                        pool.wait_ge(fold_step, 3 * b + 2)
                        nc.gpsimd.tensor_tensor(zsum[:, b, :], z_fold[:, 0, :], z_fold[:, 1, :], ALU.add).then_inc(fold_step, 1)
                        pool.wait_ge(x1z_stored, 32 * b + 32)
                        pool.wait_ge(fold_step, 3 * b + 3)
                        if not last:
                            pool.dma_start(xbuf[lane][:], batch(x, b + 2)).then_inc(xbuf_loaded[lane], 16)

                    pool.wait_ge(first_loaded[(CHUNKS - 1) % 6], 16 * ((CHUNKS - 1) // 6 + 1))
                    for lane in range(2):
                        pool.dma_start(xbuf[lane][:], batch(x, lane)).then_inc(xbuf_loaded[lane], 16)
                    with pool.Fori(0, PAIRS - 1) as p:
                        for lane in range(2):
                            number = 4 * p + 2 + lane
                            norm_apply(pool, KB, xn[lane], xn[lane], mv1[lane], rstd, stats_done, number + 1,
                                       norm_step, 2 * number + 1, ln1_done[lane])
                            pool.wait_ge(ln1_done[lane], p + 2)
                        for lane in range(2):
                            norm_out(p, lane, 4 * p + 4 + lane, False)
                    for lane in range(2):
                        norm_out(PAIRS - 1, lane, 4 * PAIRS - 2 + lane, True)

                @block.tensor
                def _(pe):
                    def x_to_features(lane, h):
                        for k in range(HK):
                            tr = nc.tensor.transpose(ps_t[h][:, k * P:(k + 1) * P], xn[lane][:, h * HK + k, :], ident[:])
                        tr.then_inc(xt_done, 1)

                    def state_to_tokens(s, q):
                        lane, h = before(q)
                        pe.wait_ge(h_done, s)
                        for k in range(HK):
                            tr = nc.tensor.transpose(ps_t[h][:, k * P:(k + 1) * P],
                                                     hT[lane][:, h * HW + k * P:h * HW + (k + 1) * P], ident[:])
                        tr.then_inc(trans_done, 1)

                    def aggregate(lane, h, nat_count):
                        for k in range(KB):
                            if k == 0 and nat_count is not None:
                                pe.wait_ge(nat_ready, nat_count)
                            if k == HK and nat_count is not None:
                                pe.wait_ge(nat_ready, nat_count + 1)
                            for part in (nat_hi, nat_lo):
                                mm = nc.tensor.matmul(ps_agg[h][:], part[lane][:, k, :], a_mat[lane][:, k, half(h)],
                                                      start=(k == 0 and part is nat_hi), stop=(k == KB - 1 and part is nat_lo))
                        mm.then_inc(agg_done, 1)

                    def gates(s, t, q, first, between):
                        lane, h = q // 2, q % 2
                        w_in, w_rec = w_cur[lane], w_hhT
                        inp = (agg_hi[h][:], agg_lo[h][:])
                        rec = (hT_hi[lane][:, half(h)], hT_lo[lane][:, half(h)])

                        def products(ps, gate, sides):
                            terms = []
                            for w, (hi, lo) in sides:
                                w_hi, w_lo = (w[:, o + gate * D:o + (gate + 1) * D] for o in (0, G))
                                terms += [(w_hi, hi), (w_hi, lo), (w_lo, hi)]
                            for n, (a, b) in enumerate(terms):
                                mm = nc.tensor.matmul(ps[:], a, b, start=(n == 0), stop=(n == len(terms) - 1))
                            return mm

                        pe.wait_ge(hT_ready[lane], 2 * t + h + 1)
                        if not first:
                            pe.wait_ge(cand_done, s)
                        products(ps_hn, 2, [(w_rec, rec)]).then_inc(hn_mm, 1)
                        pe.wait_ge(agg_split, s + 1)
                        pe.wait_ge(w_cur_loaded[lane], 16 * t + 16)
                        if not first:
                            pe.wait_ge(r_act, s)
                        products(ps_r, 0, [(w_rec, rec), (w_in, inp)]).then_inc(r_mm, 1)
                        between()
                        if not first:
                            pe.wait_ge(pre_done, s)
                        products(ps_in, 2, [(w_in, inp)]).then_inc(in_mm, 1)
                        if not first:
                            pe.wait_ge(z_act, s)
                        products(ps_z, 1, [(w_rec, rec), (w_in, inp)]).then_inc(z_mm, 1)

                    def slot(p, l, q, edge="", last=False):
                        t = LAYERS * p + l
                        s = SLOTS * t + q
                        h = q % 2
                        very_first = edge == "head" and isinstance(p, int) and p == 0 and q == 0

                        def turn_result():
                            if very_first:
                                return
                            if not (isinstance(p, int) and p == 0 and edge == "head") and not (edge == "tail" and q == 3 and last):
                                pe.wait_ge(nat_ready, s + 2)
                            if edge == "head":
                                if q == 0:
                                    pe.wait_ge(hT_ready[0], 2 * t + 2)
                                else:
                                    pe.wait_ge(hT_ready[1], 2 * t + q)
                            if edge == "tail" and q == 3:
                                if last:
                                    pe.wait_ge(final_read, 4 * p + 1)
                                else:
                                    pe.wait_ge(hT_ready[0], 2 * t + 3)
                            state_to_tokens(s, q)

                        gates(s, t, q, very_first, turn_result)
                        if edge == "head" and q < 2:
                            if not (isinstance(p, int) and p == 0):
                                pe.wait_ge(final_read, 4 * p - 1 + q)
                            pe.wait_ge(ln1_done[1], p + 1)
                            x_to_features(1, h)
                            if q == 0:
                                if isinstance(p, int) and p == 0:
                                    pe.wait_ge(a_compared, CHUNKS)
                                else:
                                    pe.wait_ge(a_act[1], 2 * p)
                                    pe.wait_ge(a_dve[1], 2 * p)
                        if edge == "tail" and q >= 2 and not last:
                            pe.wait_ge(final_read, 4 * p - 1 + q)
                            pe.wait_ge(ln1_done[0], p + 2)
                            x_to_features(0, h)
                            if q == 2:
                                pe.wait_ge(a_act[0], 2 * p + 2)
                                pe.wait_ge(a_dve[0], 2 * p + 2)
                        if not (edge == "tail" and q >= 2 and last):
                            aggregate(1 - q // 2, h, s + 3 if h == 0 else None)

                    def pair(p, last):
                        slot(p, 0, 2, "head")
                        slot(p, 0, 3, "")
                        with pe.Fori(1, LAST) as l:
                            for q in range(SLOTS):
                                slot(p, l, q)
                        for q in range(SLOTS):
                            slot(p, LAST, q, "tail", last)

                    pe.wait_ge(ln1_done[0], 1)
                    for h in range(2):
                        x_to_features(0, h)
                    pe.wait_ge(a_compared, KB)
                    aggregate(0, 0, 1)
                    aggregate(0, 1, None)
                    slot(0, 0, 0, "head")
                    slot(0, 0, 1, "head")
                    with pe.Fori(0, PAIRS - 1) as p:
                        pair(p, False)
                        slot(p + 1, 0, 0, "head")
                        slot(p + 1, 0, 1, "head")
                    pair(PAIRS - 1, True)
                    pe.wait_ge(final_read, 4 * PAIRS - 2)
                    state_to_tokens(S_PAIR * PAIRS, 0)

                @block.scalar
                def _(act):
                    def new_x_tokens(lane, h):
                        nc.scalar.activation(nat_hi[lane][:, hblocks(h), :], xn[lane][:, hblocks(h), :],
                                             ACT.Copy).then_inc(nat_hi_done, 1)

                    def new_x_features(lane, h, number):
                        act.wait_ge(xt_done, number + 1)
                        nc.scalar.activation(hT[lane][:, half(h)], ps_t[h][:], ACT.Copy).then_inc(hT_hi_done[lane], 1)
                        nc.scalar.activation(hT_hi[lane][:, half(h)], ps_t[h][:], ACT.Copy).then_inc(hT_hi_done[lane], 1)

                    def slot(p, l, q, edge="", last=False):
                        t = LAYERS * p + l
                        s = SLOTS * t + q
                        lane, h = q // 2, q % 2
                        before_lane, before_h = before(q)
                        at_start = isinstance(p, int) and p == 0 and edge == "head"
                        if not (edge == "tail" and q == 3 and last):
                            act.wait_ge(agg_done, s + 2)
                            nc.scalar.activation(agg_hi[1 - h][:], ps_agg[1 - h][:], ACT.Copy).then_inc(agg_hi_done, 1)
                        act.wait_ge(r_mm, s + 1)
                        nc.scalar.activation(cand[h][:], ps_r[:], ACT.Sigmoid, bias=bias_rz[:, 0:1]).then_inc(r_act, 1)
                        if not (at_start and q == 0):
                            new_batch = (edge == "tail" and q >= 1) or (edge == "head" and q == 0)
                            if not (new_batch and last):
                                act.wait_ge(trans_done, s)
                                if new_batch:
                                    if q == 0:
                                        act.wait_ge(ln1_done[1], p + 1)
                                    else:
                                        act.wait_ge(ln1_done[before_lane], p + 2)
                                    new_x_tokens(before_lane, before_h)
                                else:
                                    nc.scalar.activation(flat(nat_hi[before_lane][:, hblocks(before_h), :]), ps_t[before_h][:],
                                                         ACT.Copy).then_inc(nat_hi_done, 1)
                        act.wait_ge(pre_done, s + 1)
                        nc.scalar.activation(cand[h][:], cand[h][:], ACT.Tanh, bias=bias_ih[:, 2:3]).then_inc(n_act, 1)
                        act.wait_ge(z_mm, s + 1)
                        nc.scalar.activation(gate_z[h][:], ps_z[:], ACT.Sigmoid, bias=bias_rz[:, 1:2]).then_inc(z_act, 1)
                        if edge == "head" and q < 2:
                            new_x_features(1, h, 4 * p + 2 + h)
                        if edge == "tail" and q >= 2 and not last:
                            new_x_features(0, h, 4 * p + 4 + h)
                        if edge == "tail" and not last:
                            act.wait_ge(a_compared, CHUNKS * (p + 1) + (lane + 1) * KB)
                            act.wait_ge(agg_done, 4 * t + 2 * lane + 2)
                            nc.scalar.activation(a_mat[lane][:, 4 * h:4 * h + 2, :], a_next[:, KB * lane + 4 * h:KB * lane + 4 * h + 2, :],
                                                 ACT.Copy).then_inc(a_act[lane], 1)
                        if edge != "tail":
                            act.wait_ge(h_done, s + 1)
                            nc.scalar.activation(hT_hi[lane][:, half(h)], hT[lane][:, half(h)], ACT.Copy).then_inc(hT_hi_done[lane], 2)

                    def pair(p, last):
                        slot(p, 0, 2)
                        slot(p, 0, 3)
                        with act.Fori(1, LAST) as l:
                            for q in range(SLOTS):
                                slot(p, l, q)
                        for q in range(SLOTS):
                            slot(p, LAST, q, "tail", last)

                    act.wait_ge(ln1_done[0], 1)
                    new_x_tokens(0, 0)
                    new_x_tokens(0, 1)
                    new_x_features(0, 0, 0)
                    new_x_features(0, 1, 1)
                    act.wait_ge(ln1_done[1], 1)
                    new_x_tokens(1, 0)
                    new_x_tokens(1, 1)
                    act.wait_ge(agg_done, 1)
                    nc.scalar.activation(agg_hi[0][:], ps_agg[0][:], ACT.Copy).then_inc(agg_hi_done, 1)
                    slot(0, 0, 0, "head")
                    slot(0, 0, 1, "head")
                    with act.Fori(0, PAIRS - 1) as p:
                        pair(p, False)
                        slot(p + 1, 0, 0, "head")
                        slot(p + 1, 0, 1, "head")
                    pair(PAIRS - 1, True)

                @block.vector
                def _(dve):
                    def new_x_tokens(lane, h):
                        nc.vector.tensor_tensor(nat_lo[lane][:, hblocks(h), :], xn[lane][:, hblocks(h), :],
                                                exact(nat_hi[lane][:, hblocks(h), :]), ALU.subtract).then_inc(nat_ready, 1)

                    def new_x_features(lane, h, n):
                        dve.wait_ge(hT_hi_done[lane], 2 * n + 2)
                        nc.vector.tensor_tensor(hT_lo[lane][:, half(h)], ps_t[h][:], exact(hT_hi[lane][:, half(h)]),
                                                ALU.subtract).then_inc(hT_ready[lane], 1)

                    def final_state(p, lane, h):
                        n = 4 * p + 2 * lane + h
                        mask = mask_tok[:, 2 * p + lane, hblocks(h)].unsqueeze(2).to_broadcast([P, HK, D])
                        if h == 0:
                            dve.wait_ge(xbuf_loaded[lane], 16 * p + 16)
                        if (lane, h) != (0, 0):
                            dve.wait_ge(x1_done, n)
                        nc.vector.tensor_tensor(masked[:], ps_t[h][:].rearrange("p (k d) -> p k d", d=D), mask,
                                                ALU.mult).then_inc(final_read, 1)
                        dve.wait_ge(final_read, n + 1)
                        nc.vector.tensor_tensor(xbuf[lane][:, hblocks(h), :], xbuf[lane][:, hblocks(h), :], masked[:],
                                                ALU.add).then_inc(x1_done, 1)

                    def slot(p, l, q, edge="", last=False):
                        t = LAYERS * p + l
                        s = SLOTS * t + q
                        lane, h = q // 2, q % 2
                        before_lane, before_h = before(q)
                        at_start = isinstance(p, int) and p == 0 and edge == "head"
                        if not (edge == "tail" and q == 3 and last):
                            dve.wait_ge(agg_hi_done, s + 2)
                            nc.vector.tensor_tensor(agg_lo[1 - h][:], ps_agg[1 - h][:], exact(agg_hi[1 - h][:]),
                                                    ALU.subtract).then_inc(agg_split, 1)
                        dve.wait_ge(r_act, s + 1)
                        dve.wait_ge(hn_mm, s + 1)
                        nc.vector.scalar_tensor_tensor(cand[h][:], ps_hn[:], bias_hh[:, 2:3], cand[h][:], ALU.add, ALU.mult).then_inc(cand_done, 1)
                        dve.wait_ge(in_mm, s + 1)
                        dve.wait_ge(cand_done, s + 1)
                        nc.vector.tensor_tensor(cand[h][:], ps_in[:], cand[h][:], ALU.add).then_inc(pre_done, 1)
                        if not (at_start and q == 0):
                            new_batch = (edge == "tail" and q >= 1) or (edge == "head" and q == 0)
                            if not (new_batch and last):
                                dve.wait_ge(nat_hi_done, s + 4)
                                if new_batch:
                                    new_x_tokens(before_lane, before_h)
                                else:
                                    nc.vector.tensor_tensor(flat(nat_lo[before_lane][:, hblocks(before_h), :]), ps_t[before_h][:],
                                                            exact(flat(nat_hi[before_lane][:, hblocks(before_h), :])),
                                                            ALU.subtract).then_inc(nat_ready, 1)
                            if new_batch:
                                dve.wait_ge(trans_done, s)
                                final_state(p - 1 if q == 0 else p, before_lane, before_h)
                        if not last and (edge == "" or (edge == "tail" and q < 2)):
                            c = CHUNKS * (p + 1) + SLOTS * l + q - 2
                            dve.wait_ge(a_raw_loaded[q % 2], 16 * (KB * p + 2 * l + q // 2))
                            nc.vector.tensor_scalar(a_next[:, SLOTS * l + q - 2, :], a_raw[:, q % 2], 0.0, None,
                                                    ALU.not_equal).then_inc(a_compared, 1)
                        if edge == "tail" and not last:
                            dve.wait_ge(agg_done, 4 * t + 2 * lane + 2)
                            nc.vector.tensor_copy(a_mat[lane][:, 4 * h + 2:4 * h + 4, :],
                                                  a_next[:, KB * lane + 4 * h + 2:KB * lane + 4 * h + 4, :]).then_inc(a_dve[lane], 1)
                        if edge == "" and isinstance(l, int) and not last:
                            dve.wait_ge(xn_loaded[h], 16 * p + 16)
                            token_stats(dve, KB, xn[h], stat6, mv1[h], stats_step, 4 * p + 3 + h, stats_done)
                        if edge == "tail" and q == 3:
                            number = 4 * p + (2 if last else 4)
                            dve.wait_ge(x1_done, 4 * p + 2)
                            token_stats(dve, KB, xbuf[0], stat6, mv2[0], stats_step, number + 1, stats_done)
                        if edge == "head" and q == 1 and not at_start:
                            for n in range(2):
                                dve.wait_ge(a_act[n], 2 * p)
                            dve.wait_ge(x1_done, 4 * p)
                            token_stats(dve, KB, xbuf[1], stat6, mv2[1], stats_step, 4 * p + 2, stats_done)
                        dve.wait_ge(n_act, s + 1)
                        nc.vector.tensor_tensor(diff[:], hT[lane][:, half(h)], cand[h][:], ALU.subtract).then_inc(diff_done, 1)
                        dve.wait_ge(z_act, s + 1)
                        dve.wait_ge(diff_done, s + 1)
                        nc.vector.tensor_tensor(gate_z[h][:], gate_z[h][:], diff[:], ALU.mult).then_inc(zd_done, 1)
                        dve.wait_ge(zd_done, s + 1)
                        nc.vector.tensor_tensor(hT[lane][:, half(h)], cand[h][:], gate_z[h][:], ALU.add).then_inc(h_done, 1)
                        if edge == "head" and q < 2:
                            new_x_features(1, h, 2 * t + h)
                        if edge == "tail" and q >= 2 and not last:
                            new_x_features(0, h, 2 * t + 2 + h)
                        if edge != "tail":
                            n = 2 * t + 2 + h
                            dve.wait_ge(hT_hi_done[lane], 2 * n + 2)
                            nc.vector.tensor_tensor(hT_lo[lane][:, half(h)], hT[lane][:, half(h)], exact(hT_hi[lane][:, half(h)]),
                                                    ALU.subtract).then_inc(hT_ready[lane], 1)

                    def pair(p, last):
                        slot(p, 0, 2, "", last)
                        slot(p, 0, 3, "", last)
                        with dve.Fori(1, LAST) as l:
                            for q in range(SLOTS):
                                slot(p, l, q, "", last)
                        for q in range(SLOTS):
                            slot(p, LAST, q, "tail", last)

                    for h in range(2):
                        dve.wait_ge(nat_hi_done, h + 1)
                        new_x_tokens(0, h)
                    new_x_features(0, 0, 0)
                    new_x_features(0, 1, 1)
                    for c in range(KB, CHUNKS):
                        if c == CHUNKS - 2:
                            dve.wait_ge(wc_stored, 16 * LAYERS)
                        dve.wait_ge(first_loaded[c % 6], 16 * (c // 6 + 1))
                        compare_first(c)
                        if c == KB + 3:
                            dve.wait_ge(agg_hi_done, 1)
                            nc.vector.tensor_tensor(agg_lo[0][:], ps_agg[0][:], exact(agg_hi[0][:]), ALU.subtract).then_inc(agg_split, 1)
                    for h in range(2):
                        dve.wait_ge(nat_hi_done, h + 3)
                        new_x_tokens(1, h)
                    slot(0, 0, 0, "head")
                    slot(0, 0, 1, "head")
                    with dve.Fori(0, PAIRS - 1) as p:
                        pair(p, False)
                        slot(p + 1, 0, 0, "head")
                        slot(p + 1, 0, 1, "head")
                    pair(PAIRS - 1, True)
                    dve.wait_ge(trans_done, S_PAIR * PAIRS)
                    final_state(PAIRS - 1, 1, 1)
                    dve.wait_ge(x1_done, 4 * PAIRS)
                    token_stats(dve, KB, xbuf[1], stat6, mv2[1], stats_step, 4 * PAIRS, stats_done)

        with ExitStack() as phase2:
            sb, ps, sem = alloc_in(phase2, nc.sbuf_tensor), alloc_in(phase2, nc.psum_tensor), sem_in(phase2)
            C = B * TOP_K
            w_raw = [sb(f"w_raw{i}", [P, TOP_K, 2 * F]) for i in range(2)]
            w_hi = [sb(f"w_hi{i}", [P, TOP_K, 2 * F], F32R) for i in range(2)]
            w_lo = [sb(f"w_lo{i}", [P, TOP_K, 2 * F], F32R) for i in range(2)]
            z_in = [sb(f"z_in{i}", [P, KB, D]) for i in range(2)]
            z_res = [sb(f"z_res{i}", [P, KB, D]) for i in range(2)]
            x_res = [sb(f"x_res{i}", [P, KB, D]) for i in range(2)]
            zT_hi, zT_lo = sb("zT_hi", [P, N], F32R), sb("zT_lo", [P, N], F32R)
            act_out = [sb(f"act_out{i}", [P, HW]) for i in range(4)]
            g_hi = [sb(f"g_hi{i}", [P, HW], F32R) for i in range(4)]
            g_lo = [sb(f"g_lo{i}", [P, HW], F32R) for i in range(4)]
            yT = [sb(f"yT{h}", [P, HW]) for h in range(2)]
            res = [sb(f"res{h}", [P, HK, D]) for h in range(2)]
            stat6b = sb("stat6b", [P, HK, 6])
            mvb = [sb(f"mvb{h}", [P, HK, 2]) for h in range(2)]
            rstdb = [sb(f"rstdb{h}", [P, HK]) for h in range(2)]
            b1_sel = sb("b1_sel", [P, FB, C])
            b2_mix = sb("b2_mix", [P, B])
            top_w_all = sb("top_w_all", [P, C])
            gamma_all, beta_all = sb("gamma_all", [P, D]), sb("beta_all", [P, D])
            expert_row = sb("expert_row", [1, C], U32)
            z_in_loaded = [sem(f"z_in_loaded{i}") for i in range(2)]
            z_res_loaded = [sem(f"z_res_loaded{i}") for i in range(2)]
            x_res_loaded = [sem(f"x_res_loaded{i}") for i in range(2)]
            row_loaded = sem("row_loaded")

            with ExitStack() as routing:
                sbr, psr, semr = alloc_in(routing, nc.sbuf_tensor), alloc_in(routing, nc.psum_tensor), sem_in(routing)
                Wr_sb, br_row = sbr("Wr_sb", [P, E]), sbr("br_row", [1, E])
                b1_sb, b2_sb = sbr("b1_sb", [E, F]), sbr("b2_sb", [E, D])
                gb_row = sbr("gb_row", [1, 2, D])
                ones = sbr("ones", [E, P])
                mean_w = sbr("mean_w", [P, 1])
                meanT = sbr("meanT", [P, B])
                iota_e = sbr("iota_e", [B, E])
                logits, rw, rw2, e2 = (sbr(n, [B, E]) for n in ("logits", "rw", "rw2", "e2"))
                peak, total, inv_total = sbr("peak", [B, 4]), sbr("total", [B, 4]), sbr("inv_total", [B, 4])
                load, over, quot = (sbr(n, [B, E]) for n in ("load", "over", "quot"))
                top, top_i, top_f = sbr("top", [B, 8]), sbr("top_i", [B, 8], U32), sbr("top_f", [B, 8])
                onehot, w_dense = sbr("onehot", [B, TOP_K, E]), sbr("w_dense", [B, E])
                top_e, top_w = sbr("top_e", [B, TOP_K]), sbr("top_w", [B, TOP_K])
                w_diag = sbr("w_diag", [B, TOP_K, B])
                oh_T, wd_T = sbr("oh_T", [E, C]), sbr("wd_T", [E, B])
                ps_mean, ps_small = psr("ps_mean", [P, B]), psr("ps_small", [P, 512])
                ps_load, ps_t8 = psr("ps_load", [P, 512]), psr("ps_t8", [P, 512])
                ps_sel, ps_bc = psr("ps_sel", [P, 512]), psr("ps_bc", [P, 512])
                params_loaded = semr("params_loaded")
                pe_step, act_step, dve_step, pool_step = (semr(n) for n in ("pe_step", "act_step", "dve_step", "pool_step"))
                block = routing.enter_context(nc.Block())

                @block.sync
                def _(sp):
                    for dst, src in ((Wr_sb[:], Wr), (br_row[:], br.rearrange("(o e) -> o e", o=1)), (b1_sb[:], b1), (b2_sb[:], b2),
                                     (gb_row[:, 0, :], gamma.rearrange("(o d) -> o d", o=1)),
                                     (gb_row[:, 1, :], beta.rearrange("(o d) -> o d", o=1))):
                        sp.dma_start(dst, src).then_inc(params_loaded, 16)
                    for i in range(2):
                        sp.dma_start(z_in[i][:], batch(z_dram, i)).then_inc(z_in_loaded[i], 16)
                    for i in range(2):
                        sp.dma_start(z_res[i][:], batch(z_dram, i)).then_inc(z_res_loaded[i], 16)
                        sp.dma_start(x_res[i][:], batch(x1_dram, i)).then_inc(x_res_loaded[i], 16)
                    sp.wait_ge(dve_step, 17)
                    for k in range(TOP_K):
                        sp.dma_start(expert_row[:, k * B:(k + 1) * B].rearrange("o (b c) -> o b c", c=1),
                                     top_i[:, k:k + 1]).then_inc(row_loaded, 16)
                    sp.wait_ge(row_loaded, 16 * TOP_K)

                @block.gpsimd
                def _(pool):
                    nc.gpsimd.memset(mean_w[:], 1.0 / N).then_inc(pool_step, 1)
                    nc.gpsimd.memset(ones[:], 1.0).then_inc(pool_step, 1)
                    nc.gpsimd.iota(iota_e[:], pattern=[[1, E]], base=0, channel_multiplier=0,
                                   allow_small_or_imprecise_dtypes=True).then_inc(pool_step, 1)

                @block.tensor
                def _(pe):
                    pe.wait_ge(pool_step, 3)
                    for b in range(B):
                        mm = nc.tensor.matmul(ps_mean[:, b:b + 1], zsum[:, b, :], mean_w[:], start=True, stop=True)
                    mm.then_inc(pe_step, 1)
                    pe.wait_ge(params_loaded, 96)
                    nc.tensor.matmul(ps_bc[:, 256:384], ones[0:1, :], gb_row[:, 0, :], start=True, stop=True)
                    nc.tensor.matmul(ps_bc[:, 384:512], ones[0:1, :], gb_row[:, 1, :], start=True, stop=True).then_inc(pe_step, 1)
                    pe.wait_ge(dve_step, 1)
                    nc.tensor.matmul(ps_small[0:B, 0:E], meanT[:], Wr_sb[:], start=True, stop=False)
                    nc.tensor.matmul(ps_small[0:B, 0:E], ones[0:1, 0:B], br_row[:], start=False, stop=True).then_inc(pe_step, 1)
                    pe.wait_ge(dve_step, 5)
                    nc.tensor.matmul(ps_load[0:B, 0:E], ones[:, 0:B], rw[:], start=True, stop=True).then_inc(pe_step, 1)
                    pe.wait_ge(dve_step, 25)
                    for k in range(TOP_K):
                        nc.tensor.transpose(ps_t8[0:E, k * B:(k + 1) * B], onehot[:, k, :], ident[0:B, 0:B])
                    nc.tensor.transpose(ps_t8[0:E, C:C + B], w_dense[:], ident[0:B, 0:B]).then_inc(pe_step, 1)
                    pe.wait_ge(dve_step, 27)
                    for f in range(FB):
                        nc.tensor.matmul(ps_sel[:, f * C:(f + 1) * C], b1_sb[:, f * P:(f + 1) * P], oh_T[:], start=True, stop=True)
                    nc.tensor.matmul(ps_sel[:, FB * C:FB * C + B], b2_sb[:], wd_T[:], start=True, stop=True)
                    nc.tensor.matmul(ps_bc[:, 0:C], ones[:], w_diag[:].rearrange("b k c -> b (k c)"), start=True,
                                     stop=True).then_inc(pe_step, 1)

                @block.scalar
                def _(act):
                    act.wait_ge(dve_step, 3)
                    nc.scalar.activation(rw[:], logits[:], ACT.Exp, bias=peak[:, 0:1], accum_out=total[:, 0:1]).then_inc(act_step, 1)
                    act.wait_ge(dve_step, 13)
                    nc.scalar.activation(e2[:], rw2[:], ACT.Exp, bias=peak[:, 1:2], accum_out=total[:, 1:2]).then_inc(act_step, 1)
                    act.wait_ge(dve_step, 18)
                    nc.scalar.activation(top_e[:], top[:, 0:TOP_K], ACT.Exp, bias=peak[:, 2:3], accum_out=total[:, 2:3]).then_inc(act_step, 1)

                @block.vector
                def _(dve):
                    def step(ins, n):
                        ins.then_inc(dve_step, 1)
                        dve.wait_ge(dve_step, n)

                    dve.wait_ge(pe_step, 1)
                    step(nc.vector.tensor_copy(meanT[:], ps_mean[:]), 1)
                    dve.wait_ge(pe_step, 3)
                    step(nc.vector.tensor_copy(logits[:], ps_small[0:B, 0:E]), 2)
                    step(nc.vector.tensor_reduce(peak[:, 0:1], logits[:], AX_X, ALU.max, negate=True), 3)
                    dve.wait_ge(act_step, 1)
                    step(nc.vector.reciprocal(inv_total[:, 0:1], total[:, 0:1]), 4)
                    step(nc.vector.tensor_scalar(rw[:], rw[:], inv_total[:, 0:1], None, ALU.mult), 5)
                    dve.wait_ge(pe_step, 4)
                    step(nc.vector.tensor_scalar(load[:], ps_load[0:B, 0:E], float(N), CAPACITY, ALU.mult, ALU.max), 6)
                    step(nc.vector.reciprocal(quot[:], load[:]), 7)
                    step(nc.vector.tensor_scalar(over[:], load[:], CAPACITY, None, ALU.is_gt), 8)
                    step(nc.vector.scalar_tensor_tensor(quot[:], quot[:], CAPACITY, over[:], ALU.mult, ALU.mult), 9)
                    step(nc.vector.tensor_scalar(over[:], over[:], -1.0, 1.0, ALU.mult, ALU.add), 10)
                    step(nc.vector.tensor_tensor(quot[:], quot[:], over[:], ALU.add), 11)
                    step(nc.vector.tensor_tensor(rw2[:], rw[:], quot[:], ALU.mult), 12)
                    step(nc.vector.tensor_reduce(peak[:, 1:2], rw2[:], AX_X, ALU.max, negate=True), 13)
                    dve.wait_ge(act_step, 2)
                    step(nc.vector.reciprocal(inv_total[:, 1:2], total[:, 1:2]), 14)
                    step(nc.vector.tensor_scalar(rw2[:], e2[:], inv_total[:, 1:2], None, ALU.mult), 15)
                    step(nc.vector.max(top[:], rw2[:]), 16)
                    step(nc.vector.max_index(top_i[:], top[:], rw2[:]), 17)
                    step(nc.vector.tensor_scalar(peak[:, 2:3], top[:, 0:1], -1.0, None, ALU.mult), 18)
                    step(nc.vector.tensor_copy(top_f[:], top_i[:]), 19)
                    dve.wait_ge(act_step, 3)
                    step(nc.vector.reciprocal(inv_total[:, 2:3], total[:, 2:3]), 20)
                    step(nc.vector.tensor_scalar(top_w[:], top_e[:], inv_total[:, 2:3], None, ALU.mult), 21)
                    dve.wait_ge(pool_step, 3)
                    for k in range(TOP_K):
                        ins = nc.vector.tensor_scalar(onehot[:, k, :], iota_e[:], top_f[:, k:k + 1], None, ALU.is_equal)
                    step(ins, 22)
                    for k in range(TOP_K):
                        ins = nc.vector.tensor_scalar(w_diag[:, k, :], ident[0:B, 0:B], top_w[:, k:k + 1], None, ALU.mult)
                    step(ins, 23)
                    step(nc.vector.tensor_scalar(w_dense[:], onehot[:, 0, :], top_w[:, 0:1], None, ALU.mult), 24)
                    step(nc.vector.scalar_tensor_tensor(w_dense[:], onehot[:, 1, :], top_w[:, 1:2], w_dense[:], ALU.mult, ALU.add), 25)
                    dve.wait_ge(pe_step, 5)
                    step(nc.vector.tensor_copy(oh_T[:], ps_t8[0:E, 0:C]), 26)
                    step(nc.vector.tensor_copy(wd_T[:], ps_t8[0:E, C:C + B]), 27)
                    dve.wait_ge(pe_step, 6)
                    nc.vector.tensor_copy(b1_sel[:].rearrange("p f c -> p (f c)"), ps_sel[:, 0:FB * C])
                    nc.vector.tensor_copy(b2_mix[:], ps_sel[:, FB * C:FB * C + B])
                    nc.vector.tensor_copy(top_w_all[:], ps_bc[:, 0:C])
                    nc.vector.tensor_copy(gamma_all[:], ps_bc[:, 256:384])
                    step(nc.vector.tensor_copy(beta_all[:], ps_bc[:, 384:512]), 28)

            ps_l1 = [ps(f"ps_l1_{i}", [P, HW]) for i in range(4)]
            ps_y = [ps(f"ps_y{h}", [P, HW]) for h in range(2)]
            ps_zt, ps_yt = ps("ps_zt", [P, HW]), ps("ps_yt", [P, HW])
            w_raw_loaded = [sem(f"w_raw_loaded{i}") for i in range(2)]
            w_hi_done, w1_split, w2_split = sem("w_hi_done"), sem("w1_split"), sem("w2_split")
            zt_done, zt_hi_done, zt_split = sem("zt_done"), sem("zt_hi_done"), sem("zt_split")
            l1_done, gelu_done, g_hi_done, g_split = (
                sem(n) for n in ("l1_done", "gelu_done", "g_hi_done", "g_split"))
            y_mm, y_copied, yt_done, res_added, res_step, res_stats = (
                sem(n) for n in ("y_mm", "y_copied", "yt_done", "res_added", "res_step", "res_stats"))
            out_step, rstd_done, out_normed = sem("out_step"), sem("rstd_done"), sem("out_normed")
            out_stored = [sem(f"out_stored{h}") for h in range(2)]
            block = phase2.enter_context(nc.Block())

            def number(bt):
                return 2 * bt[0] + bt[1]

            def following(bt):
                return (bt[0], 1) if bt[1] == 0 else (bt[0] + 1, 0)

            def previous(bt):
                return (bt[0] - 1, 1) if bt[1] == 0 else (bt[0], 0)

            def is_first(bt):
                return isinstance(bt[0], int) and bt == (0, 0)

            def ahead(bt, u, n):
                return (bt, u + n) if u + n < UNITS else (following(bt), u + n - UNITS)

            def half(h):
                return slice(h * HW, (h + 1) * HW)

            def hblocks(h):
                return slice(h * HK, (h + 1) * HK)

            LAST_BATCH = (B // 2 - 1, 1)

            def steps(eng, step):
                def round_(bt, last=False):
                    for u in range(1, UNITS):
                        step(bt, u, last)
                    if not last:
                        step(following(bt), 0, False)

                step((0, 0), 0, False)
                round_((0, 0))
                with eng.Fori(0, B // 2 - 1) as i:
                    round_((i, 1))
                    round_((i + 1, 0))
                round_(LAST_BATCH, True)

            @block.sync
            def _(sp):
                def gather(bt):
                    i, parity = bt
                    for k in range(TOP_K):
                        e = sp.value_load(expert_row[0:1, bass.ds(k * B + number(bt), 1)], min_val=0, max_val=E - 1)
                        sp.dma_start(w_raw[parity][:, k, 0:F], W1[e]).then_inc(w_raw_loaded[parity], 16)
                        sp.dma_start(w_raw[parity][:, k, F:2 * F].rearrange("p (c d) -> p c d", d=D),
                                     W2.rearrange("e (c p) d -> e p c d", p=P)[e]).then_inc(w_raw_loaded[parity], 16)

                def refill(bt):
                    i, parity = bt
                    sp.wait_ge(w1_split, 2 * number(bt) + 2)
                    detach(sp)
                    sp.wait_ge(w2_split, 2 * number(bt) + 2)
                    gather((i + 1, parity))
                    sp.wait_ge(zt_done, 2 * number(bt) + 2)
                    sp.dma_start(z_in[parity][:], batch(z_dram, number(bt) + 2)).then_inc(z_in_loaded[parity], 16)

                def store(bt, h):
                    sp.wait_ge(out_step, 4 * (2 * number(bt) + h) + 4)
                    sp.dma_start(batch(out, number(bt))[:, hblocks(h), :], res[h][:]).then_inc(out_stored[h], 16)

                def residuals(bt):
                    parity = bt[1]
                    sp.dma_start(z_res[parity][:], batch(z_dram, number(bt) + 2)).then_inc(z_res_loaded[parity], 16)
                    sp.dma_start(x_res[parity][:], batch(x1_dram, number(bt) + 2)).then_inc(x_res_loaded[parity], 16)

                for h in range(2):
                    sp.sem_inc(out_stored[h], 16)
                gather((0, 0))
                gather((0, 1))
                refill((0, 0))
                refill((0, 1))
                with sp.Fori(0, B // 2 - 2) as i:
                    for parity in range(2):
                        store((i, parity), 0)
                        refill((i + 1, parity))
                        store((i, parity), 1)
                        residuals((i, parity))
                for i in range(B // 2 - 2, B // 2):
                    for parity in range(2):
                        store((i, parity), 0)
                        store((i, parity), 1)
                        if i < B // 2 - 1:
                            residuals((i, parity))
                for h in range(2):
                    sp.wait_ge(out_stored[h], 16 * B + 16)

            @block.gpsimd
            def _(pool):
                def split_first_weights(bt):
                    parity = bt[1]
                    for k in range(TOP_K):
                        pool.wait_ge(w_hi_done, 2 * number(bt) + k + 1)
                        nc.gpsimd.tensor_tensor(w_lo[parity][:, k, 0:F], w_raw[parity][:, k, 0:F], exact(w_hi[parity][:, k, 0:F]),
                                                ALU.subtract).then_inc(w1_split, 1)

                def finish(bt, h):
                    i, parity = bt
                    n = 2 * number(bt) + h
                    shape = [P, HK, D]
                    x_half = x_res[parity][:, hblocks(h), :]
                    inverse_deviation(pool, mvb[h], rstdb[h], res_stats, n + 1, out_step, 4 * n + 1, rstd_done)
                    pool.wait_ge(x_res_loaded[parity], 16 * i + 16)
                    nc.gpsimd.tensor_tensor(x_half, x_half, beta_all[:].unsqueeze(1).to_broadcast(shape), ALU.add).then_inc(out_step, 1)
                    pool.wait_ge(out_normed, n + 1)
                    nc.gpsimd.tensor_tensor(res[h][:], res[h][:], gamma_all[:].unsqueeze(1).to_broadcast(shape), ALU.mult).then_inc(out_step, 1)
                    pool.wait_ge(out_step, 4 * n + 3)
                    nc.gpsimd.tensor_tensor(res[h][:], res[h][:], x_half, ALU.add).then_inc(out_step, 1)

                split_first_weights((0, 0))
                split_first_weights((0, 1))
                with pool.Fori(0, B // 2 - 1) as i:
                    for parity in range(2):
                        finish((i, parity), 0)
                        split_first_weights((i + 1, parity))
                        finish((i, parity), 1)
                for parity in range(2):
                    for h in range(2):
                        finish((B // 2 - 1, parity), h)

            @block.tensor
            def _(pe):
                def tokens_to_features(bt, h):
                    n = 2 * number(bt) + h
                    pe.wait_ge(z_in_loaded[bt[1]], 16 * bt[0] + 16)
                    if not (isinstance(n, int) and n == 0):
                        pe.wait_ge(zt_split, n)
                    for k in range(HK):
                        tr = nc.tensor.transpose(ps_zt[:, k * P:(k + 1) * P], z_in[bt[1]][:, h * HK + k, :], ident[:])
                    tr.then_inc(zt_done, 1)

                def features_to_tokens(bt, h):
                    n = 2 * number(bt) + h
                    pe.wait_ge(y_copied, n + 1)
                    if not (isinstance(n, int) and n == 0):
                        pe.wait_ge(res_added, n)
                    for k in range(HK):
                        tr = nc.tensor.transpose(ps_yt[:, k * P:(k + 1) * P], yT[h][:, k * P:(k + 1) * P], ident[:])
                    tr.then_inc(yt_done, 1)

                def first_product(bt, u):
                    h, k, f = u // 4, u // 2 % 2, u % 2
                    if u % 4 == 0:
                        pe.wait_ge(zt_split, 2 * number(bt) + h + 1)
                    if u in (0, 2):
                        pe.wait_ge(w1_split, 2 * number(bt) + k + 1)
                    w_h, w_l = (w[bt[1]][:, k, f * P:(f + 1) * P] for w in (w_hi, w_lo))
                    z_h, z_l = zT_hi[:, half(h)], zT_lo[:, half(h)]
                    nc.tensor.matmul(ps_l1[u % 4][:], w_h, z_h, start=True, stop=False)
                    nc.tensor.matmul(ps_l1[u % 4][:], w_h, z_l, start=False, stop=False)
                    nc.tensor.matmul(ps_l1[u % 4][:], w_l, z_h, start=False, stop=True).then_inc(l1_done, 1)

                def second_product(bt, u):
                    h, k, f = u // 4, u // 2 % 2, u % 2
                    if u in (0, 2):
                        pe.wait_ge(w2_split, 2 * number(bt) + k + 1)
                    pe.wait_ge(g_split, UNITS * number(bt) + u + 1)
                    w_h, w_l = (w[bt[1]][:, k, F + f * P:F + (f + 1) * P] for w in (w_hi, w_lo))
                    nc.tensor.matmul(ps_y[h][:], w_h, g_hi[u % 4][:], start=(u % 4 == 0), stop=False)
                    nc.tensor.matmul(ps_y[h][:], w_h, g_lo[u % 4][:], start=False, stop=False)
                    mm = nc.tensor.matmul(ps_y[h][:], w_l, g_hi[u % 4][:], start=False, stop=(u % 4 == 3))
                    if u % 4 == 3:
                        mm.then_inc(y_mm, 1)

                def step(bt, u, last):
                    if not (last and u + 3 >= UNITS):
                        first_product(*ahead(bt, u, 3))
                    second_product(bt, u)
                    if u == 1 and not is_first(bt):
                        features_to_tokens(previous(bt), 1)
                    if u == 2 and not last:
                        tokens_to_features(following(bt), 0)
                    if u == 5:
                        features_to_tokens(bt, 0)
                    if u == 6 and not last:
                        tokens_to_features(following(bt), 1)

                tokens_to_features((0, 0), 0)
                first_product((0, 0), 0)
                first_product((0, 0), 1)
                tokens_to_features((0, 0), 1)
                first_product((0, 0), 2)
                steps(pe, step)
                features_to_tokens(LAST_BATCH, 1)

            @block.scalar
            def _(act):
                def round_tokens(bt, h):
                    act.wait_ge(zt_done, 2 * number(bt) + h + 1)
                    nc.scalar.activation(zT_hi[:, half(h)], ps_zt[:], ACT.Copy).then_inc(zt_hi_done, 1)

                def copy_mixture(bt, h):
                    act.wait_ge(y_mm, 2 * number(bt) + h + 1)
                    detach(act)
                    nc.scalar.activation(yT[h][:], ps_y[h][:], ACT.Identity,
                                         bias=b2_mix[:, bass.ds(number(bt), 1)]).then_inc(y_copied, 1)

                def activate(bt, u):
                    k, f = u // 2 % 2, u % 2
                    U = UNITS * number(bt) + u
                    act.wait_ge(l1_done, U + 1)
                    detach(act)
                    nc.scalar.activation(act_out[u % 4][:], ps_l1[u % 4][:], ACT.Gelu,
                                         bias=b1_sel[:, f, bass.ds(k * B + number(bt), 1)]).then_inc(gelu_done, 1)
                    act.wait_ge(gelu_done, U + 1)
                    nc.scalar.activation(g_hi[u % 4][:], act_out[u % 4][:], ACT.Copy).then_inc(g_hi_done, 1)

                def round_weights(bt, k):
                    i, parity = bt
                    if k == 0:
                        act.wait_ge(w_raw_loaded[parity], 32 * TOP_K * i + 32 * TOP_K)
                        if not (isinstance(i, int) and number(bt) <= 1):
                            act.wait_ge(y_mm, 2 * (number(bt) - 1))
                            detach(act)
                    nc.scalar.activation(w_hi[parity][:, k, F:2 * F], w_raw[parity][:, k, F:2 * F], ACT.Copy,
                                         scale=top_w_all[:, bass.ds(k * B + number(bt), 1)])
                    nc.scalar.activation(w_hi[parity][:, k, 0:F], w_raw[parity][:, k, 0:F], ACT.Copy).then_inc(w_hi_done, 1)

                def step(bt, u, last):
                    if not (last and u + 2 >= UNITS):
                        activate(*ahead(bt, u, 2))
                    if u == 0 and not is_first(bt):
                        copy_mixture(previous(bt), 1)
                    if u in (1, 2) and not last:
                        round_weights(following(bt), u - 1)
                    if u == 3 and not last:
                        round_tokens(following(bt), 0)
                    if u == 4:
                        copy_mixture(bt, 0)
                    if u == 7 and not last:
                        round_tokens(following(bt), 1)

                for k in range(TOP_K):
                    round_weights((0, 0), k)
                round_tokens((0, 0), 0)
                activate((0, 0), 0)
                round_tokens((0, 0), 1)
                activate((0, 0), 1)
                steps(act, step)
                copy_mixture(LAST_BATCH, 1)

            @block.vector
            def _(dve):
                def split_tokens(bt, h):
                    dve.wait_ge(zt_hi_done, 2 * number(bt) + h + 1)
                    nc.vector.tensor_tensor(zT_lo[:, half(h)], ps_zt[:], exact(zT_hi[:, half(h)]), ALU.subtract).then_inc(zt_split, 1)

                def split_second_weights(bt, k):
                    parity = bt[1]
                    dve.wait_ge(w_hi_done, 2 * number(bt) + k + 1)
                    detach(dve)
                    nc.vector.scalar_tensor_tensor(w_lo[parity][:, k, F:2 * F], w_raw[parity][:, k, F:2 * F],
                                                   top_w_all[:, bass.ds(k * B + number(bt), 1)],
                                                   exact(w_hi[parity][:, k, F:2 * F]), ALU.mult, ALU.subtract).then_inc(w2_split, 1)

                def split_activations(bt, u):
                    dve.wait_ge(g_hi_done, UNITS * number(bt) + u + 1)
                    nc.vector.tensor_tensor(g_lo[u % 4][:], act_out[u % 4][:], exact(g_hi[u % 4][:]), ALU.subtract).then_inc(g_split, 1)

                def add_residual(bt, h):
                    i, parity = bt
                    n = 2 * number(bt) + h
                    dve.wait_ge(yt_done, n + 1)
                    dve.wait_ge(z_res_loaded[parity], 16 * i + 16)
                    dve.wait_ge(out_stored[h], 16 * number(bt) + 16)
                    nc.vector.tensor_tensor(res[h][:], ps_yt[:].rearrange("p (k d) -> p k d", d=D), z_res[parity][:, hblocks(h), :],
                                            ALU.add).then_inc(res_added, 1)
                    dve.wait_ge(res_added, n + 1)
                    token_stats(dve, HK, res[h], stat6b, mvb[h], res_step, n + 1, res_stats)

                def apply_norm(bt, h):
                    n = 2 * number(bt) + h
                    dve.wait_ge(rstd_done, n + 1)
                    detach(dve)
                    for k in range(HK):
                        ins = nc.vector.tensor_scalar(res[h][:, k, :], res[h][:, k, :], mvb[h][:, k, 0:1], rstdb[h][:, k:k + 1],
                                                      ALU.subtract, ALU.mult)
                    ins.then_inc(out_normed, 1)

                def step(bt, u, last):
                    if not (last and u + 2 >= UNITS):
                        split_activations(*ahead(bt, u, 2))
                    if u == 0 and not is_first(bt):
                        apply_norm(previous(bt), 0)
                    if u == 2 and not is_first(bt):
                        add_residual(previous(bt), 1)
                    if u == 4 and not is_first(bt):
                        apply_norm(previous(bt), 1)
                    if u in (3, 4) and not last:
                        split_second_weights(following(bt), u - 3)
                    if u == 3 and not last:
                        split_tokens(following(bt), 0)
                    if u == 6:
                        add_residual(bt, 0)
                    if u == 7 and not last:
                        split_tokens(following(bt), 1)

                for k in range(TOP_K):
                    split_second_weights((0, 0), k)
                split_tokens((0, 0), 0)
                split_activations((0, 0), 0)
                split_tokens((0, 0), 1)
                split_activations((0, 0), 1)
                steps(dve, step)
                apply_norm(LAST_BATCH, 0)
                add_residual(LAST_BATCH, 1)
                apply_norm(LAST_BATCH, 1)


_INS = ["x", "adj", "nodemask", "L0_gnn_weight", "L0_gnn_w_ih", "L0_gnn_w_hh", "L0_gnn_b_ih", "L0_gnn_b_hh", "L0_ffn_Wr",
        "L0_ffn_br", "L0_ffn_W1", "L0_ffn_b1", "L0_ffn_W2", "L0_ffn_b2", "L0_ffn_gamma", "L0_ffn_beta"]


def kernel(**inputs):
    import numpy as _np
    import concourse.bacc as _bacc
    from concourse import mybir as _mybir
    from concourse.bass_utils import run_bass_kernel_spmd as _run

    nc = _bacc.Bacc("TRN2", target_bir_lowering=False, num_devices=1)
    arrays, args = {}, []
    for name in _INS:
        a = _np.ascontiguousarray(inputs[name])
        arrays[f"in_{name}_dram"] = a
        args.append(nc.dram_tensor(f"in_{name}_dram", a.shape, _mybir.dt.from_np(a.dtype), kind="ExternalInput").ap())
    args.append(nc.dram_tensor("out_dram", inputs["x"].shape, F32, kind="ExternalOutput").ap())
    build_gnn_ffn(nc, *args)
    return _run(nc, [arrays], core_ids=[0]).results[0]["out_dram"]
```

```python
from contextlib import ExitStack

import concourse.bass as bass
from concourse import mybir

ALU = mybir.AluOpType
ACT = mybir.ActivationFunctionType
F32 = mybir.dt.float32
F32R = mybir.dt.float32r
U8 = mybir.dt.uint8
U32 = mybir.dt.uint32
AX_X = mybir.AxisListType.X

P = 128
LN_EPS = 1e-5
TOP_K = 2
CAPACITY_FACTOR = (5, 4)



def exact(ap):
    return ap.bitcast(F32)


def build_gnn_ffn(nc, x, adj, nodemask, gnn_w, w_ih, w_hh, b_ih, b_hh, Wr, br, W1, b1, W2, b2, gamma, beta, out):
    B, N, D = x.shape
    LAYERS = gnn_w.shape[0]
    E, _, F = W1.shape
    KB = N // P
    HW = N // 2
    HK = KB // 2
    G = 3 * D
    PAIRS = B // 2
    SLOTS = 4
    S_PAIR = SLOTS * LAYERS
    LAST = LAYERS - 1
    CHUNKS = 2 * KB
    FB = F // P
    UNITS = 2 * TOP_K * FB
    CAPACITY = float(-(-B * N * CAPACITY_FACTOR[0] // (CAPACITY_FACTOR[1] * E)))
    assert D == P and HW == 512 and CHUNKS == SLOTS * (LAYERS - 1) and FB == 2 and UNITS == 8 and PAIRS >= 2

    wc_dram = nc.dram_tensor("wc_dram", [LAYERS, P, 2 * G], F32, kind="Internal").ap()
    x1_dram = nc.dram_tensor("x1_dram", [B, N, D], F32, kind="Internal").ap()
    z_dram = nc.dram_tensor("z_dram", [B, N, D], F32, kind="Internal").ap()

    def batch(t, b):
        return t.rearrange("b (k p) d -> b p k d", p=P)[b]

    adj_rows = adj.rearrange("b i j -> (b i) j")

    with ExitStack() as whole:
        def alloc_in(stack, space):
            return lambda name, shape, dt=F32: stack.enter_context(space(name, shape, dt))

        def sem_in(stack):
            return lambda name: stack.enter_context(nc.semaphore(name))

        sb = alloc_in(whole, nc.sbuf_tensor)
        sem = sem_in(whole)
        ident = sb("ident", [P, P])
        zsum = sb("zsum", [P, B, D])
        neg_half = sb("neg_half", [P, KB])
        ones, minus_ones = sb("ones", [P, P]), sb("minus_ones", [P, P])
        iota_e = sb("iota_e", [B, E])
        xbuf = [sb(f"xbuf{n}", [P, KB, D]) for n in range(2)]
        xn = [sb(f"xn{n}", [P, KB, D]) for n in range(2)]
        mv2 = [sb(f"mv2_{n}", [P, KB, 2]) for n in range(2)]
        rstd_last = [sb(f"rstd_last{n}", [P, KB]) for n in range(2)]
        mean_rstd = [sb(f"mean_rstd{n}", [P, KB]) for n in range(2)]
        sumT = sb("sumT", [P, B])
        warm = sb("warm", [1, 1])
        Wr_sb, br_row = sb("Wr_sb", [P, E]), sb("br_row", [1, E])
        b1_sb, b2_sb = sb("b1_sb", [E, F]), sb("b2_sb", [E, D])
        gb_row = sb("gb_row", [1, 2, D])
        params_loaded, wr_scaled = sem("params_loaded"), sem("wr_scaled")
        ident_zero, ident_ready, consts_ready = sem("ident_zero"), sem("ident_ready"), sem("consts_ready")
        waits_passed = sem("waits_passed")

        def detach(eng):
            eng.sem_inc(waits_passed, 1)

        def token_stats(dve, blocks, src, stat6, mv, step_sem, step, done_sem):
            if not (isinstance(step, int) and step == 1):
                dve.wait_ge(done_sem, step - 1)
            for k in range(blocks):
                ins = nc.vector.bn_stats(stat6[:, k, :], src[:, k, :])
            ins.then_inc(step_sem, 1)
            dve.wait_ge(step_sem, step)
            detach(dve)
            for k in range(blocks):
                ins = nc.vector.bn_aggr(mv[:, k, :], stat6[:, k, :])
            ins.then_inc(done_sem, 1)

        def inverse_deviation(pool, mv, rstd, stats_sem, stats_count, step_sem, step, done_sem):
            pool.wait_ge(stats_sem, stats_count)
            detach(pool)
            blocks = mv.shape[1]
            nc.gpsimd.tensor_scalar(rstd[:, 0:blocks], mv[:, :, 1], LN_EPS, None, ALU.add).then_inc(step_sem, 1)
            pool.wait_ge(step_sem, step)
            nc.gpsimd.tensor_tensor(rstd[:, 0:blocks], rstd[:, 0:blocks], neg_half[:, 0:blocks], ALU.pow).then_inc(done_sem, 1)

        def norm_apply(pool, blocks, src, dst, mv, rstd, stats_sem, stats_count, step_sem, step, done_sem):
            pool.wait_ge(stats_sem, stats_count)
            detach(pool)
            nc.gpsimd.tensor_scalar(rstd[:, 0:blocks], mv[:, :, 1], LN_EPS, None, ALU.add).then_inc(step_sem, 1)
            pool.wait_ge(step_sem, step)
            nc.gpsimd.tensor_tensor(rstd[:, 0:blocks], rstd[:, 0:blocks], neg_half[:, 0:blocks], ALU.pow).then_inc(step_sem, 1)
            pool.wait_ge(step_sem, step + 1)
            detach(pool)
            for k in range(blocks):
                ins = nc.gpsimd.tensor_scalar(dst[:, k, :], src[:, k, :], mv[:, k, 0:1], rstd[:, k:k + 1],
                                              ALU.subtract, ALU.mult)
            ins.then_inc(done_sem, 1)

        with ExitStack() as phase1:
            sb = alloc_in(phase1, nc.sbuf_tensor)
            sem = sem_in(phase1)
            a_mat = [sb(f"a_mat{n}", [P, KB, N], F32R) for n in range(2)]
            a_next = sb("a_next", [P, CHUNKS, N], U8)
            a_raw = sb("a_raw", [P, 2, N])
            w_cur = [sb(f"w_cur{n}", [P, 2 * G], F32R) for n in range(2)]
            w_hhT = sb("w_hhT", [P, 2 * G], F32R)
            hT = [sb(f"hT{n}", [P, N]) for n in range(2)]
            hT_hi = [sb(f"hT_hi{n}", [P, N], F32R) for n in range(2)]
            hT_lo = [sb(f"hT_lo{n}", [P, N], F32R) for n in range(2)]
            nat_hi = [sb(f"nat_hi{n}", [P, KB, D], F32R) for n in range(2)]
            nat_lo = [sb(f"nat_lo{n}", [P, KB, D], F32R) for n in range(2)]
            agg_hi = [sb(f"agg_hi{h}", [P, HW], F32R) for h in range(2)]
            agg_lo = [sb(f"agg_lo{h}", [P, HW], F32R) for h in range(2)]
            z_nat = sb("z_nat", [P, KB, D])
            z_fold = sb("z_fold", [P, HK, D])
            cand = [sb(f"cand{h}", [P, HW]) for h in range(2)]
            gate_z = [sb(f"gate_z{h}", [P, HW]) for h in range(2)]
            diff = sb("diff", [P, HW])
            stat6 = sb("stat6", [P, KB, 6])
            mv1 = [sb(f"mv1_{n}", [P, KB, 2]) for n in range(2)]
            rstd = sb("rstd", [P, KB])
            bias_ih, bias_hh, bias_rz = sb("bias_ih", [P, 3]), sb("bias_hh", [P, 3]), sb("bias_rz", [P, 2])
            mask_tok = sb("mask_tok", [P, B * KB])

            rstd_first = sb("rstd_first", [P, KB])
            a_first = [exact(a_next[:, 4 * r:4 * r + 4, :]).rearrange("p c n -> p (c n)") for r in range(4)] + [a_raw[:, r] for r in range(2)]
            first_loaded = [sem(f"first_loaded{r}") for r in range(6)]
            a_raw_loaded = [sem("a_raw_loaded0"), sem("a_raw_loaded1")]
            wc_stored = sem("wc_stored")
            w_cur_loaded = [sem(f"w_cur_loaded{n}") for n in range(2)]
            a_compared = sem("a_compared")
            stats_step, stats_done, norm_step = sem("stats_step"), sem("stats_done"), sem("norm_step")
            ln1_done = [sem(f"ln1_done{n}") for n in range(2)]
            xbuf_loaded = [sem(f"xbuf_loaded{n}") for n in range(2)]

            def compare_first(c):
                nc.vector.tensor_scalar(a_mat[c // KB][:, c % KB, :], a_first[c % 6], 0.0, None, ALU.not_equal).then_inc(a_compared, 1)

            with ExitStack() as stage0:
                sb0, ps0, sem = alloc_in(stage0, nc.sbuf_tensor), alloc_in(stage0, nc.psum_tensor), sem_in(stage0)
                w_ih_nat, w_hh_nat = sb0("w_ih_nat", [P, 3, D]), sb0("w_hh_nat", [P, 3, D])
                w_nat, w_T = sb0("w_nat", [P, LAYERS, D]), sb0("w_T", [P, LAYERS, D])
                w_ihT = sb0("w_ihT", [P, G])
                mask_nat = sb0("mask_nat", [B * KB, P])
                wc_split = [w_cur[0][:], hT_hi[1][:, 0:2 * G], hT_lo[1][:, 0:2 * G]] + [a_mat[1][:, KB - k, 0:2 * G] for k in (2, 1)]
                ps_ih, ps_hh, ps_wt = ps0("ps_ih", [P, G]), ps0("ps_hh", [P, G]), ps0("ps_wt", [P, 2, 512])
                ps_mask = ps0("ps_mask", [P, B * KB])
                ps_wc = [ps0(f"ps_wc{i}", [P, G]) for i in range(2)]
                w_loaded, mask_loaded, bias_loaded = (sem(n) for n in ("w_loaded", "mask_loaded", "bias_loaded"))
                x_loaded = [sem(f"x_loaded{n}") for n in range(2)]
                transposed, turned, hi_done, wc_done, wc_lo_done, bias_added = (
                    sem(n) for n in ("transposed", "turned", "hi_done", "wc_done", "wc_lo_done", "bias_added"))
                block = stage0.enter_context(nc.Block())

                @block.sync
                def _(sp):
                    sp.dma_start(xn[0][:], batch(x, 0)).then_inc(x_loaded[0], 16)
                    sp.dma_start(w_ih_nat[:], w_ih.rearrange("(g p) d -> p g d", p=P)).then_inc(w_loaded, 16)
                    sp.dma_start(w_hh_nat[:], w_hh.rearrange("(g p) d -> p g d", p=P)).then_inc(w_loaded, 16)
                    sp.dma_start(w_nat[:], gnn_w.rearrange("l d e -> d l e")).then_inc(w_loaded, 16)
                    sp.dma_start(xn[1][:], batch(x, 1)).then_inc(x_loaded[1], 16)
                    for c in range(CHUNKS - 2):
                        if c >= 6:
                            sp.wait_ge(a_compared, c - 5)
                        sp.dma_start(a_first[c % 6], adj_rows[c * P:(c + 1) * P, :]).then_inc(first_loaded[c % 6], 16)

                @block.scalar
                def _(act):
                    act.dma_start(mask_nat[:], nodemask.rearrange("b (k p) -> (b k) p", p=P)).then_inc(mask_loaded, 16)
                    with nc.allow_non_contiguous_dma(reason="384 bias values, one per partition"):
                        act.dma_start(bias_ih[:], b_ih.rearrange("(g p) -> p g", p=P)).then_inc(bias_loaded, 16)
                        act.dma_start(bias_hh[:], b_hh.rearrange("(g p) -> p g", p=P)).then_inc(bias_loaded, 16)
                    act.wait_ge(transposed, 1)
                    nc.scalar.activation(w_ihT[:], ps_ih[:], ACT.Copy).then_inc(turned, 1)
                    act.wait_ge(transposed, 3)
                    nc.scalar.activation(w_T[:, 0:4, :], ps_wt[:, 0, :].rearrange("p (l d) -> p l d", d=D), ACT.Copy).then_inc(turned, 1)
                    nc.scalar.activation(w_T[:, 4, :], ps_wt[:, 1, 0:D], ACT.Copy).then_inc(turned, 1)
                    nc.scalar.activation(w_hhT[:, 0:G], ps_hh[:], ACT.Copy).then_inc(hi_done, 1)
                    for n in range(LAYERS):
                        act.wait_ge(wc_done, n + 1)
                        nc.scalar.activation(wc_split[n][:, 0:G], ps_wc[n % 2][:], ACT.Copy).then_inc(hi_done, 1)
                        act.wait_ge(wc_lo_done, n + 1)
                        if n == 0:
                            nc.scalar.activation(w_cur[1][:], w_cur[0][:], ACT.Copy).then_inc(w_cur_loaded[1], 16)
                            act.sem_inc(w_cur_loaded[0], 16)
                        act.dma_start(wc_dram[n], exact(wc_split[n])).then_inc(wc_stored, 16)

                @block.gpsimd
                def _(pool):
                    nc.gpsimd.memset(ident[:], 0.0).then_inc(ident_zero, 1)
                    nc.gpsimd.memset(neg_half[:], -0.5).then_inc(consts_ready, 1)
                    nc.gpsimd.memset(ones[:], 1.0).then_inc(consts_ready, 1)
                    nc.gpsimd.memset(minus_ones[:], -1.0).then_inc(consts_ready, 1)
                    nc.gpsimd.iota(iota_e[:], pattern=[[1, E]], base=0, channel_multiplier=0,
                                   allow_small_or_imprecise_dtypes=True).then_inc(consts_ready, 1)
                    pool.wait_ge(ident_zero, 1)
                    nc.gpsimd.affine_select(out=ident[:], in_=ident[:], compare_op=ALU.not_equal, fill=1.0, base=0,
                                            pattern=[[-1, P]], channel_multiplier=1).then_inc(ident_ready, 1)
                    pool.wait_ge(consts_ready, 4)
                    inverse_deviation(pool, mv1[0], rstd_first, stats_done, 1, norm_step, 1, norm_step)
                    norm_apply(pool, KB, xn[1], xn[1], mv1[1], rstd, stats_done, 2, norm_step, 3, ln1_done[1])
                    pool.wait_ge(ln1_done[1], 1)

                @block.tensor
                def _(pe):
                    pe.wait_ge(ident_ready, 1)
                    pe.wait_ge(w_loaded, 48)
                    for g in range(3):
                        tr = nc.tensor.transpose(ps_ih[:, g * D:(g + 1) * D], w_ih_nat[:, g, :], ident[:])
                    tr.then_inc(transposed, 1)
                    for g in range(3):
                        tr = nc.tensor.transpose(ps_hh[:, g * D:(g + 1) * D], w_hh_nat[:, g, :], ident[:])
                    tr.then_inc(transposed, 1)
                    for n in range(LAYERS):
                        tr = nc.tensor.transpose(ps_wt[:, n // 4, n % 4 * D:(n % 4 + 1) * D], w_nat[:, n, :], ident[:])
                    tr.then_inc(transposed, 1)
                    pe.wait_ge(mask_loaded, 16)
                    nc.tensor.transpose(ps_mask[:], mask_nat[:], ident[0:B * KB, 0:B * KB]).then_inc(transposed, 1)
                    pe.wait_ge(turned, 3)
                    for n in range(LAYERS):
                        if n >= 2:
                            pe.wait_ge(wc_lo_done, n - 1)
                        nc.tensor.matmul(ps_wc[n % 2][:], w_T[:, n, :], w_ihT[:], start=True, stop=True).then_inc(wc_done, 1)

                @block.vector
                def _(dve):
                    def compare(c):
                        dve.wait_ge(first_loaded[c % 6], 16 * (c // 6 + 1))
                        compare_first(c)

                    for lane in range(2):
                        dve.wait_ge(x_loaded[lane], 16)
                        token_stats(dve, KB, xn[lane], stat6, mv1[lane], stats_step, lane + 1, stats_done)
                    dve.wait_ge(norm_step, 2)
                    for k in range(KB):
                        ins = nc.vector.tensor_scalar(xn[0][:, k, :], xn[0][:, k, :], mv1[0][:, k, 0:1], rstd_first[:, k:k + 1],
                                                      ALU.subtract, ALU.mult)
                    ins.then_inc(ln1_done[0], 1)
                    for n in range(LAYERS):
                        compare(n)
                        dve.wait_ge(hi_done, 2 + n)
                        nc.vector.tensor_tensor(wc_split[n][:, G:2 * G], ps_wc[n % 2][:], exact(wc_split[n][:, 0:G]),
                                                ALU.subtract).then_inc(wc_lo_done, 1)
                    for c in range(LAYERS, KB):
                        compare(c)
                    dve.wait_ge(hi_done, 1)
                    nc.vector.tensor_tensor(w_hhT[:, G:2 * G], ps_hh[:], exact(w_hhT[:, 0:G]), ALU.subtract).then_inc(turned, 1)
                    dve.wait_ge(transposed, 4)
                    nc.vector.tensor_copy(mask_tok[:], ps_mask[:]).then_inc(turned, 1)
                    dve.wait_ge(bias_loaded, 32)
                    nc.vector.tensor_tensor(bias_rz[:], bias_ih[:, 0:2], bias_hh[:, 0:2], ALU.add).then_inc(bias_added, 1)

            with ExitStack() as stage1:
                ps1, sem = alloc_in(stage1, nc.psum_tensor), sem_in(stage1)
                ps_agg = [ps1(f"ps_agg{h}", [P, HW]) for h in range(2)]
                ps_t = [ps1(f"ps_t{h}", [P, HW]) for h in range(2)]
                ps_r, ps_z, ps_hn, ps_in = (ps1(n, [P, HW]) for n in ("ps_r", "ps_z", "ps_hn", "ps_in"))

                xn_loaded = [sem(f"xn_loaded{n}") for n in range(2)]
                a_widened = [sem(f"a_widened{n}") for n in range(2)]
                trans_done, xt_done = sem("trans_done"), sem("xt_done")
                nat_hi_done, nat_ready = sem("nat_hi_done"), sem("nat_ready")
                agg_done, agg_hi_done, agg_split = sem("agg_done"), sem("agg_hi_done"), sem("agg_split")
                r_mm, hn_mm, in_mm, z_mm = sem("r_mm"), sem("hn_mm"), sem("in_mm"), sem("z_mm")
                r_act, n_act, z_act = sem("r_act"), sem("n_act"), sem("z_act")
                cand_done, pre_done, diff_done, zd_done = sem("cand_done"), sem("pre_done"), sem("diff_done"), sem("zd_done")
                h_done = sem("h_done")
                hT_hi_done = [sem(f"hT_hi_done{n}") for n in range(2)]
                hT_ready = [sem(f"hT_ready{n}") for n in range(2)]
                x1_done, ln2_done, fold_step = sem("x1_done"), sem("ln2_done"), sem("fold_step")
                x1z_stored = sem("x1z_stored")
                last_stat_step, last_stats, last_step = sem("last_stat_step"), sem("last_stats"), sem("last_step")
                sums_done, sums_copied, x_last_stored = sem("sums_done"), sem("sums_copied"), sem("x_last_stored")
                block = stage1.enter_context(nc.Block())

                def half(h):
                    return slice(h * HW, (h + 1) * HW)

                def hblocks(h):
                    return slice(h * HK, (h + 1) * HK)

                def flat(ap):
                    return ap.rearrange("p k d -> p (k d)")

                def before(q):
                    return (q - 1) % SLOTS // 2, (q - 1) % 2

                @block.sync
                def _(sp):
                    def chunk(p, l, q):
                        c = CHUNKS * (p + 1) + SLOTS * (l - 1) + q
                        sp.wait_ge(a_compared, c - 1)
                        sp.dma_start(a_raw[:, q % 2], adj_rows[bass.ds(c * P, P), :]).then_inc(a_raw_loaded[q % 2], 16)

                    def weights(lane, layer, slots_done):
                        sp.wait_ge(z_mm, slots_done)
                        sp.dma_start(exact(w_cur[lane][:]), wc_dram[layer]).then_inc(w_cur_loaded[lane], 16)

                    def pair(p, last):
                        if not last:
                            for lane in range(2):
                                sp.wait_ge(hT_ready[lane], 2 * LAYERS * p + 2)
                                detach(sp)
                                sp.wait_ge(nat_ready, S_PAIR * p + 2 + 2 * lane)
                                sp.dma_start(xn[lane][:], batch(x, 2 * p + 2 + lane)).then_inc(xn_loaded[lane], 16)
                        weights(0, 1, S_PAIR * p + 2)
                        with sp.Fori(1, LAST) as l:
                            if not last:
                                chunk(p, l, 0)
                                chunk(p, l, 1)
                            weights(1, l, S_PAIR * p + SLOTS * l)
                            if not last:
                                chunk(p, l, 2)
                                chunk(p, l, 3)
                            weights(0, l + 1, S_PAIR * p + SLOTS * l + 2)
                        if not last:
                            chunk(p, LAST, 0)
                            chunk(p, LAST, 1)
                        weights(1, LAST, S_PAIR * p + SLOTS * LAST)
                        if not last:
                            chunk(p, LAST, 2)
                            chunk(p, LAST, 3)
                            weights(0, 0, S_PAIR * p + SLOTS * LAST + 2)
                            weights(1, 0, S_PAIR * (p + 1))

                    for c in range(CHUNKS - 2, CHUNKS):
                        sp.wait_ge(a_compared, c - 5)
                        sp.dma_start(a_first[c % 6], adj_rows[c * P:(c + 1) * P, :]).then_inc(first_loaded[c % 6], 16)
                    for dst, src in ((Wr_sb[:], Wr), (br_row[:], br.rearrange("(o e) -> o e", o=1)), (b1_sb[:], b1), (b2_sb[:], b2),
                                     (gb_row[:, 0, :], gamma.rearrange("(o d) -> o d", o=1)),
                                     (gb_row[:, 1, :], beta.rearrange("(o d) -> o d", o=1))):
                        sp.dma_start(dst, src).then_inc(params_loaded, 16)
                    sp.wait_ge(wc_stored, 16 * LAYERS)
                    with sp.Fori(0, PAIRS - 1) as p:
                        pair(p, False)
                    pair(PAIRS - 1, True)
                    for lane in range(2):
                        sp.wait_ge(x1_done, 4 * (PAIRS - 1) + 2 * lane + 2)
                        sp.dma_start(batch(x1_dram, B - 2 + lane), xbuf[lane][:]).then_inc(x_last_stored, 16)
                    sp.wait_ge(x_last_stored, 32)

                @block.gpsimd
                def _(pool):
                    def norm_out(p, lane, number):
                        b = 2 * p + lane
                        pool.wait_ge(x1_done, 2 * b + 2)
                        detach(pool)
                        pool.dma_start(batch(x1_dram, b), xbuf[lane][:]).then_inc(x1z_stored, 16)
                        norm_apply(pool, KB, xbuf[lane], z_nat, mv2[lane], rstd, stats_done, number + 1,
                                   norm_step, 2 * number + 1, ln2_done)
                        pool.wait_ge(ln2_done, b + 1)
                        detach(pool)
                        pool.dma_start(batch(z_dram, b), z_nat[:]).then_inc(x1z_stored, 16)
                        nc.gpsimd.tensor_tensor(z_fold[:], z_nat[:, 0:HK, :], z_nat[:, HK:KB, :], ALU.add).then_inc(fold_step, 1)
                        pool.wait_ge(fold_step, 3 * b + 1)
                        nc.gpsimd.tensor_tensor(z_fold[:, 0:2, :], z_fold[:, 0:2, :], z_fold[:, 2:4, :], ALU.add).then_inc(fold_step, 1)
                        pool.wait_ge(fold_step, 3 * b + 2)
                        nc.gpsimd.tensor_tensor(zsum[:, b, :], z_fold[:, 0, :], z_fold[:, 1, :], ALU.add).then_inc(fold_step, 1)
                        pool.wait_ge(x1z_stored, 32 * b + 32)
                        pool.wait_ge(fold_step, 3 * b + 3)
                        pool.dma_start(xbuf[lane][:], batch(x, b + 2)).then_inc(xbuf_loaded[lane], 16)

                    pool.wait_ge(first_loaded[(CHUNKS - 1) % 6], 16 * ((CHUNKS - 1) // 6 + 1))
                    for lane in range(2):
                        pool.dma_start(xbuf[lane][:], batch(x, lane)).then_inc(xbuf_loaded[lane], 16)
                    with pool.Fori(0, PAIRS - 1) as p:
                        for lane in range(2):
                            number = 4 * p + 2 + lane
                            norm_apply(pool, KB, xn[lane], xn[lane], mv1[lane], rstd, stats_done, number + 1,
                                       norm_step, 2 * number + 1, ln1_done[lane])
                            pool.wait_ge(ln1_done[lane], p + 2)
                        for lane in range(2):
                            norm_out(p, lane, 4 * p + 4 + lane)
                    pool.wait_ge(params_loaded, 96)
                    nc.gpsimd.tensor_scalar(Wr_sb[:], Wr_sb[:], 1.0 / N, None, ALU.mult).then_inc(wr_scaled, 1)
                    for n in range(4):
                        lane, h = n // 2, n % 2
                        inverse_deviation(pool, mv2[lane][:, hblocks(h), :], rstd_last[lane][:, hblocks(h)], last_stats, n + 1,
                                          last_step, 3 * n + 1, last_step)
                        pool.wait_ge(last_step, 3 * n + 2)
                        nc.gpsimd.tensor_tensor(mean_rstd[lane][:, hblocks(h)], mv2[lane][:, hblocks(h), 0],
                                                rstd_last[lane][:, hblocks(h)], ALU.mult).then_inc(last_step, 1)

                @block.tensor
                def _(pe):
                    def x_to_features(lane, h):
                        for k in range(HK):
                            tr = nc.tensor.transpose(ps_t[h][:, k * P:(k + 1) * P], xn[lane][:, h * HK + k, :], ident[:])
                        tr.then_inc(xt_done, 1)

                    def state_to_tokens(s, q):
                        lane, h = before(q)
                        pe.wait_ge(h_done, s)
                        for k in range(HK):
                            tr = nc.tensor.transpose(ps_t[h][:, k * P:(k + 1) * P],
                                                     hT[lane][:, h * HW + k * P:h * HW + (k + 1) * P], ident[:])
                        tr.then_inc(trans_done, 1)

                    def aggregate(lane, h, nat_count):
                        for k in range(KB):
                            if k == 0 and nat_count is not None:
                                pe.wait_ge(nat_ready, nat_count)
                            if k == HK and nat_count is not None:
                                pe.wait_ge(nat_ready, nat_count + 1)
                            for part in (nat_hi, nat_lo):
                                mm = nc.tensor.matmul(ps_agg[h][:], part[lane][:, k, :], a_mat[lane][:, k, half(h)],
                                                      start=(k == 0 and part is nat_hi), stop=(k == KB - 1 and part is nat_lo))
                        mm.then_inc(agg_done, 1)

                    def gates(s, t, q, first, between):
                        lane, h = q // 2, q % 2
                        w_in, w_rec = w_cur[lane], w_hhT
                        inp = (agg_hi[h][:], agg_lo[h][:])
                        rec = (hT_hi[lane][:, half(h)], hT_lo[lane][:, half(h)])

                        def products(ps, gate, sides):
                            terms = []
                            for w, (hi, lo) in sides:
                                w_hi, w_lo = (w[:, o + gate * D:o + (gate + 1) * D] for o in (0, G))
                                terms += [(w_hi, hi), (w_hi, lo), (w_lo, hi)]
                            for n, (a, b) in enumerate(terms):
                                mm = nc.tensor.matmul(ps[:], a, b, start=(n == 0), stop=(n == len(terms) - 1))
                            return mm

                        pe.wait_ge(hT_ready[lane], 2 * t + h + 1)
                        if not first:
                            pe.wait_ge(cand_done, s)
                        products(ps_hn, 2, [(w_rec, rec)]).then_inc(hn_mm, 1)
                        pe.wait_ge(agg_split, s + 1)
                        pe.wait_ge(w_cur_loaded[lane], 16 * t + 16)
                        if not first:
                            pe.wait_ge(r_act, s)
                        products(ps_r, 0, [(w_rec, rec), (w_in, inp)]).then_inc(r_mm, 1)
                        between()
                        if not first:
                            pe.wait_ge(pre_done, s)
                        products(ps_in, 2, [(w_in, inp)]).then_inc(in_mm, 1)
                        if not first:
                            pe.wait_ge(z_act, s)
                        products(ps_z, 1, [(w_rec, rec), (w_in, inp)]).then_inc(z_mm, 1)

                    def slot(p, l, q, edge="", last=False):
                        t = LAYERS * p + l
                        s = SLOTS * t + q
                        h = q % 2
                        very_first = edge == "head" and isinstance(p, int) and p == 0 and q == 0

                        def turn_result():
                            if very_first:
                                return
                            if not (isinstance(p, int) and p == 0 and edge == "head") and not (edge == "tail" and q == 3 and last):
                                pe.wait_ge(nat_ready, s + 2)
                            if edge == "head":
                                if q == 0:
                                    pe.wait_ge(hT_ready[0], 2 * t + 2)
                                else:
                                    pe.wait_ge(hT_ready[1], 2 * t + q)
                            if edge == "tail" and q == 3:
                                if last:
                                    pe.wait_ge(x1_done, 4 * p + 1)
                                else:
                                    pe.wait_ge(hT_ready[0], 2 * t + 3)
                            state_to_tokens(s, q)

                        if last and edge == "tail" and q == 3:
                            gates(s, t, q, False, lambda: None)
                            turn_result()
                        else:
                            gates(s, t, q, very_first, turn_result)
                        if edge == "head" and q < 2:
                            if not (isinstance(p, int) and p == 0):
                                pe.wait_ge(x1_done, 4 * p - 1 + q)
                            pe.wait_ge(ln1_done[1], p + 1)
                            x_to_features(1, h)
                            if q == 0:
                                if isinstance(p, int) and p == 0:
                                    pe.wait_ge(a_compared, CHUNKS)
                                else:
                                    pe.wait_ge(a_widened[1], 2 * p)
                        if edge == "tail" and q >= 2 and not last:
                            pe.wait_ge(x1_done, 4 * p - 1 + q)
                            pe.wait_ge(ln1_done[0], p + 2)
                            x_to_features(0, h)
                            if q == 2:
                                pe.wait_ge(a_widened[0], 2 * p + 2)
                        if not (edge == "tail" and q >= 2 and last):
                            aggregate(1 - q // 2, h, s + 3 if h == 0 else None)

                    def pair(p, last):
                        slot(p, 0, 2, "head")
                        slot(p, 0, 3, "")
                        with pe.Fori(1, LAST) as l:
                            for q in range(SLOTS):
                                slot(p, l, q)
                        for q in range(SLOTS):
                            slot(p, LAST, q, "tail", last)

                    pe.wait_ge(ln1_done[0], 1)
                    for h in range(2):
                        x_to_features(0, h)
                    pe.wait_ge(a_compared, KB)
                    aggregate(0, 0, 1)
                    aggregate(0, 1, None)
                    slot(0, 0, 0, "head")
                    slot(0, 0, 1, "head")
                    with pe.Fori(0, PAIRS - 1) as p:
                        pair(p, False)
                        slot(p + 1, 0, 0, "head")
                        slot(p + 1, 0, 1, "head")
                    pair(PAIRS - 1, True)
                    pe.wait_ge(fold_step, 3 * (B - 2))
                    pe.wait_ge(consts_ready, 4)
                    for b in range(B - 2):
                        mm = nc.tensor.matmul(ps_agg[1][:, b:b + 1], zsum[:, b, :], ones[:, 0:1], start=True, stop=True)
                    mm.then_inc(sums_done, 1)
                    pe.wait_ge(x1_done, 4 * PAIRS - 2)
                    state_to_tokens(S_PAIR * PAIRS, 0)
                    for lane in range(2):
                        col = (KB + 1) * lane
                        for k in range(KB):
                            if k % HK == 0:
                                pe.wait_ge(last_step, 3 * (2 * lane + k // HK) + 3)
                            nc.tensor.matmul(ps_agg[0][:, col:col + 1], xbuf[lane][:, k, :], rstd_last[lane][:, k:k + 1],
                                             start=(k == 0), stop=(k == KB - 1))
                        nc.tensor.matmul(ps_agg[0][:, col + 1:col + 1 + KB], minus_ones[:], mean_rstd[lane][:],
                                         start=True, stop=True).then_inc(sums_done, 1)

                @block.scalar
                def _(act):
                    def new_x_tokens(lane, h):
                        nc.scalar.activation(nat_hi[lane][:, hblocks(h), :], xn[lane][:, hblocks(h), :],
                                             ACT.Copy).then_inc(nat_hi_done, 1)

                    def new_x_features(lane, h, number):
                        act.wait_ge(xt_done, number + 1)
                        nc.scalar.activation(hT[lane][:, half(h)], ps_t[h][:], ACT.Copy).then_inc(hT_hi_done[lane], 1)
                        nc.scalar.activation(hT_hi[lane][:, half(h)], ps_t[h][:], ACT.Copy).then_inc(hT_hi_done[lane], 1)

                    def slot(p, l, q, edge="", last=False):
                        t = LAYERS * p + l
                        s = SLOTS * t + q
                        lane, h = q // 2, q % 2
                        before_lane, before_h = before(q)
                        at_start = isinstance(p, int) and p == 0 and edge == "head"
                        if not (edge == "tail" and q == 3 and last):
                            act.wait_ge(agg_done, s + 2)
                            nc.scalar.activation(agg_hi[1 - h][:], ps_agg[1 - h][:], ACT.Copy).then_inc(agg_hi_done, 1)
                        act.wait_ge(r_mm, s + 1)
                        nc.scalar.activation(cand[h][:], ps_r[:], ACT.Sigmoid, bias=bias_rz[:, 0:1]).then_inc(r_act, 1)
                        if not (at_start and q == 0):
                            new_batch = (edge == "tail" and q >= 1) or (edge == "head" and q == 0)
                            if not (new_batch and last):
                                act.wait_ge(trans_done, s)
                                if new_batch:
                                    if q == 0:
                                        act.wait_ge(ln1_done[1], p + 1)
                                    else:
                                        act.wait_ge(ln1_done[before_lane], p + 2)
                                    new_x_tokens(before_lane, before_h)
                                else:
                                    nc.scalar.activation(flat(nat_hi[before_lane][:, hblocks(before_h), :]), ps_t[before_h][:],
                                                         ACT.Copy).then_inc(nat_hi_done, 1)
                        act.wait_ge(pre_done, s + 1)
                        nc.scalar.activation(cand[h][:], cand[h][:], ACT.Tanh, bias=bias_ih[:, 2:3]).then_inc(n_act, 1)
                        act.wait_ge(z_mm, s + 1)
                        nc.scalar.activation(gate_z[h][:], ps_z[:], ACT.Sigmoid, bias=bias_rz[:, 1:2]).then_inc(z_act, 1)
                        if edge == "head" and q < 2:
                            new_x_features(1, h, 4 * p + 2 + h)
                        if edge == "tail" and q >= 2 and not last:
                            new_x_features(0, h, 4 * p + 4 + h)
                        if edge == "tail" and not last:
                            act.wait_ge(a_compared, CHUNKS * (p + 1) + (lane + 1) * KB)
                            act.wait_ge(agg_done, 4 * t + 2 * lane + 2)
                            nc.scalar.activation(a_mat[lane][:, hblocks(h), :], a_next[:, KB * lane + HK * h:KB * lane + HK * (h + 1), :],
                                                 ACT.Copy).then_inc(a_widened[lane], 1)
                        if edge != "tail":
                            act.wait_ge(h_done, s + 1)
                            nc.scalar.activation(hT_hi[lane][:, half(h)], hT[lane][:, half(h)], ACT.Copy).then_inc(hT_hi_done[lane], 2)

                    def pair(p, last):
                        slot(p, 0, 2)
                        slot(p, 0, 3)
                        with act.Fori(1, LAST) as l:
                            for q in range(SLOTS):
                                slot(p, l, q)
                        for q in range(SLOTS):
                            slot(p, LAST, q, "tail", last)

                    act.wait_ge(ln1_done[0], 1)
                    new_x_tokens(0, 0)
                    new_x_tokens(0, 1)
                    new_x_features(0, 0, 0)
                    new_x_features(0, 1, 1)
                    act.wait_ge(ln1_done[1], 1)
                    new_x_tokens(1, 0)
                    new_x_tokens(1, 1)
                    act.wait_ge(agg_done, 1)
                    nc.scalar.activation(agg_hi[0][:], ps_agg[0][:], ACT.Copy).then_inc(agg_hi_done, 1)
                    slot(0, 0, 0, "head")
                    slot(0, 0, 1, "head")
                    with act.Fori(0, PAIRS - 1) as p:
                        pair(p, False)
                        slot(p + 1, 0, 0, "head")
                        slot(p + 1, 0, 1, "head")
                    pair(PAIRS - 1, True)
                    nc.scalar.activation(warm[:], ones[0:1, 0:1], ACT.Exp)

                @block.vector
                def _(dve):
                    def new_x_tokens(lane, h):
                        nc.vector.tensor_tensor(nat_lo[lane][:, hblocks(h), :], xn[lane][:, hblocks(h), :],
                                                exact(nat_hi[lane][:, hblocks(h), :]), ALU.subtract).then_inc(nat_ready, 1)

                    def new_x_features(lane, h, n):
                        dve.wait_ge(hT_hi_done[lane], 2 * n + 2)
                        nc.vector.tensor_tensor(hT_lo[lane][:, half(h)], ps_t[h][:], exact(hT_hi[lane][:, half(h)]),
                                                ALU.subtract).then_inc(hT_ready[lane], 1)

                    def final_state(p, lane, h):
                        if h == 0:
                            dve.wait_ge(xbuf_loaded[lane], 16 * p + 16)
                            detach(dve)
                        for k in range(HK):
                            x_block = xbuf[lane][:, h * HK + k, :]
                            ins = nc.vector.scalar_tensor_tensor(x_block, ps_t[h][:, k * P:(k + 1) * P],
                                                                 mask_tok[:, bass.ds((2 * p + lane) * KB + h * HK + k, 1)],
                                                                 x_block, ALU.mult, ALU.add)
                        ins.then_inc(x1_done, 1)

                    def compare(p, l, n):
                        dve.wait_ge(a_raw_loaded[n % 2], 16 * (KB * p + 2 * (l - 1) + n // 2 + 1))
                        nc.vector.tensor_scalar(a_next[:, SLOTS * (l - 1) + n, :], a_raw[:, n % 2], 0.0, None,
                                                ALU.not_equal).then_inc(a_compared, 1)

                    def half_stats(n):
                        lane, h = n // 2, n % 2
                        dve.wait_ge(x1_done, 4 * (PAIRS - 1) + n + 1)
                        token_stats(dve, HK, xbuf[lane][:, hblocks(h), :], stat6, mv2[lane][:, hblocks(h), :],
                                    last_stat_step, n + 1, last_stats)

                    def slot(p, l, q, edge="", last=False):
                        t = LAYERS * p + l
                        s = SLOTS * t + q
                        lane, h = q // 2, q % 2
                        before_lane, before_h = before(q)
                        at_start = isinstance(p, int) and p == 0 and edge == "head"
                        if not (edge == "tail" and q == 3 and last):
                            dve.wait_ge(agg_hi_done, s + 2)
                            nc.vector.tensor_tensor(agg_lo[1 - h][:], ps_agg[1 - h][:], exact(agg_hi[1 - h][:]),
                                                    ALU.subtract).then_inc(agg_split, 1)
                        if edge == "tail" and q == 2 and last:
                            dve.wait_ge(stats_done, 4 * PAIRS - 2)
                            half_stats(0)
                        dve.wait_ge(r_act, s + 1)
                        dve.wait_ge(hn_mm, s + 1)
                        nc.vector.scalar_tensor_tensor(cand[h][:], ps_hn[:], bias_hh[:, 2:3], cand[h][:], ALU.add, ALU.mult).then_inc(cand_done, 1)
                        dve.wait_ge(in_mm, s + 1)
                        dve.wait_ge(cand_done, s + 1)
                        nc.vector.tensor_tensor(cand[h][:], ps_in[:], cand[h][:], ALU.add).then_inc(pre_done, 1)
                        if not (at_start and q == 0):
                            new_batch = (edge == "tail" and q >= 1) or (edge == "head" and q == 0)
                            if not (new_batch and last):
                                dve.wait_ge(nat_hi_done, s + 4)
                                if new_batch:
                                    new_x_tokens(before_lane, before_h)
                                else:
                                    nc.vector.tensor_tensor(flat(nat_lo[before_lane][:, hblocks(before_h), :]), ps_t[before_h][:],
                                                            exact(flat(nat_hi[before_lane][:, hblocks(before_h), :])),
                                                            ALU.subtract).then_inc(nat_ready, 1)
                            if new_batch:
                                dve.wait_ge(trans_done, s)
                                detach(dve)
                                final_state(p - 1 if q == 0 else p, before_lane, before_h)
                        if not last and edge == "" and not isinstance(l, int):
                            compare(p, l, q)
                        if not last and edge == "tail" and q < 2:
                            compare(p, l, 2 * q)
                            compare(p, l, 2 * q + 1)
                        if edge == "" and isinstance(l, int) and not last:
                            dve.wait_ge(xn_loaded[h], 16 * p + 16)
                            token_stats(dve, KB, xn[h], stat6, mv1[h], stats_step, 4 * p + 3 + h, stats_done)
                        if edge == "tail" and q == 3 and not last:
                            dve.wait_ge(x1_done, 4 * p + 2)
                            token_stats(dve, KB, xbuf[0], stat6, mv2[0], stats_step, 4 * p + 5, stats_done)
                        if edge == "head" and q == 1 and not at_start:
                            for n in range(2):
                                dve.wait_ge(a_widened[n], 2 * p)
                            dve.wait_ge(x1_done, 4 * p)
                            token_stats(dve, KB, xbuf[1], stat6, mv2[1], stats_step, 4 * p + 2, stats_done)
                        dve.wait_ge(n_act, s + 1)
                        nc.vector.tensor_tensor(diff[:], hT[lane][:, half(h)], cand[h][:], ALU.subtract).then_inc(diff_done, 1)
                        dve.wait_ge(z_act, s + 1)
                        dve.wait_ge(diff_done, s + 1)
                        nc.vector.tensor_tensor(gate_z[h][:], gate_z[h][:], diff[:], ALU.mult).then_inc(zd_done, 1)
                        dve.wait_ge(zd_done, s + 1)
                        nc.vector.tensor_tensor(hT[lane][:, half(h)], cand[h][:], gate_z[h][:], ALU.add).then_inc(h_done, 1)
                        if edge == "head" and q < 2:
                            new_x_features(1, h, 2 * t + h)
                        if edge == "tail" and q >= 2 and not last:
                            new_x_features(0, h, 2 * t + 2 + h)
                        if edge != "tail":
                            n = 2 * t + 2 + h
                            dve.wait_ge(hT_hi_done[lane], 2 * n + 2)
                            nc.vector.tensor_tensor(hT_lo[lane][:, half(h)], hT[lane][:, half(h)], exact(hT_hi[lane][:, half(h)]),
                                                    ALU.subtract).then_inc(hT_ready[lane], 1)

                    def pair(p, last):
                        slot(p, 0, 2, "", last)
                        slot(p, 0, 3, "", last)
                        with dve.Fori(1, LAST) as l:
                            for q in range(SLOTS):
                                slot(p, l, q, "", last)
                        for q in range(SLOTS):
                            slot(p, LAST, q, "tail", last)

                    for h in range(2):
                        dve.wait_ge(nat_hi_done, h + 1)
                        new_x_tokens(0, h)
                    new_x_features(0, 0, 0)
                    new_x_features(0, 1, 1)
                    for c in range(KB, CHUNKS):
                        if c == CHUNKS - 2:
                            dve.wait_ge(wc_stored, 16 * LAYERS)
                        dve.wait_ge(first_loaded[c % 6], 16 * (c // 6 + 1))
                        compare_first(c)
                        if c == KB + 3:
                            dve.wait_ge(agg_hi_done, 1)
                            nc.vector.tensor_tensor(agg_lo[0][:], ps_agg[0][:], exact(agg_hi[0][:]), ALU.subtract).then_inc(agg_split, 1)
                    for h in range(2):
                        dve.wait_ge(nat_hi_done, h + 3)
                        new_x_tokens(1, h)
                    slot(0, 0, 0, "head")
                    slot(0, 0, 1, "head")
                    with dve.Fori(0, PAIRS - 1) as p:
                        pair(p, False)
                        slot(p + 1, 0, 0, "head")
                        slot(p + 1, 0, 1, "head")
                    pair(PAIRS - 1, True)
                    half_stats(1)
                    half_stats(2)
                    dve.wait_ge(trans_done, S_PAIR * PAIRS)
                    final_state(PAIRS - 1, 1, 1)
                    half_stats(3)
                    dve.wait_ge(sums_done, 1)
                    nc.vector.tensor_copy(sumT[:, 0:B - 2], ps_agg[1][:, 0:B - 2]).then_inc(sums_copied, 1)
                    dve.wait_ge(sums_done, 3)
                    nc.vector.tensor_reduce(sumT[:, B - 2:B], ps_agg[0][:, 0:2 * (KB + 1)].rearrange("p (l c) -> p l c", c=KB + 1),
                                            AX_X, ALU.add).then_inc(sums_copied, 1)

        with ExitStack() as phase2:
            sb, ps, sem = alloc_in(phase2, nc.sbuf_tensor), alloc_in(phase2, nc.psum_tensor), sem_in(phase2)
            C = B * TOP_K
            w_raw = [sb(f"w_raw{i}", [P, TOP_K, 2 * F]) for i in range(2)]
            w_hi = [sb(f"w_hi{i}", [P, TOP_K, 2 * F], F32R) for i in range(2)]
            w_lo = [sb(f"w_lo{i}", [P, TOP_K, 2 * F], F32R) for i in range(2)]
            z_in = [sb(f"z_in{i}", [P, KB, D]) for i in range(2)]
            z_res = [sb(f"z_res{i}", [P, KB, D]) for i in range(2)]
            x_res = [sb(f"x_res{i}", [P, KB, D]) for i in range(2)]
            zT_hi, zT_lo = sb("zT_hi", [P, N], F32R), sb("zT_lo", [P, N], F32R)
            act_out = [sb(f"act_out{i}", [P, HW]) for i in range(4)]
            g_hi = [sb(f"g_hi{i}", [P, HW], F32R) for i in range(4)]
            g_lo = [sb(f"g_lo{i}", [P, HW], F32R) for i in range(4)]
            yT = [sb(f"yT{h}", [P, HW]) for h in range(2)]
            res = [sb(f"res{h}", [P, HK, D]) for h in range(2)]
            stat6b = sb("stat6b", [P, HK, 6])
            mvb = [sb(f"mvb{h}", [P, HK, 2]) for h in range(2)]
            rstdb = [sb(f"rstdb{h}", [P, HK]) for h in range(2)]
            b1_sel = sb("b1_sel", [P, FB, C])
            b2_mix = sb("b2_mix", [P, B])
            top_w_all = sb("top_w_all", [P, C])
            gamma_all, beta_all = sb("gamma_all", [P, D]), sb("beta_all", [P, D])
            expert_row = sb("expert_row", [1, C], U32)
            z_in_loaded = [sem(f"z_in_loaded{i}") for i in range(2)]
            z_res_loaded = [sem(f"z_res_loaded{i}") for i in range(2)]
            x_res_loaded = [sem(f"x_res_loaded{i}") for i in range(2)]

            logit_max, total, inv_total = (sb(n, [B, 3]) for n in ("logit_max", "total", "inv_total"))
            rw, rw2, e2, quot = (sb(n, [B, E]) for n in ("rw", "rw2", "e2", "quot"))
            top, top_i, top_f = sb("top", [B, 8]), sb("top_i", [B, 8], U32), sb("top_f", [B, 8])
            onehot, w_dense = sb("onehot", [B, TOP_K, E]), sb("w_dense", [B, E])
            top_e, top_w = sb("top_e", [B, TOP_K]), sb("top_w", [B, TOP_K])
            w_diag = sb("w_diag", [B, TOP_K, B])
            oh_T, wd_T = sb("oh_T", [E, C]), sb("wd_T", [E, B])
            pe_step, act_step, dve_step = (sem(n) for n in ("pe_step", "act_step", "dve_step"))
            z_last_done = [sem(f"z_last_done{n}") for n in range(2)]
            z_last_stored = sem("z_last_stored")

            ps_l1 = [ps(f"ps_l1_{i}", [P, HW]) for i in range(4)]
            ps_y = [ps(f"ps_y{h}", [P, HW]) for h in range(2)]
            ps_zt, ps_yt = ps("ps_zt", [P, HW]), ps("ps_yt", [P, HW])
            w1_loaded = [[sem(f"w1_loaded{i}_{k}") for k in range(TOP_K)] for i in range(2)]
            w2_loaded = [sem(f"w2_loaded{i}") for i in range(2)]
            w1_hi_done, w2_hi_done, w1_split, w2_split = (sem(n) for n in ("w1_hi_done", "w2_hi_done", "w1_split", "w2_split"))
            zt_done, zt_hi_done, zt_split = sem("zt_done"), sem("zt_hi_done"), sem("zt_split")
            l1_done, gelu_done, g_hi_done, g_split = (
                sem(n) for n in ("l1_done", "gelu_done", "g_hi_done", "g_split"))
            y_mm, y_copied, yt_done, res_added, res_step, res_stats = (
                sem(n) for n in ("y_mm", "y_copied", "yt_done", "res_added", "res_step", "res_stats"))
            out_step, rstd_done, out_normed, x_beta = (sem(n) for n in ("out_step", "rstd_done", "out_normed", "x_beta"))
            last_out = sem("last_out")
            out_stored = [sem(f"out_stored{h}") for h in range(2)]
            ps_logits, ps_load, ps_rows, ps_t8 = (ps_l1[i] for i in range(4))
            ps_sel, ps_bc = ps_y
            block = phase2.enter_context(nc.Block())

            def number(bt):
                return 2 * bt[0] + bt[1]

            def following(bt):
                return (bt[0], 1) if bt[1] == 0 else (bt[0] + 1, 0)

            def previous(bt):
                return (bt[0] - 1, 1) if bt[1] == 0 else (bt[0], 0)

            def is_first(bt):
                return isinstance(bt[0], int) and bt == (0, 0)

            def ahead(bt, u, n):
                return (bt, u + n) if u + n < UNITS else (following(bt), u + n - UNITS)

            def half(h):
                return slice(h * HW, (h + 1) * HW)

            def hblocks(h):
                return slice(h * HK, (h + 1) * HK)

            LAST_BATCH = (B // 2 - 1, 1)
            last_res = z_in[0]

            def steps(eng, step):
                def round_(bt, last=False):
                    for u in range(1, UNITS):
                        step(bt, u, last)
                    if not last:
                        step(following(bt), 0, False)

                step((0, 0), 0, False)
                round_((0, 0))
                with eng.Fori(0, B // 2 - 1) as i:
                    round_((i, 1))
                    round_((i + 1, 0))
                round_(LAST_BATCH, True)

            @block.sync
            def _(sp):
                def gather(bt):
                    i, parity = bt
                    for k in range(TOP_K):
                        e = sp.value_load(expert_row[0:1, bass.ds(k * B + number(bt), 1)], min_val=0, max_val=E - 1)
                        sp.dma_start(w_raw[parity][:, k, 0:F], W1[e]).then_inc(w1_loaded[parity][k], 16)
                        sp.dma_start(w_raw[parity][:, k, F:2 * F].rearrange("p (c d) -> p c d", d=D),
                                     W2.rearrange("e (c p) d -> e p c d", p=P)[e]).then_inc(w2_loaded[parity], 16)

                def refill(bt):
                    i, parity = bt
                    sp.wait_ge(w1_split, 2 * number(bt) + 2)
                    detach(sp)
                    sp.wait_ge(w2_split, 2 * number(bt) + 2)
                    gather((i + 1, parity))
                    sp.wait_ge(zt_done, 2 * number(bt) + 2)
                    sp.dma_start(z_in[parity][:], batch(z_dram, number(bt) + 2)).then_inc(z_in_loaded[parity], 16)

                def store(bt, h):
                    sp.wait_ge(out_step, 3 * (2 * number(bt) + h) + 3)
                    sp.dma_start(batch(out, number(bt))[:, hblocks(h), :], res[h][:]).then_inc(out_stored[h], 16)

                def residuals(bt):
                    parity = bt[1]
                    sp.dma_start(z_res[parity][:], batch(z_dram, number(bt) + 2)).then_inc(z_res_loaded[parity], 16)
                    sp.dma_start(x_res[parity][:], batch(x1_dram, number(bt) + 2)).then_inc(x_res_loaded[parity], 16)

                sp.dma_start(z_in[0][:], batch(z_dram, 0)).then_inc(z_in_loaded[0], 16)
                for h in range(2):
                    sp.sem_inc(out_stored[h], 16)
                sp.wait_ge(dve_step, 14)
                gather((0, 0))
                sp.dma_start(z_in[1][:], batch(z_dram, 1)).then_inc(z_in_loaded[1], 16)
                gather((0, 1))
                for i in range(2):
                    sp.dma_start(z_res[i][:], batch(z_dram, i)).then_inc(z_res_loaded[i], 16)
                    sp.dma_start(x_res[i][:], batch(x1_dram, i)).then_inc(x_res_loaded[i], 16)
                for n in (1, 0):
                    sp.wait_ge(z_last_done[n], 1)
                    sp.dma_start(batch(z_dram, B - 2 + n), xn[n][:]).then_inc(z_last_stored, 16)
                refill((0, 0))
                refill((0, 1))
                sp.wait_ge(z_last_stored, 32)
                with sp.Fori(0, B // 2 - 2) as i:
                    for parity in range(2):
                        store((i, parity), 0)
                        refill((i + 1, parity))
                        store((i, parity), 1)
                        residuals((i, parity))
                for i in range(B // 2 - 2, B // 2):
                    for parity in range(2):
                        if (i, parity) == LAST_BATCH:
                            continue
                        store((i, parity), 0)
                        store((i, parity), 1)
                        if i < B // 2 - 1:
                            residuals((i, parity))
                for h in range(2):
                    sp.wait_ge(last_out, h + 1)
                    sp.dma_start(batch(out, B - 1)[:, hblocks(h), :], last_res[:, hblocks(h), :]).then_inc(out_stored[h], 16)
                for h in range(2):
                    sp.wait_ge(out_stored[h], 16 * B + 16)

            @block.gpsimd
            def _(pool):
                def split_first_weights(bt):
                    parity = bt[1]
                    for k in range(TOP_K):
                        pool.wait_ge(w1_hi_done, 2 * number(bt) + k + 1)
                        nc.gpsimd.tensor_tensor(w_lo[parity][:, k, 0:F], w_raw[parity][:, k, 0:F], exact(w_hi[parity][:, k, 0:F]),
                                                ALU.subtract).then_inc(w1_split, 1)

                def add_beta(bt, h):
                    i, parity = bt
                    x_half = x_res[parity][:, hblocks(h), :]
                    pool.wait_ge(x_res_loaded[parity], 16 * i + 16)
                    nc.gpsimd.tensor_tensor(x_half, x_half, beta_all[:].unsqueeze(1).to_broadcast([P, HK, D]), ALU.add).then_inc(x_beta, 1)

                def deviations(bt, h, step=None):
                    n = 2 * number(bt) + h
                    inverse_deviation(pool, mvb[h], rstdb[h], res_stats, n + 1, out_step, 3 * n + 1 if step is None else step, rstd_done)

                def finish(bt, h):
                    n = 2 * number(bt) + h
                    pool.wait_ge(out_normed, n + 1)
                    nc.gpsimd.tensor_tensor(res[h][:], res[h][:], gamma_all[:].unsqueeze(1).to_broadcast([P, HK, D]), ALU.mult).then_inc(out_step, 1)
                    pool.wait_ge(out_step, 3 * n + 2)
                    pool.wait_ge(x_beta, n + 1)
                    nc.gpsimd.tensor_tensor(res[h][:], res[h][:], x_res[bt[1]][:, hblocks(h), :], ALU.add).then_inc(out_step, 1)

                for k in range(KB):
                    ins = nc.gpsimd.tensor_scalar(xn[0][:, k, :], xbuf[0][:, k, :], mv2[0][:, k, 0:1], rstd_last[0][:, k:k + 1],
                                                  ALU.subtract, ALU.mult)
                ins.then_inc(z_last_done[0], 1)
                split_first_weights((0, 0))
                split_first_weights((0, 1))
                add_beta((0, 0), 0)

                def whole_half(bt, h):
                    deviations(bt, h)
                    add_beta(*((bt, 1) if h == 0 else (following(bt), 0)))
                    finish(bt, h)

                with pool.Fori(0, B // 2 - 1) as i:
                    for parity in range(2):
                        whole_half((i, parity), 0)
                        split_first_weights((i + 1, parity))
                        whole_half((i, parity), 1)
                for h in range(2):
                    whole_half((B // 2 - 1, 0), h)
                add_beta(LAST_BATCH, 1)
                for h in range(2):
                    deviations(LAST_BATCH, h, 6 * (B - 1) + 1 + h)

            @block.tensor
            def _(pe):
                def tokens_to_features(bt, h):
                    n = 2 * number(bt) + h
                    pe.wait_ge(z_in_loaded[bt[1]], 16 * bt[0] + 16)
                    if not (isinstance(n, int) and n == 0):
                        pe.wait_ge(zt_split, n)
                    for k in range(HK):
                        tr = nc.tensor.transpose(ps_zt[:, k * P:(k + 1) * P], z_in[bt[1]][:, h * HK + k, :], ident[:])
                    tr.then_inc(zt_done, 1)

                def features_to_tokens(bt, h):
                    n = 2 * number(bt) + h
                    pe.wait_ge(y_copied, n + 1)
                    if not (isinstance(n, int) and n == 0):
                        pe.wait_ge(res_added, n)
                    for k in range(HK):
                        tr = nc.tensor.transpose(ps_yt[:, k * P:(k + 1) * P], yT[h][:, k * P:(k + 1) * P], ident[:])
                    tr.then_inc(yt_done, 1)

                def first_product(bt, u):
                    h, k, f = u // 4, u // 2 % 2, u % 2
                    if u % 4 == 0:
                        pe.wait_ge(zt_split, 2 * number(bt) + h + 1)
                    if u in (0, 2):
                        pe.wait_ge(w1_split, 2 * number(bt) + k + 1)
                    w_h, w_l = (w[bt[1]][:, k, f * P:(f + 1) * P] for w in (w_hi, w_lo))
                    z_h, z_l = zT_hi[:, half(h)], zT_lo[:, half(h)]
                    nc.tensor.matmul(ps_l1[u % 4][:], w_h, z_h, start=True, stop=False)
                    nc.tensor.matmul(ps_l1[u % 4][:], w_h, z_l, start=False, stop=False)
                    nc.tensor.matmul(ps_l1[u % 4][:], w_l, z_h, start=False, stop=True).then_inc(l1_done, 1)

                def second_product(bt, u):
                    h, k, f = u // 4, u // 2 % 2, u % 2
                    if u in (0, 2):
                        pe.wait_ge(w2_split, 2 * number(bt) + k + 1)
                    pe.wait_ge(g_split, UNITS * number(bt) + u + 1)
                    w_h, w_l = (w[bt[1]][:, k, F + f * P:F + (f + 1) * P] for w in (w_hi, w_lo))
                    nc.tensor.matmul(ps_y[h][:], w_h, g_hi[u % 4][:], start=(u % 4 == 0), stop=False)
                    nc.tensor.matmul(ps_y[h][:], w_h, g_lo[u % 4][:], start=False, stop=False)
                    mm = nc.tensor.matmul(ps_y[h][:], w_l, g_hi[u % 4][:], start=False, stop=(u % 4 == 3))
                    if u % 4 == 3:
                        mm.then_inc(y_mm, 1)

                def step(bt, u, last):
                    if not (last and u + 3 >= UNITS):
                        first_product(*ahead(bt, u, 3))
                    second_product(bt, u)
                    if u == 1 and not is_first(bt):
                        features_to_tokens(previous(bt), 1)
                    if u in (1, 5) and not last:
                        tokens_to_features(following(bt), u // 4)
                    if u == 5:
                        features_to_tokens(bt, 0)

                pe.wait_ge(wr_scaled, 1)
                nc.tensor.matmul(ps_logits[0:B, 0:E], sumT[:], Wr_sb[:], start=True, stop=False)
                nc.tensor.matmul(ps_logits[0:B, 0:E], ones[0:1, 0:B], br_row[:], start=False, stop=True).then_inc(pe_step, 1)
                nc.tensor.matmul(ps_bc[:, 256:384], ones[0:1, :], gb_row[:, 0, :], start=True, stop=True)
                nc.tensor.matmul(ps_bc[:, 384:512], ones[0:1, :], gb_row[:, 1, :], start=True, stop=True).then_inc(pe_step, 1)
                pe.wait_ge(dve_step, 3)
                nc.tensor.matmul(ps_load[0:B, 0:E], ones[0:B, 0:B], rw[:], start=True, stop=True).then_inc(pe_step, 1)
                pe.wait_ge(dve_step, 12)
                for k in range(TOP_K):
                    mm = nc.tensor.matmul(ps_rows[0:1, k * B:(k + 1) * B], top_f[:, k:k + 1], ident[0:B, 0:B], start=True, stop=True)
                mm.then_inc(pe_step, 1)
                tokens_to_features((0, 0), 0)
                pe.wait_ge(dve_step, 20)
                for k in range(TOP_K):
                    nc.tensor.transpose(ps_t8[0:E, k * B:(k + 1) * B], onehot[:, k, :], ident[0:B, 0:B])
                nc.tensor.transpose(ps_t8[0:E, C:C + B], w_dense[:], ident[0:B, 0:B]).then_inc(pe_step, 1)
                nc.tensor.matmul(ps_bc[:, 0:C], ones[0:B, :], w_diag[:].rearrange("b k c -> b (k c)"), start=True, stop=True)
                pe.wait_ge(dve_step, 22)
                for f in range(FB):
                    nc.tensor.matmul(ps_sel[:, f * C:(f + 1) * C], b1_sb[:, f * P:(f + 1) * P], oh_T[:], start=True, stop=True)
                nc.tensor.matmul(ps_sel[:, FB * C:FB * C + B], b2_sb[:], wd_T[:], start=True, stop=True).then_inc(pe_step, 1)
                first_product((0, 0), 0)
                first_product((0, 0), 1)
                tokens_to_features((0, 0), 1)
                first_product((0, 0), 2)
                steps(pe, step)
                features_to_tokens(LAST_BATCH, 1)

            @block.scalar
            def _(act):
                def round_tokens(bt, h):
                    act.wait_ge(zt_done, 2 * number(bt) + h + 1)
                    nc.scalar.activation(zT_hi[:, half(h)], ps_zt[:], ACT.Copy).then_inc(zt_hi_done, 1)

                def copy_mixture(bt, h):
                    act.wait_ge(y_mm, 2 * number(bt) + h + 1)
                    detach(act)
                    nc.scalar.activation(yT[h][:], ps_y[h][:], ACT.Identity,
                                         bias=b2_mix[:, bass.ds(number(bt), 1)]).then_inc(y_copied, 1)

                def activate(bt, u):
                    k, f = u // 2 % 2, u % 2
                    U = UNITS * number(bt) + u
                    act.wait_ge(l1_done, U + 1)
                    detach(act)
                    nc.scalar.activation(act_out[u % 4][:], ps_l1[u % 4][:], ACT.Gelu,
                                         bias=b1_sel[:, f, bass.ds(k * B + number(bt), 1)]).then_inc(gelu_done, 1)
                    act.wait_ge(gelu_done, U + 1)
                    nc.scalar.activation(g_hi[u % 4][:], act_out[u % 4][:], ACT.Copy).then_inc(g_hi_done, 1)

                def round_first_weights(bt, k):
                    i, parity = bt
                    act.wait_ge(w1_loaded[parity][k], 16 * i + 16)
                    if k == 0 and not (isinstance(i, int) and number(bt) <= 1):
                        act.wait_ge(y_mm, 2 * (number(bt) - 1))
                    detach(act)
                    nc.scalar.activation(w_hi[parity][:, k, 0:F], w_raw[parity][:, k, 0:F], ACT.Copy).then_inc(w1_hi_done, 1)

                def round_second_weights(bt, k):
                    i, parity = bt
                    if k == 0:
                        act.wait_ge(w2_loaded[parity], 16 * TOP_K * i + 16 * TOP_K)
                        detach(act)
                    nc.scalar.activation(w_hi[parity][:, k, F:2 * F], w_raw[parity][:, k, F:2 * F], ACT.Copy,
                                         scale=top_w_all[:, bass.ds(k * B + number(bt), 1)]).then_inc(w2_hi_done, 1)

                def step(bt, u, last):
                    if not (last and u + 2 >= UNITS):
                        activate(*ahead(bt, u, 2))
                    if u == 0 and not is_first(bt):
                        copy_mixture(previous(bt), 1)
                    if u in (1, 2) and not last:
                        round_first_weights(following(bt), u - 1)
                        round_second_weights(following(bt), u - 1)
                    if u in (2, 6) and not last:
                        round_tokens(following(bt), u // 4)
                    if u == 4:
                        copy_mixture(bt, 0)

                act.wait_ge(dve_step, 1)
                nc.scalar.activation(rw[:], ps_logits[0:B, 0:E], ACT.Exp, bias=logit_max[:, 0:1],
                                     accum_out=total[:, 0:1]).then_inc(act_step, 1)
                act.wait_ge(dve_step, 7)
                nc.scalar.activation(e2[:], rw2[:], ACT.Exp, bias=logit_max[:, 1:2], accum_out=total[:, 1:2]).then_inc(act_step, 1)
                act.wait_ge(dve_step, 13)
                nc.scalar.activation(top_e[:], top[:, 0:TOP_K], ACT.Exp, bias=logit_max[:, 2:3], accum_out=total[:, 2:3]).then_inc(act_step, 1)
                nc.scalar.activation(warm[:], ones[0:1, 0:1], ACT.Gelu)
                round_tokens((0, 0), 0)
                for k in range(TOP_K):
                    round_first_weights((0, 0), k)
                act.wait_ge(dve_step, 23)
                activate((0, 0), 0)
                for k in range(TOP_K):
                    round_second_weights((0, 0), k)
                round_tokens((0, 0), 1)
                activate((0, 0), 1)
                steps(act, step)
                copy_mixture(LAST_BATCH, 1)

            @block.vector
            def _(dve):
                def split_tokens(bt, h):
                    dve.wait_ge(zt_hi_done, 2 * number(bt) + h + 1)
                    nc.vector.tensor_tensor(zT_lo[:, half(h)], ps_zt[:], exact(zT_hi[:, half(h)]), ALU.subtract).then_inc(zt_split, 1)

                def split_second_weights(bt, k):
                    parity = bt[1]
                    dve.wait_ge(w2_hi_done, 2 * number(bt) + k + 1)
                    detach(dve)
                    nc.vector.scalar_tensor_tensor(w_lo[parity][:, k, F:2 * F], w_raw[parity][:, k, F:2 * F],
                                                   top_w_all[:, bass.ds(k * B + number(bt), 1)],
                                                   exact(w_hi[parity][:, k, F:2 * F]), ALU.mult, ALU.subtract).then_inc(w2_split, 1)

                def split_activations(bt, u):
                    dve.wait_ge(g_hi_done, UNITS * number(bt) + u + 1)
                    nc.vector.tensor_tensor(g_lo[u % 4][:], act_out[u % 4][:], exact(g_hi[u % 4][:]), ALU.subtract).then_inc(g_split, 1)

                def add_residual(bt, h, target=None):
                    i, parity = bt
                    n = 2 * number(bt) + h
                    dve.wait_ge(yt_done, n + 1)
                    dve.wait_ge(z_res_loaded[parity], 16 * i + 16)
                    if target is None:
                        target = res[h][:]
                        dve.wait_ge(out_stored[h], 16 * number(bt) + 16)
                    nc.vector.tensor_tensor(target, ps_yt[:].rearrange("p (k d) -> p k d", d=D), z_res[parity][:, hblocks(h), :],
                                            ALU.add).then_inc(res_added, 1)
                    dve.wait_ge(res_added, n + 1)
                    token_stats(dve, HK, target, stat6b, mvb[h], res_step, n + 1, res_stats)

                def apply_norm(bt, h):
                    n = 2 * number(bt) + h
                    dve.wait_ge(rstd_done, n + 1)
                    detach(dve)
                    for k in range(HK):
                        ins = nc.vector.tensor_scalar(res[h][:, k, :], res[h][:, k, :], mvb[h][:, k, 0:1], rstdb[h][:, k:k + 1],
                                                      ALU.subtract, ALU.mult)
                    ins.then_inc(out_normed, 1)

                def step(bt, u, last):
                    if u in (3, 7) and not last:
                        split_tokens(following(bt), u // 4)
                    if not (last and u + 2 >= UNITS):
                        split_activations(*ahead(bt, u, 2))
                    if u in (3, 4) and not last:
                        split_second_weights(following(bt), u - 3)
                    if u == 6 and not last:
                        add_residual(bt, 0)
                    if u == 2 and not is_first(bt):
                        add_residual(previous(bt), 1)
                    if u == 0 and not is_first(bt):
                        apply_norm(previous(bt), 0)
                    if u == 4 and not is_first(bt):
                        apply_norm(previous(bt), 1)

                def step_done(ins, n):
                    ins.then_inc(dve_step, 1)
                    dve.wait_ge(dve_step, n)

                def last_z(blocks):
                    for k in blocks:
                        ins = nc.vector.tensor_scalar(xn[1][:, k, :], xbuf[1][:, k, :], mv2[1][:, k, 0:1], rstd_last[1][:, k:k + 1],
                                                      ALU.subtract, ALU.mult)
                    return ins

                dve.wait_ge(pe_step, 1)
                step_done(nc.vector.tensor_reduce(logit_max[:, 0:1], ps_logits[0:B, 0:E], AX_X, ALU.max, negate=True), 1)
                last_z(range(0, 2))
                dve.wait_ge(act_step, 1)
                step_done(nc.vector.reciprocal(inv_total[:, 0:1], total[:, 0:1]), 2)
                step_done(nc.vector.tensor_scalar(rw[:], rw[:], inv_total[:, 0:1], None, ALU.mult), 3)
                last_z(range(2, 3))
                dve.wait_ge(pe_step, 3)
                step_done(nc.vector.reciprocal(quot[:], ps_load[0:B, 0:E]), 4)
                step_done(nc.vector.tensor_scalar(quot[:], quot[:], CAPACITY / N, 1.0, ALU.mult, ALU.min), 5)
                step_done(nc.vector.tensor_tensor(rw2[:], rw[:], quot[:], ALU.mult), 6)
                step_done(nc.vector.tensor_reduce(logit_max[:, 1:2], rw2[:], AX_X, ALU.max, negate=True), 7)
                last_z(range(3, 5))
                dve.wait_ge(act_step, 2)
                step_done(nc.vector.reciprocal(inv_total[:, 1:2], total[:, 1:2]), 8)
                step_done(nc.vector.tensor_scalar(rw2[:], e2[:], inv_total[:, 1:2], None, ALU.mult), 9)
                step_done(nc.vector.max(top[:], rw2[:]), 10)
                step_done(nc.vector.max_index(top_i[:], top[:], rw2[:]), 11)
                step_done(nc.vector.tensor_copy(top_f[:], top_i[:]), 12)
                step_done(nc.vector.tensor_scalar(logit_max[:, 2:3], top[:, 0:1], -1.0, None, ALU.mult), 13)
                dve.wait_ge(pe_step, 4)
                step_done(nc.vector.tensor_copy(expert_row[:], ps_rows[0:1, 0:C]), 14)
                dve.wait_ge(act_step, 3)
                step_done(nc.vector.reciprocal(inv_total[:, 2:3], total[:, 2:3]), 15)
                step_done(nc.vector.tensor_scalar(top_w[:], top_e[:], inv_total[:, 2:3], None, ALU.mult), 16)
                for k in range(TOP_K):
                    ins = nc.vector.tensor_scalar(onehot[:, k, :], iota_e[:], top_f[:, k:k + 1], None, ALU.is_equal)
                step_done(ins, 17)
                for k in range(TOP_K):
                    ins = nc.vector.tensor_scalar(w_diag[:, k, :], ident[0:B, 0:B], top_w[:, k:k + 1], None, ALU.mult)
                step_done(ins, 18)
                step_done(nc.vector.tensor_scalar(w_dense[:], onehot[:, 0, :], top_w[:, 0:1], None, ALU.mult), 19)
                step_done(nc.vector.scalar_tensor_tensor(w_dense[:], onehot[:, 1, :], top_w[:, 1:2], w_dense[:], ALU.mult, ALU.add), 20)
                split_tokens((0, 0), 0)
                dve.wait_ge(pe_step, 5)
                step_done(nc.vector.tensor_copy(oh_T[:], ps_t8[0:E, 0:C]), 21)
                step_done(nc.vector.tensor_copy(wd_T[:], ps_t8[0:E, C:C + B]), 22)
                last_z(range(5, KB)).then_inc(z_last_done[1], 1)
                dve.wait_ge(pe_step, 6)
                nc.vector.tensor_copy(b1_sel[:].rearrange("p f c -> p (f c)"), ps_sel[:, 0:FB * C])
                nc.vector.tensor_copy(b2_mix[:], ps_sel[:, FB * C:FB * C + B])
                nc.vector.tensor_copy(top_w_all[:], ps_bc[:, 0:C])
                nc.vector.tensor_copy(gamma_all[:], ps_bc[:, 256:384])
                step_done(nc.vector.tensor_copy(beta_all[:], ps_bc[:, 384:512]), 23)
                split_activations((0, 0), 0)
                for k in range(TOP_K):
                    split_second_weights((0, 0), k)
                split_tokens((0, 0), 1)
                split_activations((0, 0), 1)
                steps(dve, step)
                n = 2 * number(LAST_BATCH)
                for h in range(2):
                    add_residual(LAST_BATCH, h, last_res[:, hblocks(h), :])
                for h in range(2):
                    dve.wait_ge(res_stats, n + h + 1)
                    for k in range(HK):
                        ins = nc.vector.scalar_tensor_tensor(last_res[:, h * HK + k, :], last_res[:, h * HK + k, :], mvb[h][:, k, 0:1], gamma_all[:],
                                                             ALU.subtract, ALU.mult)
                    ins.then_inc(out_normed, 1)
                for h in range(2):
                    dve.wait_ge(rstd_done, n + h + 1)
                    dve.wait_ge(out_normed, n + h + 1)
                    dve.wait_ge(x_beta, n + h + 1)
                    for k in range(HK):
                        ins = nc.vector.scalar_tensor_tensor(last_res[:, h * HK + k, :], last_res[:, h * HK + k, :], rstdb[h][:, k:k + 1],
                                                             x_res[1][:, h * HK + k, :], ALU.mult, ALU.add)
                    ins.then_inc(last_out, 1)


_INS = ["x", "adj", "nodemask", "L0_gnn_weight", "L0_gnn_w_ih", "L0_gnn_w_hh", "L0_gnn_b_ih", "L0_gnn_b_hh", "L0_ffn_Wr",
        "L0_ffn_br", "L0_ffn_W1", "L0_ffn_b1", "L0_ffn_W2", "L0_ffn_b2", "L0_ffn_gamma", "L0_ffn_beta"]


def kernel(**inputs):
    import numpy as _np
    import concourse.bacc as _bacc
    from concourse import mybir as _mybir
    from concourse.bass_utils import run_bass_kernel_spmd as _run

    nc = _bacc.Bacc("TRN2", target_bir_lowering=False, num_devices=1)
    arrays, args = {}, []
    for name in _INS:
        a = _np.ascontiguousarray(inputs[name])
        arrays[f"in_{name}_dram"] = a
        args.append(nc.dram_tensor(f"in_{name}_dram", a.shape, _mybir.dt.from_np(a.dtype), kind="ExternalInput").ap())
    args.append(nc.dram_tensor("out_dram", inputs["x"].shape, F32, kind="ExternalOutput").ap())
    build_gnn_ffn(nc, *args)
    return _run(nc, [arrays], core_ids=[0]).results[0]["out_dram"]
```
